# Optimizing a Trainium2 kernel written in Bass

```python
import numpy as np
import jax
import jax.numpy as jnp

def _softmax(x, axis=-1):
    return jax.nn.softmax(x, axis=axis)

def _gelu(x):
    return jax.nn.gelu(x, approximate=True)

def _silu(x):
    return jax.nn.silu(x)

def _sigmoid(x):
    return jax.nn.sigmoid(x)

def _layernorm(x, axis=-1, eps=1e-05):
    m = jnp.mean(x, axis=axis, keepdims=True)
    v = jnp.var(x, axis=axis, keepdims=True)
    return (x - m) / jnp.sqrt(v + eps)

def _scatter_add(tgt, idx, src, axis=0):
    return tgt.at[idx].add(src)

def _segment_sum(src, seg, n):
    return jax.ops.segment_sum(src, seg, n)
kernel_name = 'mk_early_fusion_d2_tok_img1024_r4_8f649b'

def setup_inputs(seed: int=0):
    np.random.seed(seed)
    _w = jnp.asarray

    def _rec_inputs():
        import jax
        import jax.numpy as jnp
        _rk = jax.random.key(seed)
        x = -0.00016672 + 0.999947 * jax.random.normal(jax.random.fold_in(_rk, 1), (32, 3, 96, 96), jnp.float32)
        txt = -1.44135e-05 + 0.554504 * jax.random.normal(jax.random.fold_in(_rk, 2), (32, 32, 256), jnp.float32)
        return (x, txt)
    x, txt = _rec_inputs()

    def _L0_tok_setup():
        import jax, jax.numpy as jnp
        import numpy as np
        P = 16

        def _patchify(x):
            B, C, H, W = x.shape
            gh, gw = (H // P, W // P)
            x = x.reshape(B, C, gh, P, gw, P)
            x = x.transpose(0, 2, 4, 1, 3, 5)
            return x.reshape(B, gh * gw, C * P * P)
        key = jax.random.key(seed)
        k1, k2, k3, k4, k5 = jax.random.split(key, 5)
        B, C, S = (64, 3, 96)
        lin_in, lout = (P * P * C, 256)
        n_patches = (S // P) ** 2
        return {'x': jax.random.normal(k1, (B, C, S, S), dtype=jnp.float32), 'W': jax.random.normal(k2, (lout, lin_in), dtype=jnp.float32) * 0.02, 'b': jax.random.normal(k3, (lout,), dtype=jnp.float32) * 0.02, 'class_token': jax.random.normal(k4, (1, 1, lout), dtype=jnp.float32) * 0.02, 'pos_embedding': jax.random.normal(k5, (1, n_patches + 1, lout), dtype=jnp.float32) * 0.02}
    _L0_tok_all = _L0_tok_setup()
    _L0_tok_in = {k: v for k, v in _L0_tok_all.items() if k in ('W', 'b', 'class_token', 'pos_embedding')}
    del _L0_tok_all

    def _L0_attn_setup():
        import jax, jax.numpy as jnp
        import numpy as np
        D_MODEL = 256
        STATE = 64
        HEADS = 8
        EXPAND = 2
        INNER = EXPAND * D_MODEL
        HEAD_DIM = INNER // HEADS
        PROJ_OUT = 2 * INNER + 2 * STATE + HEADS
        BATCH, SEQ = (2, 256)
        EPS = 1e-05

        def _layer_norm(x, gamma, beta):
            mu = jnp.mean(x, axis=-1, keepdims=True)
            xc = x - mu
            var = jnp.mean(xc * xc, axis=-1, keepdims=True)
            return xc * jax.lax.rsqrt(var + EPS) * gamma + beta

        def _mamba2(u, W_in, b_in, A_log, D_skip, dt_bias, W_out, b_out):
            B, L, _ = u.shape
            zxbcdt = u @ W_in + b_in
            z = zxbcdt[..., :INNER]
            xs = zxbcdt[..., INNER:2 * INNER].reshape(B, L, HEADS, HEAD_DIM)
            Bm = zxbcdt[..., 2 * INNER:2 * INNER + STATE]
            Cm = zxbcdt[..., 2 * INNER + STATE:2 * INNER + 2 * STATE]
            dt = jax.nn.softplus(zxbcdt[..., 2 * INNER + 2 * STATE:] + dt_bias)
            A = -jnp.exp(A_log)
            decay = jnp.exp(dt * A)
            dtx = dt[..., None] * xs

            def step(h, inp):
                dec_t, dtx_t, B_t, C_t = inp
                h = dec_t[:, :, None, None] * h + dtx_t[..., None] * B_t[:, None, None, :]
                y = jnp.einsum('bhpn,bn->bhp', h, C_t)
                return (h, y)
            h0 = jnp.zeros((B, HEADS, HEAD_DIM, STATE), u.dtype)
            scan_in = (jnp.moveaxis(decay, 1, 0), jnp.moveaxis(dtx, 1, 0), jnp.moveaxis(Bm, 1, 0), jnp.moveaxis(Cm, 1, 0))
            _, ys = jax.lax.scan(step, h0, scan_in)
            y = jnp.moveaxis(ys, 0, 1)
            y = y + D_skip[None, None, :, None] * xs
            y = y.reshape(B, L, INNER) * jax.nn.silu(z)
            return y @ W_out + b_out
        key = jax.random.key(seed)
        ks = jax.random.split(key, 6)
        g = lambda k, shape, sc: jax.random.normal(k, shape, jnp.float32) * sc
        return {'input_tensor': jax.random.normal(ks[0], (BATCH, SEQ, D_MODEL), jnp.float32), 'ln_gamma': jnp.ones((D_MODEL,), jnp.float32), 'ln_beta': jnp.zeros((D_MODEL,), jnp.float32), 'W_in': g(ks[1], (D_MODEL, PROJ_OUT), 0.02), 'b_in': jnp.zeros((PROJ_OUT,), jnp.float32), 'A_log': jnp.log(jnp.arange(1, HEADS + 1, dtype=jnp.float32)), 'D_skip': jnp.ones((HEADS,), jnp.float32), 'dt_bias': g(ks[2], (HEADS,), 0.1), 'W_out': g(ks[3], (INNER, D_MODEL), 0.02), 'b_out': jnp.zeros((D_MODEL,), jnp.float32)}
    _L0_attn_all = _L0_attn_setup()
    _L0_attn_in = {k: v for k, v in _L0_attn_all.items() if k in ('ln_gamma', 'ln_beta', 'W_in', 'b_in', 'A_log', 'D_skip', 'dt_bias', 'W_out', 'b_out')}
    del _L0_attn_all

    def _L0_ffn_setup():
        import jax, jax.numpy as jnp
        import numpy as np
        B, S, D = (2, 256, 256)
        E, K, I = (8, 2, 256)
        LIMIT = 7.0
        ALPHA = 1.702

        def _swiglu(t, limit):
            glu = jnp.minimum(t[..., ::2], limit)
            lin = jnp.clip(t[..., 1::2], -limit, limit)
            return glu * jax.nn.sigmoid(ALPHA * glu) * (lin + 1.0)
        key = jax.random.key(seed)
        k0, k1, k2, k3 = jax.random.split(key, 4)
        return {'x': jax.random.normal(k0, (B, S, D), jnp.float32), 'norm_w': jnp.ones((D,), jnp.float32), 'gate_w': jax.random.normal(k1, (E, D), jnp.float32) / np.sqrt(D).astype(np.float32), 'gate_b': jnp.zeros((E,), jnp.float32), 'mlp1_w': jax.random.normal(k2, (E, 2 * I, D), jnp.float32) / np.sqrt(D).astype(np.float32), 'mlp1_b': jnp.zeros((E, 2 * I), jnp.float32), 'mlp2_w': jax.random.normal(k3, (E, D, I), jnp.float32) / np.sqrt(I).astype(np.float32), 'mlp2_b': jnp.zeros((E, D), jnp.float32)}
    _L0_ffn_all = _L0_ffn_setup()
    _L0_ffn_in = {k: v for k, v in _L0_ffn_all.items() if k in ('norm_w', 'gate_w', 'gate_b', 'mlp1_w', 'mlp1_b', 'mlp2_w', 'mlp2_b')}
    del _L0_ffn_all

    def _L1_attn_setup():
        import jax, jax.numpy as jnp
        import numpy as np
        B, S, DM, H = (4, 256, 256, 16)
        D = DM // H

        def _split_heads(x):
            return x.reshape(x.shape[0], x.shape[1], H, D).transpose(0, 2, 1, 3)
        key = jax.random.key(seed)
        ks = jax.random.split(key, 16)
        sc = 0.02
        return {'hidden_states': jax.random.normal(ks[0], (B, S, DM), jnp.float32), 'wq': jax.random.normal(ks[1], (DM, DM), jnp.float32) * sc, 'bq': jax.random.normal(ks[2], (DM,), jnp.float32) * sc, 'wk': jax.random.normal(ks[3], (DM, DM), jnp.float32) * sc, 'bk': jax.random.normal(ks[4], (DM,), jnp.float32) * sc, 'wv': jax.random.normal(ks[5], (DM, DM), jnp.float32) * sc, 'bv': jax.random.normal(ks[6], (DM,), jnp.float32) * sc, 'wo': jax.random.normal(ks[7], (DM, DM), jnp.float32) * sc, 'bo': jax.random.normal(ks[8], (DM,), jnp.float32) * sc, 'wfq': jax.random.normal(ks[9], (DM, DM), jnp.float32) * sc, 'bfq': jax.random.normal(ks[10], (DM,), jnp.float32) * sc, 'wfg': jax.random.normal(ks[11], (DM, DM), jnp.float32) * sc, 'bfg': jax.random.normal(ks[12], (DM,), jnp.float32) * sc, 'up': jax.random.normal(ks[13], (H, 1, D), jnp.float32) * sc, 'uz': jax.random.normal(ks[14], (H, 1, D), jnp.float32) * sc}
    _L1_attn_all = _L1_attn_setup()
    _L1_attn_in = {k: v for k, v in _L1_attn_all.items() if k in ('wq', 'bq', 'wk', 'bk', 'wv', 'bv', 'wo', 'bo', 'wfq', 'bfq', 'wfg', 'bfg', 'up', 'uz')}
    del _L1_attn_all

    def _L1_ffn_setup():
        import jax, jax.numpy as jnp
        from jax import lax
        import numpy as np
        B, S, D, H, DO, E, K = (4, 512, 256, 1024, 256, 8, 2)
        CAP_FACTOR = 1.5
        LN_EPS = 1e-05
        key = jax.random.key(seed)
        ks = jax.random.split(key, 8)
        s_in = 1.0 / np.sqrt(D)
        s_h = 1.0 / np.sqrt(H)
        return {'x': jax.random.normal(ks[0], (B, S, D), dtype=jnp.float32), 'router_w': jax.random.normal(ks[1], (D, E), dtype=jnp.float32) * s_in, 'router_b': jnp.zeros((E,), dtype=jnp.float32), 'w1': jax.random.normal(ks[2], (E, D, H), dtype=jnp.float32) * s_in, 'b1': jnp.zeros((E, H), dtype=jnp.float32), 'w2': jax.random.normal(ks[3], (E, H, DO), dtype=jnp.float32) * s_h, 'b2': jnp.zeros((E, DO), dtype=jnp.float32), 'ln_g': jnp.ones((DO,), dtype=jnp.float32), 'ln_b': jnp.zeros((DO,), dtype=jnp.float32)}
    _L1_ffn_all = _L1_ffn_setup()
    _L1_ffn_in = {k: v for k, v in _L1_ffn_all.items() if k in ('router_w', 'router_b', 'w1', 'b1', 'w2', 'b2', 'ln_g', 'ln_b')}
    del _L1_ffn_all
    return {'x': x, 'txt': txt, 'L0_tok_W': _L0_tok_in['W'], 'L0_tok_b': _L0_tok_in['b'], 'L0_tok_class_token': _L0_tok_in['class_token'], 'L0_tok_pos_embedding': _L0_tok_in['pos_embedding'], 'L0_attn_ln_gamma': _L0_attn_in['ln_gamma'], 'L0_attn_ln_beta': _L0_attn_in['ln_beta'], 'L0_attn_W_in': _L0_attn_in['W_in'], 'L0_attn_b_in': _L0_attn_in['b_in'], 'L0_attn_A_log': _L0_attn_in['A_log'], 'L0_attn_D_skip': _L0_attn_in['D_skip'], 'L0_attn_dt_bias': _L0_attn_in['dt_bias'], 'L0_attn_W_out': _L0_attn_in['W_out'], 'L0_attn_b_out': _L0_attn_in['b_out'], 'L0_ffn_norm_w': _L0_ffn_in['norm_w'], 'L0_ffn_gate_w': _L0_ffn_in['gate_w'], 'L0_ffn_gate_b': _L0_ffn_in['gate_b'], 'L0_ffn_mlp1_w': _L0_ffn_in['mlp1_w'], 'L0_ffn_mlp1_b': _L0_ffn_in['mlp1_b'], 'L0_ffn_mlp2_w': _L0_ffn_in['mlp2_w'], 'L0_ffn_mlp2_b': _L0_ffn_in['mlp2_b'], 'L1_attn_wq': _L1_attn_in['wq'], 'L1_attn_bq': _L1_attn_in['bq'], 'L1_attn_wk': _L1_attn_in['wk'], 'L1_attn_bk': _L1_attn_in['bk'], 'L1_attn_wv': _L1_attn_in['wv'], 'L1_attn_bv': _L1_attn_in['bv'], 'L1_attn_wo': _L1_attn_in['wo'], 'L1_attn_bo': _L1_attn_in['bo'], 'L1_attn_wfq': _L1_attn_in['wfq'], 'L1_attn_bfq': _L1_attn_in['bfq'], 'L1_attn_wfg': _L1_attn_in['wfg'], 'L1_attn_bfg': _L1_attn_in['bfg'], 'L1_attn_up': _L1_attn_in['up'], 'L1_attn_uz': _L1_attn_in['uz'], 'L1_ffn_router_w': _L1_ffn_in['router_w'], 'L1_ffn_router_b': _L1_ffn_in['router_b'], 'L1_ffn_w1': _L1_ffn_in['w1'], 'L1_ffn_b1': _L1_ffn_in['b1'], 'L1_ffn_w2': _L1_ffn_in['w2'], 'L1_ffn_b2': _L1_ffn_in['b2'], 'L1_ffn_ln_g': _L1_ffn_in['ln_g'], 'L1_ffn_ln_b': _L1_ffn_in['ln_b']}

def reference(x, txt, L0_tok_W, L0_tok_b, L0_tok_class_token, L0_tok_pos_embedding, L0_attn_ln_gamma, L0_attn_ln_beta, L0_attn_W_in, L0_attn_b_in, L0_attn_A_log, L0_attn_D_skip, L0_attn_dt_bias, L0_attn_W_out, L0_attn_b_out, L0_ffn_norm_w, L0_ffn_gate_w, L0_ffn_gate_b, L0_ffn_mlp1_w, L0_ffn_mlp1_b, L0_ffn_mlp2_w, L0_ffn_mlp2_b, L1_attn_wq, L1_attn_bq, L1_attn_wk, L1_attn_bk, L1_attn_wv, L1_attn_bv, L1_attn_wo, L1_attn_bo, L1_attn_wfq, L1_attn_bfq, L1_attn_wfg, L1_attn_bfg, L1_attn_up, L1_attn_uz, L1_ffn_router_w, L1_ffn_router_b, L1_ffn_w1, L1_ffn_b1, L1_ffn_w2, L1_ffn_b2, L1_ffn_ln_g, L1_ffn_ln_b):
    import jax
    import jax.numpy as jnp

    def _L0_tok_ref(x, W, b, class_token, pos_embedding):
        import jax, jax.numpy as jnp
        import numpy as np
        P = 16

        def _patchify(x):
            B, C, H, W = x.shape
            gh, gw = (H // P, W // P)
            x = x.reshape(B, C, gh, P, gw, P)
            x = x.transpose(0, 2, 4, 1, 3, 5)
            return x.reshape(B, gh * gw, C * P * P)
        patches = _patchify(x)
        proj = jnp.einsum('bnk,dk->bnd', patches, W) + b
        B = x.shape[0]
        cls = jnp.broadcast_to(class_token, (B, 1, proj.shape[-1]))
        out = jnp.concatenate([cls, proj], axis=1) + pos_embedding
        return out

    def _L0_attn_ref(input_tensor, ln_gamma, ln_beta, W_in, b_in, A_log, D_skip, dt_bias, W_out, b_out):
        import jax, jax.numpy as jnp
        import numpy as np
        D_MODEL = 256
        STATE = 64
        HEADS = 8
        EXPAND = 2
        INNER = EXPAND * D_MODEL
        HEAD_DIM = INNER // HEADS
        PROJ_OUT = 2 * INNER + 2 * STATE + HEADS
        BATCH, SEQ = (2, 256)
        EPS = 1e-05

        def _layer_norm(x, gamma, beta):
            mu = jnp.mean(x, axis=-1, keepdims=True)
            xc = x - mu
            var = jnp.mean(xc * xc, axis=-1, keepdims=True)
            return xc * jax.lax.rsqrt(var + EPS) * gamma + beta

        def _mamba2(u, W_in, b_in, A_log, D_skip, dt_bias, W_out, b_out):
            B, L, _ = u.shape
            zxbcdt = u @ W_in + b_in
            z = zxbcdt[..., :INNER]
            xs = zxbcdt[..., INNER:2 * INNER].reshape(B, L, HEADS, HEAD_DIM)
            Bm = zxbcdt[..., 2 * INNER:2 * INNER + STATE]
            Cm = zxbcdt[..., 2 * INNER + STATE:2 * INNER + 2 * STATE]
            dt = jax.nn.softplus(zxbcdt[..., 2 * INNER + 2 * STATE:] + dt_bias)
            A = -jnp.exp(A_log)
            decay = jnp.exp(dt * A)
            dtx = dt[..., None] * xs

            def step(h, inp):
                dec_t, dtx_t, B_t, C_t = inp
                h = dec_t[:, :, None, None] * h + dtx_t[..., None] * B_t[:, None, None, :]
                y = jnp.einsum('bhpn,bn->bhp', h, C_t)
                return (h, y)
            h0 = jnp.zeros((B, HEADS, HEAD_DIM, STATE), u.dtype)
            scan_in = (jnp.moveaxis(decay, 1, 0), jnp.moveaxis(dtx, 1, 0), jnp.moveaxis(Bm, 1, 0), jnp.moveaxis(Cm, 1, 0))
            _, ys = jax.lax.scan(step, h0, scan_in)
            y = jnp.moveaxis(ys, 0, 1)
            y = y + D_skip[None, None, :, None] * xs
            y = y.reshape(B, L, INNER) * jax.nn.silu(z)
            return y @ W_out + b_out
        normed = _layer_norm(input_tensor, ln_gamma, ln_beta)
        out = _mamba2(normed, W_in, b_in, A_log, D_skip, dt_bias, W_out, b_out)
        return input_tensor + out

    def _L0_ffn_ref(x, norm_w, gate_w, gate_b, mlp1_w, mlp1_b, mlp2_w, mlp2_b):
        import jax, jax.numpy as jnp
        import numpy as np
        B, S, D = (2, 256, 256)
        E, K, I = (8, 2, 256)
        LIMIT = 7.0
        ALPHA = 1.702

        def _swiglu(t, limit):
            glu = jnp.minimum(t[..., ::2], limit)
            lin = jnp.clip(t[..., 1::2], -limit, limit)
            return glu * jax.nn.sigmoid(ALPHA * glu) * (lin + 1.0)
        eps = jnp.finfo(x.dtype).eps
        h = x * jax.lax.rsqrt(jnp.mean(x * x, axis=-1, keepdims=True) + eps) * norm_w
        flat = h.reshape(-1, D)
        logits = flat @ gate_w.T + gate_b
        vals, idx = jax.lax.top_k(logits, K)
        wts = jax.nn.softmax(vals, axis=-1)
        t1 = jnp.einsum('td,efd->tef', flat, mlp1_w) + mlp1_b
        act = _swiglu(t1, LIMIT)
        y = jnp.einsum('tei,edi->ted', act, mlp2_w) + mlp2_b
        sel = jnp.take_along_axis(y, idx[:, :, None], axis=1)
        out = jnp.sum(sel * wts[:, :, None], axis=1).reshape(x.shape)
        return x + out

    def _L1_attn_ref(hidden_states, wq, bq, wk, bk, wv, bv, wo, bo, wfq, bfq, wfg, bfg, up, uz):
        import jax, jax.numpy as jnp
        import numpy as np
        B, S, DM, H = (4, 256, 256, 16)
        D = DM // H

        def _split_heads(x):
            return x.reshape(x.shape[0], x.shape[1], H, D).transpose(0, 2, 1, 3)
        key_len = hidden_states.shape[1]
        mixed_q = hidden_states @ wq + bq
        mixed_k = hidden_states @ wk + bk
        mixed_v = hidden_states @ wv + bv
        glo = jnp.mean(mixed_q, axis=1, keepdims=True)
        c = jnp.tanh(mixed_q @ wfq + bfq + (glo @ wfg + bfg))
        c = _split_heads(c)
        p = jnp.sum(c * up[None], axis=-1)
        z = jnp.sum(c * uz[None], axis=-1)
        P = jax.nn.sigmoid(p) * key_len
        Z = jax.nn.sigmoid(z) * key_len
        j = jnp.arange(key_len, dtype=P.dtype)
        G = -(j[None, None, None, :] - P[..., None]) ** 2 * 2.0 / Z[..., None] ** 2
        q = _split_heads(mixed_q)
        k = _split_heads(mixed_k)
        v = _split_heads(mixed_v)
        scores = jnp.einsum('bhqd,bhkd->bhqk', q, k) / jnp.sqrt(jnp.float32(D))
        scores = scores + G
        probs = jax.nn.softmax(scores, axis=-1)
        ctx = jnp.einsum('bhqk,bhkd->bhqd', probs, v)
        ctx = ctx.transpose(0, 2, 1, 3).reshape(ctx.shape[0], key_len, H * D)
        return ctx @ wo + bo

    def _L1_ffn_ref(x, router_w, router_b, w1, b1, w2, b2, ln_g, ln_b):
        import jax, jax.numpy as jnp
        from jax import lax
        import numpy as np
        B, S, D, H, DO, E, K = (4, 512, 256, 1024, 256, 8, 2)
        CAP_FACTOR = 1.5
        LN_EPS = 1e-05
        Bx, Sx, Dx = x.shape
        N = Bx * Sx
        capacity = max(int(N * CAP_FACTOR / E), K)
        logits = jnp.einsum('bsd,de->bse', x, router_w) + router_b
        probs = jax.nn.softmax(logits, axis=-1)
        topv, topi = lax.top_k(probs, K)
        topv = topv / topv.sum(axis=-1, keepdims=True)
        flat_i = topi.reshape(-1)
        flat_v = topv.reshape(-1)
        mask = flat_i[None, :] == jnp.arange(E)[:, None]
        prio = jnp.where(mask, flat_v[None, :], -1.0)
        pv, pp = lax.top_k(prio, capacity)
        valid = pv > 0.0
        tok = jnp.where(valid, pp // K, 0)
        w = jnp.where(valid, pv, 0.0)
        x_flat = x.reshape(N, Dx)
        xin = x_flat[tok]
        h = jax.nn.gelu(jnp.einsum('ecd,edh->ech', xin, w1) + b1[:, None, :], approximate=False)
        out_e = jnp.einsum('ech,eho->eco', h, w2) + b2[:, None, :]
        out_e = out_e * w[..., None]
        out = jnp.zeros((N, DO), dtype=x.dtype)
        out = out.at[tok.reshape(-1)].add(out_e.reshape(-1, DO))
        out = out.reshape(Bx, Sx, DO)
        mu = out.mean(axis=-1, keepdims=True)
        var = out.var(axis=-1, keepdims=True)
        out = (out - mu) / jnp.sqrt(var + LN_EPS) * ln_g + ln_b
        return out
    h = _L0_tok_ref(x, L0_tok_W, L0_tok_b, L0_tok_class_token, L0_tok_pos_embedding)
    h = jnp.concatenate([h, txt], axis=1)
    h = h + _L0_attn_ref(_layernorm(h, axis=-1), L0_attn_ln_gamma, L0_attn_ln_beta, L0_attn_W_in, L0_attn_b_in, L0_attn_A_log, L0_attn_D_skip, L0_attn_dt_bias, L0_attn_W_out, L0_attn_b_out)
    h = h + _L0_ffn_ref(_layernorm(h, axis=-1), L0_ffn_norm_w, L0_ffn_gate_w, L0_ffn_gate_b, L0_ffn_mlp1_w, L0_ffn_mlp1_b, L0_ffn_mlp2_w, L0_ffn_mlp2_b)
    h = h + _L1_attn_ref(_layernorm(h, axis=-1), L1_attn_wq, L1_attn_bq, L1_attn_wk, L1_attn_bk, L1_attn_wv, L1_attn_bv, L1_attn_wo, L1_attn_bo, L1_attn_wfq, L1_attn_bfq, L1_attn_wfg, L1_attn_bfg, L1_attn_up, L1_attn_uz)
    h = h + _L1_ffn_ref(_layernorm(h, axis=-1), L1_ffn_router_w, L1_ffn_router_b, L1_ffn_w1, L1_ffn_b1, L1_ffn_w2, L1_ffn_b2, L1_ffn_ln_g, L1_ffn_ln_b)
    return h

_drawn_inputs = setup_inputs


def setup_inputs(seed=0):
    import zlib

    import numpy as np

    out = dict(_drawn_inputs(seed))
    spreads = {'L0_attn_ln_gamma': (1.0, 0.2),
     'L0_attn_ln_beta': (0.0, 0.1),
     'L0_attn_b_in': (0.0, 0.1),
     'L0_attn_D_skip': (1.0, 0.6),
     'L0_attn_b_out': (0.0, 0.1),
     'L0_ffn_norm_w': (1.0, 0.2),
     'L0_ffn_gate_b': (0.0, 0.1),
     'L0_ffn_mlp1_b': (0.0, 0.1),
     'L0_ffn_mlp2_b': (0.0, 0.1),
     'L1_ffn_router_b': (0.0, 0.1),
     'L1_ffn_b1': (0.0, 0.1),
     'L1_ffn_b2': (0.0, 0.1),
     'L1_ffn_ln_g': (1.0, 0.2),
     'L1_ffn_ln_b': (0.0, 0.1)}
    factors = {'L0_attn_A_log': 33.627,
     'L0_attn_dt_bias': 4.788,
     'L1_attn_wq': 7.178,
     'L1_attn_bq': 7.269,
     'L1_attn_wk': 7.191,
     'L1_attn_bk': 200.0,
     'L1_attn_wv': 2.703,
     'L1_attn_bv': 3.384,
     'L1_attn_wfq': 8.0,
     'L1_attn_bfq': 136.012,
     'L1_attn_wfg': 8.0,
     'L1_attn_bfg': 116.274,
     'L1_attn_up': 8.0,
     'L1_attn_uz': 8.0}
    for name, (base, spread) in spreads.items():
        noise = np.random.default_rng([zlib.crc32(name.encode()), seed]).standard_normal(out[name].shape)
        drawn = base * np.exp(spread * noise) if base else spread * noise
        out[name] = jnp.asarray(drawn.astype(out[name].dtype))
    for name, factor in factors.items():
        out[name] = (out[name] * factor).astype(out[name].dtype)
    return out
```

```python
from contextlib import ExitStack

import concourse.bass as bass
from concourse import mybir

ALU = mybir.AluOpType
ACT = mybir.ActivationFunctionType
AX = mybir.AxisListType
F32 = mybir.dt.float32
BF16 = mybir.dt.bfloat16
U32 = mybir.dt.uint32
I32 = mybir.dt.int32

P = 128
B, NPATCH, NTXT = 32, 36, 32
S = 1 + NPATCH + NTXT
N = B * S
T = -(-N // P)
NPAD = T * P
LAST = N - (T - 1) * P
D = 256
DC = D // P
KP = 768
KC = KP // P
PT = B * NPATCH // P
POS = P // B
HM, HD, NST = 8, 64, 64
INNER = HM * HD
IC = INNER // P
PROJ = 2 * INNER + 2 * NST + HM
HS = HM * S
G4 = 4 * S
NG = N // G4
E8 = 8
ET = E8 * T
F1 = 512
NBLK = (2 * N + E8 * (P - 1)) // P
NH, AD = 16, 16
AS = NH * S
HID = 1024
MC = HID // P
CAP = max(int(N * 1.5 / E8), 2)
XG, XQ = 4, 104
ROWS = XG * XQ
LN_EPS = 1e-5
RMS_EPS = 1.1920928955078125e-07
FAR = 1.0e6


def tile_of(x, i, n=1):
    return x[:, bass.ds(i, n), :].rearrange("p a b -> p (a b)")


def cols(x, start, n):
    return x[:, :, bass.ds(start, n)]


def bc(ap, shape):
    return ap.broadcast_to(shape)


def mid(ap2, n):
    p, k = ap2.shape
    return ap2.unsqueeze(1).broadcast_to([p, n, k])


def last(ap2, n):
    p, k = ap2.shape
    return ap2.unsqueeze(2).broadcast_to([p, k, n])


class Steps:

    def __init__(self, eng, sem):
        self.eng, self.sem, self.n = eng, sem, 0

    def after(self, ins):
        self.n += 1
        ins.then_inc(self.sem, 1)
        self.eng.wait_ge(self.sem, self.n)


def mean_and_var(nc, steps, st, mean, var, tmp):
    me, ve, mo, vo = st[:, :, 1], st[:, :, 2], st[:, :, 4], st[:, :, 5]
    steps.after(nc.vector.tensor_tensor(mean, me, mo, ALU.add))
    steps.after(nc.vector.tensor_scalar(mean, mean, 0.5, None, ALU.mult))
    steps.after(nc.vector.tensor_tensor(tmp, me, mo, ALU.subtract))
    steps.after(nc.vector.tensor_tensor(var, ve, vo, ALU.add))
    steps.after(nc.vector.scalar_tensor_tensor(out=tmp, in0=tmp, scalar=0.25, in1=tmp, op0=ALU.mult, op1=ALU.mult))
    steps.after(nc.vector.scalar_tensor_tensor(out=var, in0=var, scalar=1.0 / D, in1=tmp, op0=ALU.mult, op1=ALU.add))


def build(nc, a, out):
    with ExitStack() as top:
        named = {}

        def unique(name):
            named[name] = named.get(name, 0) + 1
            return name if named[name] == 1 else f"{name}_{named[name]}"

        def sb(name, shape, dt=F32, ctx=top):
            return ctx.enter_context(nc.sbuf_tensor(unique(name), shape, dt))

        phase_sems = []

        def sem(name, ctx=None):
            handle = nc.alloc_semaphore(name=unique(name))
            if ctx is not None:
                phase_sems.append(handle)
            return handle

        def scratch(name, shape):
            return nc.dram_tensor(name, shape, F32, kind="Internal").ap()

        m = {}
        m["sb"], m["sem"] = sb, sem
        m["ps"] = lambda name, shape, ctx, dt=F32: ctx.enter_context(nc.psum_tensor(unique(name), shape, dt))
        m["tokens"] = scratch("tokens", (N, D))
        m["bcast"] = scratch("bcast", (B, 2, HM, S))
        m["rows1"] = scratch("rows1", (NBLK * P, D))
        m["outs1"] = scratch("outs1", (NBLK * P, D))
        m["rows2"] = scratch("rows2", (E8 * ROWS, D))
        m["outs2"] = scratch("outs2", (E8 * ROWS, D))
        m["H"] = sb("H", [P, T, D])
        m["A"] = sb("A", [P, T, D])
        m["ident"] = sb("ident", [P, P])
        m["st"] = sb("st", [P, T, 6])
        for name in ("mean", "var", "rstd", "tmp", "std"):
            m[name] = sb(name, [P, T])
        m["eps"] = sb("eps", [P, 2])
        for name, shape, dt in (("before", [P, P], BF16), ("ones_bf", [P, P], BF16), ("keep", [P, ET], F32), ("iota8", [P, E8], F32), ("valid", [P, T], F32)):
            m[name] = sb(name, shape, dt)
        m["lg"], m["w"] = sb("lg", [P, T, E8]), sb("w", [P, 2, T])
        m["gidx"], m["sidx"] = sb("gidx", [P, 2, T], U32), sb("sidx", [P, 2, T], U32)
        m["w1"] = sb("moe1_w1", [P, E8, DC, F1])
        m["w2"] = sb("moe1_w2", [P, E8, DC, D])
        m["moe1_loaded"] = sem("moe1_loaded")
        for phase in (embed, mamba, moe1, attention, moe2):
            with ExitStack() as ctx:
                phase(nc, a, out, m, ctx)
            nc.clear_and_free_semaphores(phase_sems)
            nc.all_engine_barrier()
            phase_sems.clear()


def embed(nc, a, out, m, ctx):
    sb = lambda name, shape, dt=F32: m["sb"](name, shape, dt, ctx)
    sem = lambda name: m["sem"](name, ctx)
    tokens, H, A = m["tokens"], m["H"], m["A"]
    rows = tokens.rearrange("(b s) d -> b s d", s=S)
    w = sb("patch_w", [P, KC, D])
    patches = sb("patches", [P, 3, KC, P])
    pos = sb("pos", [P, PT, D])
    bias = sb("patch_b", [P, D])
    cls = sb("cls", [B, 2, D])
    emb = sb("emb", [P, 3, D])
    zero = sb("zero", [P, 8 * D])
    acc = [m["ps"](f"patch_acc{i}", [P, 512], ctx) for i in range(3)]
    w_loaded, consts, patches_free = map(sem, ("pw_loaded", "pc_loaded", "p_free"))
    patches_loaded = [sem(f"patches_loaded{p}") for p in range(3)]
    emb_stored = [sem(f"emb_stored{p}") for p in range(3)]
    pos_ready, acc_ready = map(sem, ("pos_ready", "acc_ready"))
    cls_ready, direct, zeroed, zeros_stored, h_loaded, pad_ready = map(
        sem, ("cls_ready", "direct", "zeroed", "zeros_stored", "h_loaded", "pad_ready"))

    with nc.Block() as block:
        @block.sync
        def _(sp):
            sp.dma_start(w[:, :, :], a["patch_w"]).then_inc(w_loaded, 16)
            sp.dma_start(bias[:, :], a["patch_b"].partition_broadcast(P)).then_inc(consts, 16)
            for q in range(POS):
                src = a["pos"][1:, :].rearrange("(t q) d -> q t d", q=POS)[q]
                sp.dma_start(pos[q * B:(q + 1) * B, :, :], src.partition_broadcast(B)).then_inc(consts, 16)
            sp.dma_start(cls[:, 0, :], a["cls"].partition_broadcast(B)).then_inc(consts, 16)
            sp.dma_start(cls[:, 1, :], a["pos"][0].partition_broadcast(B)).then_inc(consts, 16)
            with sp.Fori(0, PT // 3) as j:
                for p in range(3):
                    sp.wait_ge(patches_free, j * 3 + (p + 1))
                    sp.dma_start(patches[:, p, :, :], a["patches"][bass.ds(j * 3 + p, 1)].rearrange("o p c q -> (o p) c q")).then_inc(patches_loaded[p], 16)
            for name in ("ident", "keep", "iota8", "valid"):
                sp.dma_start(m[name][:, :], a[name]).then_inc(h_loaded, 16)
            for name in ("before", "ones_bf"):
                sp.dma_start(m[name][:, :].bitcast(mybir.dt.uint16), a[name]).then_inc(h_loaded, 16)
            sp.dma_start(rows[:, 1 + NPATCH:, :], a["txt"]).then_inc(direct, 16)
            sp.wait_ge(cls_ready, 1)
            sp.dma_start(rows[:, 0, :], cls[:, 0, :]).then_inc(direct, 16)
            sp.wait_ge(zeroed, 1)
            for name in ("rows1", "rows2"):
                r = m[name].rearrange("(n p) d -> p n d", p=P)
                for c in range(0, r.shape[1], 8):
                    k = min(8, r.shape[1] - c)
                    sp.dma_start(r[:, c:c + k, :], zero[:, 0:k * D].rearrange("p (n d) -> p n d", d=D)).then_inc(zeros_stored, 16)
            sp.wait_ge(direct, 32)
            for p in range(3):
                sp.wait_ge(emb_stored[p], 16 * POS * (PT // 3 + 1))
            sp.wait_ge(pad_ready, 1)
            full = (T - 1) * P
            sp.dma_start(H[:, 0:T - 1, :], tokens[0:full, :].rearrange("(t p) d -> p t d", p=P)).then_inc(h_loaded, 16)
            sp.dma_start(H[0:LAST, T - 1, :], tokens[full:N, :]).then_inc(h_loaded, 16)
            sp.dma_start(m["w1"][:, :, :, :], a["moe1_w1"]).then_inc(m["moe1_loaded"], 16)
            sp.dma_start(m["w2"][:, :, :, :], a["moe1_w2"]).then_inc(m["moe1_loaded"], 16)
            sp.wait_ge(h_loaded, 16 * 8)
            sp.wait_ge(zeros_stored, 16 * (-(-NBLK // 8) + -(-(E8 * ROWS // P) // 8)))

        @block.gpsimd
        def _(pool):
            nc.gpsimd.memset(zero[:, :], 0.0).then_inc(zeroed, 1)
            nc.gpsimd.memset(H[:, T - 1, :], 0.0).then_inc(pad_ready, 1)
            nc.gpsimd.memset(m["eps"][:, 0:1], LN_EPS)
            nc.gpsimd.memset(m["eps"][:, 1:2], RMS_EPS)

        @block.tensor
        def _(pe):
            pe.sem_inc(patches_free, 3)
            pe.wait_ge(w_loaded, 16)
            with pe.Fori(0, PT // 3) as j:
                for p in range(3):
                    pe.wait_ge(patches_loaded[p], j * 16 + 16)
                    pe.wait_ge(acc_ready, j * 3 + (p + 1))
                    for c in range(KC):
                        mm = nc.tensor.matmul(acc[p][:, 0:D], patches[:, p, c, :], w[:, c, :], start=(c == 0), stop=(c == KC - 1))
                    mm.then_inc(patches_free, 1)

        @block.vector
        def _(v):
            v.sem_inc(acc_ready, 3)
            v.wait_ge(consts, 16 * (3 + POS))
            nc.vector.tensor_tensor(cls[:, 0, :], cls[:, 0, :], cls[:, 1, :], ALU.add).then_inc(cls_ready, 1)
            nc.vector.tensor_tensor(pos[:, :, :], pos[:, :, :], mid(bias[:, :], PT), ALU.add).then_inc(pos_ready, 1)
            v.wait_ge(pos_ready, 1)
            with v.Fori(0, PT // 3) as j:
                for p in range(3):
                    v.wait_ge(patches_free, j * 3 + (p + 4))
                    v.wait_ge(emb_stored[p], j * (16 * POS) + 16 * POS)
                    nc.vector.tensor_tensor(emb[:, p, :], acc[p][:, 0:D], tile_of(pos, j * 3 + p), ALU.add).then_inc(acc_ready, 1)

        @block.scalar
        def _(act):
            for p in range(3):
                act.sem_inc(emb_stored[p], 16 * POS)
            with act.Fori(0, PT // 3) as j:
                for p in range(3):
                    act.wait_ge(acc_ready, j * 3 + (p + 4))
                    for q in range(POS):
                        dst = rows[:, bass.ds((j * 3 + p) * POS + (1 + q), 1), :].rearrange("b o d -> b (o d)")
                        act.dma_start(dst, emb[q * B:(q + 1) * B, p, :]).then_inc(emb_stored[p], 16)


def layer_stats(nc, v, steps, m, x, sem_name_done):
    with v.Fori(0, T // 3) as j:
        for p in range(3):
            nc.vector.bn_stats(m["st"][:, bass.ds(j * 3 + p, 1), :], x[:, bass.ds(j * 3 + p, 1), :]).then_inc(sem_name_done, 1)
    v.wait_ge(sem_name_done, T)
    mean_and_var(nc, steps, m["st"], m["mean"][:, :], m["var"][:, :], m["tmp"][:, :])


def normalise(nc, dst, src, m, i):
    return nc.vector.tensor_scalar(dst, src, m["mean"][:, bass.ds(i, 1)], m["rstd"][:, bass.ds(i, 1)], ALU.subtract, ALU.mult)


def pre_mamba(nc, a, out, m, ctx):
    sem = lambda name: m["sem"](name, ctx)
    H, A, uT, ident = m["H"], m["A"], m["uT"], m["ident"]
    gamma = m["sb"]("m_gamma", [P, DC], F32, ctx)
    beta = m["sb"]("m_beta", [P, DC], F32, ctx)
    bout = m["sb"]("m_bout", [P, D], F32, ctx)
    u = m["sb"]("u", [P, 2, D], F32, ctx)
    ut = [m["ps"](f"ut{i}", [P, DC, P], ctx) for i in range(2)]
    stats1, stats2, var_ready, std_ready, dve, norm_ready, u_ready, ut_ready, ut_free, consts, summed = map(
        sem, ("stats1", "stats2", "var_ready", "std_ready", "dve", "norm_ready", "u_ready", "ut_ready", "ut_free", "gb", "summed"))

    with nc.Block() as block:
        @block.sync
        def _(sp):
            sp.dma_start(gamma[:, :], a["m_gamma"]).then_inc(consts, 16)
            sp.dma_start(beta[:, :], a["m_beta"]).then_inc(consts, 16)
            sp.dma_start(bout[:, :], a["m_bout"].partition_broadcast(P)).then_inc(consts, 16)
            sp.wait_ge(consts, 48)

        @block.vector
        def _(v):
            steps = Steps(v, dve)
            layer_stats(nc, v, steps, m, H, stats1)
            v.sem_inc(var_ready, 1)
            v.wait_ge(std_ready, 1)
            steps.after(nc.vector.reciprocal(m["rstd"][:, :], m["std"][:, :]))
            with v.Fori(0, T // 2) as j:
                for p in range(2):
                    normalise(nc, tile_of(A, j * 2 + p), tile_of(H, j * 2 + p), m, j * 2 + p).then_inc(norm_ready, 1)
            v.wait_ge(norm_ready, T)
            layer_stats(nc, v, steps, m, A, stats2)
            v.sem_inc(var_ready, 1)
            v.wait_ge(std_ready, 2)
            steps.after(nc.vector.reciprocal(m["rstd"][:, :], m["std"][:, :]))
            with v.Fori(0, T // 2) as j:
                for p in range(2):
                    v.wait_ge(ut_ready, j * 2 + (p + 1))
                    normalise(nc, u[:, p, :], tile_of(A, j * 2 + p), m, j * 2 + p).then_inc(u_ready, 1)

        @block.gpsimd
        def _(pool):
            pool.wait_ge(consts, 48)
            pool.wait_ge(norm_ready, T)
            nc.gpsimd.tensor_tensor(H[:, :, :], H[:, :, :], A[:, :, :], ALU.add).then_inc(summed, 1)
            pool.wait_ge(summed, 1)
            nc.gpsimd.tensor_tensor(H[:, :, :], H[:, :, :], mid(bout[:, :], T), ALU.add).then_inc(summed, 1)

        @block.scalar
        def _(act):
            for n in range(2):
                act.wait_ge(var_ready, n + 1)
                nc.scalar.activation(m["std"][:, :], m["var"][:, :], ACT.Sqrt, bias=m["eps"][:, 0:1]).then_inc(std_ready, 1)
            act.wait_ge(consts, 48)
            act.sem_inc(ut_free, 2)
            with act.Fori(0, T // 2) as j:
                for p in range(2):
                    act.wait_ge(ut_ready, j * 2 + (p + 3))
                    for c in range(DC):
                        ins = nc.scalar.activation(uT[:, c, bass.ds((j * 2 + p) * P, P)], ut[p][:, c, :], ACT.Identity,
                                                   bias=beta[:, c:c + 1], scale=gamma[:, c:c + 1])
                    ins.then_inc(ut_free, 1)

        @block.tensor
        def _(pe):
            pe.sem_inc(ut_ready, 2)
            with pe.Fori(0, T // 2) as j:
                for p in range(2):
                    pe.wait_ge(u_ready, j * 2 + (p + 1))
                    pe.wait_ge(ut_free, j * 2 + (p + 1))
                    for c in range(DC):
                        ins = nc.tensor.transpose(ut[p][:, c, :], u[:, p, c * P:(c + 1) * P], ident[:, :])
                    ins.then_inc(ut_ready, 1)


def mamba(nc, a, out, m, ctx):
    sb = lambda name, shape: m["sb"](name, shape, F32, ctx)
    m["uT"] = sb("uT", [P, DC + 1, NPAD])
    pre_ctx = ExitStack()
    with pre_ctx:
        pre_mamba(nc, a, out, m, pre_ctx)
    m["cT"] = sb("cT", [NST, NPAD])
    m["gate"] = sb("gate", [P, IC, NPAD])
    m["win"] = sb("win", [P, DC, PROJ])
    for part in (mamba_project, mamba_core, mamba_out):
        with ExitStack() as c:
            part(nc, a, out, m, c)


def mamba_project(nc, a, out, m, ctx):
    sb = lambda name, shape: m["sb"](name, shape, F32, ctx)
    sem = lambda name: m["sem"](name, ctx)
    uT, cT, gate, win = m["uT"], m["cT"], m["gate"], m["win"]
    bz, bb, bcc = sb("bz", [P, IC]), sb("bb", [NST, 1]), sb("bcc", [NST, 1])
    bdt, dtb, alog = sb("bdt", [HM, 1]), sb("dtb", [HM, 1]), sb("alog", [HM, 1])
    dt, low, dec = sb("dt", [HM, N]), sb("low", [HM, N]), sb("dec", [HM, N])
    loaded, dve, dt_done, bc_done, psum_free, dt_raw, soft, decayed, stored, z_done, z_free, padded, prep = map(
        sem, ("pj_loaded", "pj_dve", "dt_done", "bc_done", "bc_free", "dt_raw", "soft", "decayed", "dt_stored", "z_done", "z_free", "padded", "prep"))
    OB, OC, ODT = 2 * INNER, 2 * INNER + NST, 2 * INNER + 2 * NST

    with ExitStack() as c1:
        acc = [[m["ps"](f"acc_{k}{i}", [P, 512], c1) for i in range(2)] for k in ("dt", "b", "c")]
        with nc.Block() as block:
            @block.sync
            def _(sp):
                sp.dma_start(win[:, :, :], a["m_win"]).then_inc(loaded, 16)
                for t, k in ((bz, "m_bz"), (bb, "m_bb"), (bcc, "m_bc"), (bdt, "m_bdt"), (dtb, "m_dtb"), (alog, "m_alog")):
                    sp.dma_start(t[:, :], a[k]).then_inc(loaded, 16)
                sp.wait_ge(loaded, 7 * 16)

            @block.gpsimd
            def _(pool):
                nc.gpsimd.memset(uT[NST:P, DC, :], 0.0).then_inc(padded, 1)
                pool.wait_ge(padded, 1)
                nc.gpsimd.memset(gate[:, :, N:NPAD], 0.0).then_inc(padded, 1)

            @block.tensor
            def _(pe):
                pe.wait_ge(loaded, 7 * 16)
                with pe.Fori(0, NG // 2) as j:
                    for p in range(2):
                        pe.wait_ge(psum_free, j * 2 + (p + 1))
                        for k, (o, n) in enumerate(((ODT, HM), (OB, NST), (OC, NST))):
                            for c in range(DC):
                                mm = nc.tensor.matmul(acc[k][p][0:n, 0:G4], win[:, c, o:o + n], uT[:, c, bass.ds((j * 2 + p) * G4, G4)],
                                                      start=(c == 0), stop=(c == DC - 1))
                        mm.then_inc(bc_done, 1)

            @block.vector
            def _(v):
                steps = Steps(v, dve)
                v.sem_inc(psum_free, 2)
                v.wait_ge(loaded, 7 * 16)
                steps.after(nc.vector.tensor_tensor(bdt[:, :], bdt[:, :], dtb[:, :], ALU.add))
                with v.Fori(0, NG // 2) as j:
                    for p in range(2):
                        v.wait_ge(bc_done, j * 2 + (p + 1))
                        here = bass.ds((j * 2 + p) * G4, G4)
                        nc.vector.tensor_scalar(dt[:, here], acc[0][p][0:HM, 0:G4], bdt[:, 0:1], None, ALU.add)
                        nc.vector.tensor_scalar(uT[0:NST, DC, here], acc[1][p][0:NST, 0:G4], bb[:, 0:1], None, ALU.add)
                        nc.vector.tensor_scalar(cT[:, here], acc[2][p][0:NST, 0:G4], bcc[:, 0:1], None, ALU.add).then_inc(psum_free, 1)

    zacc = [[m["ps"](f"zacc{i}{k}", [P, 512], ctx) for k in range(IC)] for i in range(2)]
    rows = m["bcast"]
    with nc.Block() as block:
        @block.vector
        def _(v):
            nc.vector.tensor_scalar(low[:, :], dt[:, :], -1.0, None, ALU.mult).then_inc(dt_raw, 1)
            v.wait_ge(dt_raw, 1)
            nc.vector.tensor_tensor(low[:, :], low[:, :], dt[:, :], ALU.min).then_inc(dt_raw, 1)
            v.wait_ge(soft, 2)
            nc.vector.scalar_tensor_tensor(out=dt[:, :], in0=dt[:, :], scalar=0.0, in1=low[:, :], op0=ALU.max, op1=ALU.add).then_inc(dt_raw, 1)
            v.wait_ge(decayed, 2)
            nc.vector.memset(dec[:, :].rearrange("h (b s) -> h b s", s=S)[:, :, 0:1], 0.0).then_inc(dt_raw, 1)

        @block.scalar
        def _(act):
            act.wait_ge(dt_raw, 2)
            nc.scalar.activation(low[:, :], low[:, :], ACT.Exp).then_inc(soft, 1)
            act.wait_ge(soft, 1)
            nc.scalar.activation(low[:, :], low[:, :], ACT.Ln, bias=1.0).then_inc(soft, 1)
            nc.scalar.activation(alog[:, :], alog[:, :], ACT.Exp).then_inc(decayed, 1)
            act.wait_ge(decayed, 1)
            act.wait_ge(dt_raw, 3)
            nc.scalar.activation(dec[:, :], dt[:, :], ACT.Copy, scale=alog[:, 0:1]).then_inc(prep, 1)
            act.wait_ge(prep, 1)
            nc.scalar.activation(dec[:, :], dec[:, :], ACT.Exp, scale=-1.0).then_inc(decayed, 1)
            act.sem_inc(z_free, 2)
            with act.Fori(0, NG // 2) as j:
                for p in range(2):
                    act.wait_ge(z_done, j * 2 + (p + 1))
                    for k in range(IC):
                        ins = nc.scalar.activation(gate[:, k, bass.ds((j * 2 + p) * G4, G4)], zacc[p][k][:, 0:G4], ACT.Silu, bias=bz[:, k:k + 1])
                    ins.then_inc(z_free, 1)

        @block.sync
        def _(sp):
            sp.wait_ge(dt_raw, 4)
            sp.dma_start(rows[:, 0].rearrange("b h s -> h b s"), dec[:, :].rearrange("h (b s) -> h b s", s=S)).then_inc(stored, 16)
            sp.dma_start(rows[:, 1].rearrange("b h s -> h b s"), dt[:, :].rearrange("h (b s) -> h b s", s=S)).then_inc(stored, 16)
            sp.wait_ge(stored, 32)

        @block.tensor
        def _(pe):
            with pe.Fori(0, NG // 2) as j:
                for p in range(2):
                    pe.wait_ge(z_free, j * 2 + (p + 1))
                    for k in range(IC):
                        for c in range(DC):
                            mm = nc.tensor.matmul(zacc[p][k][:, 0:G4], win[:, c, k * P:(k + 1) * P], uT[:, c, bass.ds((j * 2 + p) * G4, G4)],
                                                  start=(c == 0), stop=(c == DC - 1))
                    mm.then_inc(z_done, 1)


def mamba_core(nc, a, out, m, ctx):
    sb = lambda name, shape: m["sb"](name, shape, F32, ctx)
    sem = lambda name: m["sem"](name, ctx)
    uT, cT, gate, win, ident = m["uT"], m["cT"], m["gate"], m["win"], m["ident"]
    KB = 80
    us = sb("us", [P, 2, DC + 1, S])
    rows = sb("rows_b", [KB, 2, 2, HS])
    xs = sb("xs", [S, 2, INNER])
    inj = sb("inj", [S, 2, HS])
    sc = sb("sc", [S, 2, HS])
    bx = sb("bx", [S, INNER])
    dd = sb("dd", [S, HM])
    dI = sb("dI", [S, HS])
    x_ps = [m["ps"](f"x_ps{i}", [P, 512], ctx) for i in range(2)]
    g_ps = [m["ps"](f"g_ps{i}", [P, 512], ctx) for i in range(2)]
    y_ps = [m["ps"](f"y_ps{i}", [P, IC, P], ctx) for i in range(2)]
    consts, d_ready, us_ready, xg_done, x_ready, inj_ready, scanned, mult, m_ready, y_done, y_out = map(
        sem, ("mc_consts", "d_ready", "us_ready", "xg_done", "x_ready", "inj_ready", "scanned", "mult", "m_ready", "y_done", "y_out"))
    rows_loaded = [sem(f"rows_loaded{p}") for p in range(2)]
    S3 = [S, HM, S]

    def v3(x):
        return x.rearrange("p (h s) -> p h s", s=S)

    with nc.Block() as block:
        @block.sync
        def _(sp):
            sp.dma_start(bx[:, :], a["m_bx"].partition_broadcast(S)).then_inc(consts, 16)
            sp.dma_start(dd[:, :], a["m_d"].partition_broadcast(S)).then_inc(consts, 16)
            with sp.Fori(0, B // 2) as j:
                for p in range(2):
                    sp.wait_ge(scanned, j * 2 + (p + 1))
                    sp.dma_start(rows[:, p, :, :], m["bcast"][bass.ds(j * 2 + p, 1)].rearrange("o k h s -> (o k) (h s)").partition_broadcast(KB)).then_inc(rows_loaded[p], 16)

        @block.scalar
        def _(act):
            with act.Fori(0, B // 2) as j:
                for p in range(2):
                    act.wait_ge(xg_done, j * 2 + (p + 1))
                    nc.scalar.activation(us[:, p, :, :], cols(uT, (j * 2 + p) * S, S), ACT.Copy).then_inc(us_ready, 1)

        @block.gpsimd
        def _(pool):
            pool.wait_ge(consts, 32)
            nc.gpsimd.tensor_tensor(v3(dI[:, :]), mid(ident[0:S, 0:S], HM), last(dd[:, :], S), ALU.mult).then_inc(d_ready, 1)

            def inject(i, p):
                pool.wait_ge(rows_loaded[p], (i - p) * 8 + 16)
                pool.wait_ge(scanned, i + 1)
                nc.gpsimd.tensor_tensor(v3(inj[:, p, :]), mid(ident[0:S, 0:S], HM), v3(rows[0:S, p, 1, :]), ALU.mult).then_inc(inj_ready, 1)

            def skip(i, p):
                pool.wait_ge(mult, i + 3)
                nc.gpsimd.tensor_tensor(sc[:, p, :], sc[:, p, :], dI[:, :], ALU.add).then_inc(m_ready, 1)

            inject(0, 0)
            pool.wait_ge(d_ready, 1)
            with pool.Fori(0, B // 2 - 1) as j:
                for p in range(2):
                    inject(j * 2 + (p + 1), 1 - p)
                    skip(j * 2 + p, p)
            inject(B - 1, 1)
            skip(B - 2, 0)
            skip(B - 1, 1)

        @block.tensor
        def _(pe):
            pe.sem_inc(xg_done, 2)

            def front(i, p):
                pe.wait_ge(us_ready, i + 1)
                pe.wait_ge(x_ready, i + 1)
                for c in range(DC):
                    nc.tensor.matmul(x_ps[p][0:S, 0:INNER], us[:, p, c, :], win[:, c, INNER:2 * INNER], start=(c == 0), stop=(c == DC - 1))
                pe.wait_ge(mult, i + 1)
                nc.tensor.matmul(g_ps[p][0:S, 0:S], us[0:NST, p, DC, :], cT[:, bass.ds(i * S, S)], start=True, stop=True).then_inc(xg_done, 1)

            def back(i, p):
                pe.wait_ge(m_ready, i + 1)
                pe.wait_ge(y_out, i + 1)
                for h in range(HM):
                    o = (h % 2) * HD
                    mm = nc.tensor.matmul(y_ps[p][o:o + HD, h // 2, 0:S], xs[:, p, h * HD:(h + 1) * HD], sc[:, p, h * S:(h + 1) * S], start=True, stop=True)
                mm.then_inc(y_done, 1)

            front(0, 0)
            front(1, 1)
            with pe.Fori(0, B // 2 - 1) as j:
                for p in range(2):
                    back(j * 2 + p, p)
                    front(j * 2 + (p + 2), p)
            back(B - 2, 0)
            back(B - 1, 1)

        @block.vector
        def _(v):
            v.sem_inc(x_ready, 2)
            v.sem_inc(scanned, 2)
            v.sem_inc(mult, 2)
            v.sem_inc(y_done, 2)
            v.sem_inc(y_out, 2)
            v.wait_ge(consts, 32)

            def front(i, p):
                v.wait_ge(xg_done, i + 3)
                v.wait_ge(y_done, i + 1)
                nc.vector.tensor_tensor(xs[:, p, :], x_ps[p][0:S, 0:INNER], bx[:, :], ALU.add).then_inc(x_ready, 1)
                v.wait_ge(inj_ready, i + 1)
                nc.vector.tensor_tensor_scan(sc[:, p, :], rows[0:S, p, 0, :], inj[:, p, :], 0.0, ALU.mult, ALU.add).then_inc(scanned, 1)
                v.wait_ge(scanned, i + 3)
                nc.vector.tensor_tensor(v3(sc[:, p, :]), v3(sc[:, p, :]), mid(g_ps[p][0:S, 0:S], HM), ALU.mult).then_inc(mult, 1)

            def back(i, p):
                v.wait_ge(y_done, i + 3)
                g = cols(gate, i * S, S)
                nc.vector.tensor_tensor(g, y_ps[p][:, :, 0:S], g, ALU.mult).then_inc(y_out, 1)

            front(0, 0)
            with v.Fori(0, B // 2 - 1) as j:
                for p in range(2):
                    front(j * 2 + (p + 1), 1 - p)
                    back(j * 2 + p, p)
            front(B - 1, 1)
            back(B - 2, 0)
            back(B - 1, 1)


def mamba_out(nc, a, out, m, ctx):
    out_project(nc, m, ctx, m["gate"], IC, a["m_wout"])


def out_project(nc, m, ctx, src, chunks, w_dram):
    H = m["H"]
    w = m["sb"]("w_out", [P, chunks, D], F32, ctx)
    lhs = m["sb"]("lhs", [P, 2, chunks, P], F32, ctx)
    ps = [m["ps"](f"o_ps{i}", [P, 512], ctx) for i in range(2)]
    loaded, lhs_ready, done, added = (m["sem"](n, ctx) for n in ("wo_loaded", "lhs_ready", "o_done", "added"))
    with nc.Block() as block:
        @block.sync
        def _(sp):
            sp.dma_start(w[:, :, :], w_dram).then_inc(loaded, 16)

        @block.scalar
        def _(act):
            with act.Fori(0, T // 2) as j:
                for p in range(2):
                    act.wait_ge(done, j * 2 + (p + 1))
                    nc.scalar.activation(lhs[:, p, :, :], cols(src, (j * 2 + p) * P, P), ACT.Copy).then_inc(lhs_ready, 1)

        @block.tensor
        def _(pe):
            pe.sem_inc(done, 2)
            pe.wait_ge(loaded, 16)
            with pe.Fori(0, T // 2) as j:
                for p in range(2):
                    pe.wait_ge(lhs_ready, j * 2 + (p + 1))
                    pe.wait_ge(added, j * 2 + (p + 1))
                    for c in range(chunks):
                        mm = nc.tensor.matmul(ps[p][:, 0:D], lhs[:, p, c, :], w[:, c, :], start=(c == 0), stop=(c == chunks - 1))
                    mm.then_inc(done, 1)

        @block.vector
        def _(v):
            v.sem_inc(added, 2)
            with v.Fori(0, T // 2) as j:
                for p in range(2):
                    v.wait_ge(done, j * 2 + (p + 3))
                    h = tile_of(H, j * 2 + p)
                    nc.vector.tensor_tensor(h, ps[p][:, 0:D], h, ALU.add).then_inc(added, 1)


def route_front(nc, a, m, ctx, rms, norm, gw_dram, gb_dram):
    sb = lambda name, shape, dt=F32: m["sb"](name, shape, dt, ctx)
    sem = lambda name: m["sem"](name, ctx)
    H, A, ident, lg = m["H"], m["A"], m["ident"], m["lg"]
    R = m["R"]
    gw, gb, nw = sb("gw", [P, DC, E8]), sb("gb", [P, E8]), sb("nw", [P, DC])
    x = sb("rx", [P, 2, D])
    xT = sb("rxT", [P, 2, DC, P])
    t_ps = [m["ps"](f"rt_ps{i}", [P, DC, P], ctx) for i in range(2)]
    l_ps = [m["ps"](f"rl_ps{i}", [P, 512], ctx) for i in range(2)]
    loaded, stats1, stats2, dve, var_ready, std_ready, norm_ready, r_ready, x_ready, t_done, t_out, l_done, l_out, summed = map(
        sem, ("rf_loaded", "rstats1", "rstats2", "rdve", "rvar", "rstd_", "rnorm", "r_ready", "rx_ready", "rt_done", "rt_out", "rl_done", "rl_out", "rsum"))
    with nc.Block() as block:
        @block.sync
        def _(sp):
            sp.dma_start(gw[:, :, :], gw_dram).then_inc(loaded, 16)
            sp.dma_start(gb[:, :], gb_dram.partition_broadcast(P)).then_inc(loaded, 16)
            if norm is not None:
                sp.dma_start(nw[:, :], norm).then_inc(loaded, 16)
            sp.wait_ge(loaded, 48 if rms else 32)

        @block.vector
        def _(v):
            steps = Steps(v, dve)
            v.sem_inc(l_out, 2)
            layer_stats(nc, v, steps, m, H, stats1)
            v.sem_inc(var_ready, 1)
            v.wait_ge(std_ready, 1)
            steps.after(nc.vector.reciprocal(m["rstd"][:, :], m["std"][:, :]))
            first = norm_ready if rms else r_ready
            with v.Fori(0, T // 2) as j:
                for p in range(2):
                    normalise(nc, tile_of(A, j * 2 + p), tile_of(H, j * 2 + p), m, j * 2 + p).then_inc(first, 1)
            if rms:
                v.wait_ge(norm_ready, T)
                layer_stats(nc, v, steps, m, A, stats2)
                steps.after(nc.vector.tensor_tensor(m["tmp"][:, :], m["mean"][:, :], m["mean"][:, :], ALU.mult))
                steps.after(nc.vector.tensor_tensor(m["var"][:, :], m["var"][:, :], m["tmp"][:, :], ALU.add))
                v.sem_inc(var_ready, 1)
                v.wait_ge(std_ready, 2)
                steps.after(nc.vector.reciprocal(m["rstd"][:, :], m["std"][:, :]))
                with v.Fori(0, T // 2) as j:
                    for p in range(2):
                        i = j * 2 + p
                        nc.vector.tensor_scalar(tile_of(R, i), tile_of(A, i), m["rstd"][:, bass.ds(i, 1)], None, ALU.mult).then_inc(r_ready, 1)
            v.wait_ge(loaded, 48 if rms else 32)
            with v.Fori(0, T // 2) as j:
                for p in range(2):
                    v.wait_ge(l_done, j * 2 + (p + 3))
                    nc.vector.tensor_tensor(tile_of(lg, j * 2 + p), l_ps[p][:, 0:E8], gb[:, :], ALU.add).then_inc(l_out, 1)

        @block.gpsimd
        def _(pool):
            if rms:
                pool.wait_ge(norm_ready, T)
                nc.gpsimd.tensor_tensor(H[:, :, :], H[:, :, :], A[:, :, :], ALU.add).then_inc(summed, 1)

        @block.scalar
        def _(act):
            for n in range(2 if rms else 1):
                act.wait_ge(var_ready, n + 1)
                nc.scalar.activation(m["std"][:, :], m["var"][:, :], ACT.Sqrt, bias=m["eps"][:, n:n + 1]).then_inc(std_ready, 1)
            act.wait_ge(loaded, 48 if rms else 32)

            def fetch(i, p):
                act.wait_ge(r_ready, i + 1)
                act.wait_ge(t_done, i + 1)
                nc.scalar.activation(x[:, p, :], tile_of(R, i), ACT.Copy).then_inc(x_ready, 1)

            def turned(i, p):
                act.wait_ge(t_done, i + 3)
                act.wait_ge(l_done, i + 1)
                for c in range(DC):
                    if norm is not None:
                        ins = nc.scalar.activation(xT[:, p, c, :], t_ps[p][:, c, :], ACT.Copy, scale=nw[:, c:c + 1])
                    else:
                        ins = nc.scalar.activation(xT[:, p, c, :], t_ps[p][:, c, :], ACT.Copy)
                ins.then_inc(t_out, 1)

            fetch(0, 0)
            with act.Fori(0, T // 2 - 1) as j:
                for p in range(2):
                    fetch(j * 2 + (p + 1), 1 - p)
                    turned(j * 2 + p, p)
            fetch(T - 1, 1)
            turned(T - 2, 0)
            turned(T - 1, 1)

        @block.tensor
        def _(pe):
            pe.sem_inc(t_done, 2)
            pe.sem_inc(l_done, 2)
            pe.sem_inc(t_out, 2)
            pe.wait_ge(loaded, 48 if rms else 32)

            def turn(i, p):
                pe.wait_ge(x_ready, i + 1)
                pe.wait_ge(t_out, i + 1)
                for c in range(DC):
                    ins = nc.tensor.transpose(t_ps[p][:, c, :], x[:, p, c * P:(c + 1) * P], ident[:, :])
                ins.then_inc(t_done, 1)

            def logits(i, p):
                pe.wait_ge(t_out, i + 3)
                pe.wait_ge(l_out, i + 1)
                for c in range(DC):
                    ins = nc.tensor.matmul(l_ps[p][:, 0:E8], xT[:, p, c, :], gw[:, c, :], start=(c == 0), stop=(c == DC - 1))
                ins.then_inc(l_done, 1)

            turn(0, 0)
            with pe.Fori(0, T // 2 - 1) as j:
                for p in range(2):
                    turn(j * 2 + (p + 1), 1 - p)
                    logits(j * 2 + p, p)
            turn(T - 1, 1)
            logits(T - 2, 0)
            logits(T - 1, 1)


def by_tile(x):
    return x.rearrange("p (e t) -> p e t", t=T)


def top2(nc, v, steps, m, t):
    lg, m8, ix8, ixf, oh, w = m["lg"], t["m8"], t["ix8"], t["ixf"], t["oh"], m["w"]
    for i in range(T):
        ins = nc.vector.max(m8[:, i, :], lg[:, i, :])
    steps.after(ins)
    for i in range(T):
        ins = nc.vector.max_index(ix8[:, i, :], m8[:, i, :], lg[:, i, :])
    steps.after(ins)
    steps.after(nc.vector.tensor_tensor(w[:, 1, :], m8[:, :, 1], m8[:, :, 0], ALU.subtract))
    v.sem_inc(t["gap_ready"], 1)
    for k in range(2):
        ins = nc.vector.tensor_copy(ixf[:, k, :], ix8[:, :, k])
    steps.after(ins)
    for k in range(2):
        ins = nc.vector.tensor_tensor(by_tile(oh[:, k, :]), mid(ixf[:, k, :], E8), last(m["iota8"][:, :], T), ALU.is_equal)
    steps.after(ins)
    for k in range(2):
        ins = nc.vector.tensor_tensor(by_tile(oh[:, k, :]), by_tile(oh[:, k, :]), mid(m["valid"][:, :], E8), ALU.mult)
    steps.after(ins)
    v.wait_ge(t["exp_ready"], 1)
    steps.after(nc.vector.tensor_scalar(w[:, 0, :], w[:, 1, :], 1.0, None, ALU.add))
    steps.after(nc.vector.reciprocal(w[:, 0, :], w[:, 0, :]))
    steps.after(nc.vector.tensor_tensor(w[:, 1, :], w[:, 1, :], w[:, 0, :], ALU.mult))


def positions(nc, v, steps, m, t, chosen, ps_before, ps_total, asked, counted, n):
    steps.after(nc.vector.tensor_copy(t["chosen_bf"][:, :], chosen))
    v.sem_inc(asked, 1)
    v.wait_ge(counted, n)
    steps.after(nc.vector.tensor_tensor_scan(t["incl"][:, :], m["keep"][:, :], ps_total[:, 0:ET], 0.0, ALU.mult, ALU.add))
    steps.after(nc.vector.tensor_tensor(t["pos"][:, :], t["incl"][:, :], ps_total[:, 0:ET], ALU.subtract))
    steps.after(nc.vector.tensor_tensor(t["pos"][:, :], ps_before[:, 0:ET], t["pos"][:, :], ALU.add))


def count_matmuls(nc, pe, m, t, ps_before, ps_total, asked, counted, n):
    pe.wait_ge(asked, n)
    nc.tensor.matmul(ps_before[:, 0:ET], m["before"][:, :], t["chosen_bf"][:, :], start=True, stop=True)
    nc.tensor.matmul(ps_total[:, 0:ET], m["ones_bf"][:, :], t["chosen_bf"][:, :], start=True, stop=True).then_inc(counted, 1)


def row_indices(nc, steps, m, t, taken):
    for k in range(2):
        steps.after(nc.vector.tensor_tensor(t["incl"][:, :], t["oh"][:, k, :], t["pos"][:, :], ALU.mult))
        steps.after(nc.vector.tensor_reduce(t["row"][:, k, :], t["incl"][:, :].rearrange("p (e t) -> p t e", t=T), AX.X, ALU.add))
        steps.after(nc.vector.tensor_copy(m["gidx"][:, k, :], t["row"][:, k, :]))
        steps.after(nc.vector.tensor_scalar(t["ixf"][:, k, :], taken[k], -FAR, FAR, ALU.mult, ALU.add))
        steps.after(nc.vector.tensor_tensor(m["sidx"][:, k, :], t["row"][:, k, :], t["ixf"][:, k, :], ALU.add))


def routing_tensors(m, ctx):
    sb = lambda name, shape, dt=F32: m["sb"](name, shape, dt, ctx)
    t = {"m8": sb("m8", [P, T, 8]), "ix8": sb("ix8", [P, T, 8], U32), "ixf": sb("ixf", [P, 2, T]),
         "oh": sb("oh", [P, 2, ET]), "chosen": sb("chosen", [P, ET]), "chosen_bf": sb("chosen_bf", [P, ET], BF16),
         "incl": sb("incl", [P, ET]), "pos": sb("pos_e", [P, ET]), "row": sb("row", [P, 2, T])}
    for n in ("gap_ready", "exp_ready"):
        t[n] = m["sem"](n, ctx)
    return t


def scatter_rows(nc, pool, m, rows, nrows, sem):
    for k in range(2):
        for i in range(T):
            nc.gpsimd.indirect_dma_start(
                out=rows[:, :], out_offset=bass.IndirectOffsetOnAxis(ap=m["sidx"][:, k, i:i + 1], axis=0),
                in_=m["R"][:, i, :], in_offset=None, bounds_check=nrows - 1, oob_is_err=False).then_inc(sem, 16)
    pool.wait_ge(sem, 16 * 2 * T)


def moe1(nc, a, out, m, ctx):
    sb = lambda name, shape, dt=F32: m["sb"](name, shape, dt, ctx)
    sem = lambda name: m["sem"](name, ctx)
    m["R"] = sb("R", [P, T, D])
    m["nw1"] = sb("nw1", [P, DC])
    b1, b2 = sb("b1", [P, E8, F1]), sb("b2", [P, E8, D])
    table = sb("table", [1, NBLK], I32)
    nw_loaded = sem("nw_loaded")
    with ExitStack() as c:
        route_front(nc, a, m, c, True, a["f_norm"], a["f_gw"], a["f_gb"])
    with ExitStack() as c:
        t = routing_tensors(m, c)
        csb = lambda name, shape, dt=F32: m["sb"](name, shape, dt, c)
        iota_blk, full, nb, nbi = csb("iota_blk", [1, NBLK * E8]), csb("full", [1, NBLK * E8]), csb("nb", [P, E8]), csb("nbi", [P, E8], I32)
        ends, ones8, cntf = csb("ends", [P, E8]), csb("ones8", [P, E8]), csb("cntf", [1, NBLK])
        pb, pt = (m["ps"](n, [P, 512], c) for n in ("ps_before", "ps_total"))
        dve, asked, counted, idx_ready, scattered, iota_loaded = (m["sem"](n, c) for n in (
            "rt_dve", "asked", "counted", "idx_ready", "scattered", "iota_loaded"))
        with nc.Block() as block:
            @block.sync
            def _(sp):
                sp.dma_start(iota_blk[:, :], a["iota_blk"]).then_inc(iota_loaded, 16)
                sp.dma_start(b1[:, :, :], a["moe1_b1"].rearrange("(e f) -> e f", e=E8).partition_broadcast(P)).then_inc(nw_loaded, 16)
                sp.dma_start(b2[:, :, :], a["moe1_b2"].rearrange("(e f) -> e f", e=E8).partition_broadcast(P)).then_inc(nw_loaded, 16)
                sp.dma_start(m["nw1"][:, :], a["f_norm"]).then_inc(nw_loaded, 16)
                sp.wait_ge(nw_loaded, 48)

            @block.scalar
            def _(act):
                act.wait_ge(t["gap_ready"], 1)
                nc.scalar.activation(m["w"][:, 1, :], m["w"][:, 1, :], ACT.Exp).then_inc(t["exp_ready"], 1)

            @block.vector
            def _(v):
                steps = Steps(v, dve)
                top2(nc, v, steps, m, t)
                steps.after(nc.vector.tensor_tensor(t["chosen"][:, :], t["oh"][:, 0, :], t["oh"][:, 1, :], ALU.add))
                positions(nc, v, steps, m, t, t["chosen"][:, :], pb, pt, asked, counted, 1)
                steps.after(nc.vector.tensor_scalar(nbi[:, :], by_tile(t["incl"][:, :])[:, :, T - 1], float(P - 1), None, ALU.add))
                steps.after(nc.vector.tensor_scalar(nbi[:, :], nbi[:, :], 7, None, ALU.logical_shift_right))
                steps.after(nc.vector.tensor_copy(nb[:, :], nbi[:, :]))
                steps.after(nc.vector.memset(ones8[:, :], 1.0))
                steps.after(nc.vector.tensor_tensor_scan(ends[:, :], ones8[:, :], nb[:, :], 0.0, ALU.mult, ALU.add))
                steps.after(nc.vector.tensor_tensor(nb[:, :], ends[:, :], nb[:, :], ALU.subtract))
                steps.after(nc.vector.scalar_tensor_tensor(out=by_tile(t["pos"][:, :]), in0=last(nb[:, :], T), scalar=float(P),
                                                           in1=by_tile(t["pos"][:, :]), op0=ALU.mult, op1=ALU.add))
                row_indices(nc, steps, m, t, [m["valid"][:, :], m["valid"][:, :]])
                v.sem_inc(idx_ready, 1)
                v.wait_ge(iota_loaded, 16)
                steps.after(nc.vector.tensor_tensor(full[:, :].rearrange("p (n e) -> p n e", e=E8), iota_blk[:, :].rearrange("p (n e) -> p n e", e=E8),
                                                    mid(ends[0:1, :], NBLK), ALU.is_ge))
                steps.after(nc.vector.tensor_reduce(cntf[:, :], full[:, :].rearrange("p (n e) -> p n e", e=E8), AX.X, ALU.add))
                steps.after(nc.vector.tensor_scalar(table[:, :], cntf[:, :], float(E8 - 1), None, ALU.min))

            @block.tensor
            def _(pe):
                count_matmuls(nc, pe, m, t, pb, pt, asked, counted, 1)

            @block.gpsimd
            def _(pool):
                pool.wait_ge(idx_ready, 1)
                scatter_rows(nc, pool, m, m["rows1"], NBLK * P, scattered)

    with ExitStack() as c:
        moe1_experts(nc, a, m, c, b1, b2, table)
    with ExitStack() as c:
        combine1(nc, m, c)


def moe1_experts(nc, a, m, ctx, b1, b2, table):
    sb = lambda name, shape, dt=F32: m["sb"](name, shape, dt, ctx)
    sem = lambda name: m["sem"](name, ctx)
    ident, w1, w2 = m["ident"], m["w1"], m["w2"]
    x = sb("ex", [P, 2, D])
    xT = sb("exT", [P, 2, DC, P])
    h = sb("eh", [P, 2, F1])
    sg = sb("esg", [P, 2, D])
    act_b = sb("eact", [P, 2, D])
    actT = sb("eactT", [P, 2, DC, P])
    o = sb("eo", [P, 2, D])
    psum = lambda name: [m["ps"](f"{name}{i}", [P, 512], ctx) for i in range(2)]
    x_ps, h_ps, t_ps, o_ps = psum("ex_ps"), psum("eh_ps"), psum("et_ps"), psum("eo_ps")
    x_used, xT_ready, h_done, h_out, glu_ready, sig_ready, act_ready, t_done, actT_ready, o_done, o_ready, dve = map(
        sem, ("x_used", "xT_ready", "h_done", "h_out", "glu_ready", "sig_ready", "act_ready", "et_done", "actT_ready", "eo_done", "o_ready", "e_dve"))
    x_loaded = [sem(f"x_loaded{p}") for p in range(2)]
    o_stored = [sem(f"o_stored{p}") for p in range(2)]
    LO, HI = 2, NBLK - 2

    with nc.Block() as block:
        @block.sync
        def _(sp):
            for p in range(2):
                sp.sem_inc(o_stored[p], 16)

            def load(i, p):
                sp.wait_ge(x_used, i + 1)
                sp.dma_start(x[:, p, :], m["rows1"][bass.ds(i * P, P), :]).then_inc(x_loaded[p], 16)

            def store(i, p):
                sp.wait_ge(o_ready, i + 3)
                sp.dma_start(m["outs1"][bass.ds(i * P, P), :], o[:, p, :]).then_inc(o_stored[p], 16)

            AHEAD = 4
            for i in range(AHEAD):
                load(i, i % 2)
            with sp.Fori(AHEAD // 2, NBLK // 2) as j:
                for p in range(2):
                    load(j * 2 + p, p)
                    store(j * 2 + (p - AHEAD), p)
            for i in range(NBLK - AHEAD, NBLK):
                store(i, i % 2)
            for p in range(2):
                sp.wait_ge(o_stored[p], 16 * (NBLK // 2 + 1))

        @block.tensor
        def _(pe):
            pe.sem_inc(x_used, 2)
            pe.sem_inc(t_done, 2)
            pe.wait_ge(m["moe1_loaded"], 32)

            def turn_x(i, p):
                pe.wait_ge(x_loaded[p], (i - p) * 8 + 16)
                pe.wait_ge(xT_ready, i + 1)
                for c in range(DC):
                    mm = nc.tensor.transpose(x_ps[p][:, c * P:(c + 1) * P], x[:, p, c * P:(c + 1) * P], ident[:, :])
                mm.then_inc(x_used, 1)

            def hidden(i, p):
                e = nc.tensor.value_load(table[0:1, bass.ds(i, 1)], min_val=0, max_val=E8 - 1)
                pe.wait_ge(xT_ready, i + 3)
                pe.wait_ge(h_out, i + 1)
                for c in range(DC):
                    mm = nc.tensor.matmul(h_ps[p][:, :], xT[:, p, c, :], w1[:, bass.ds(e, 1), c, :].rearrange("p a f -> p (a f)"),
                                          start=(c == 0), stop=(c == DC - 1))
                mm.then_inc(h_done, 1)

            def turn_act(i, p):
                pe.wait_ge(act_ready, i + 1)
                pe.wait_ge(actT_ready, i + 1)
                for c in range(DC):
                    mm = nc.tensor.transpose(t_ps[p][:, c * P:(c + 1) * P], act_b[:, p, c * P:(c + 1) * P], ident[:, :])
                mm.then_inc(t_done, 1)

            def output(i, p):
                e = nc.tensor.value_load(table[0:1, bass.ds(i, 1)], min_val=0, max_val=E8 - 1)
                pe.wait_ge(actT_ready, i + 3)
                pe.wait_ge(o_ready, i + 1)
                for c in range(DC):
                    mm = nc.tensor.matmul(o_ps[p][:, 0:D], actT[:, p, c, :], w2[:, bass.ds(e, 1), c, :].rearrange("p a f -> p (a f)"),
                                          start=(c == 0), stop=(c == DC - 1))
                mm.then_inc(o_done, 1)

            turn_x(0, 0)
            turn_x(1, 1)
            hidden(0, 0)
            turn_x(2, 0)
            hidden(1, 1)
            with pe.Fori(LO // 2, HI // 2) as j:
                for p in range(2):
                    i = j * 2 + p
                    turn_act(j * 2 + (p - 2), p)
                    turn_x(j * 2 + (p + 1), 1 - p)
                    hidden(i, p)
                    output(j * 2 + (p - 2), p)
            for i in (NBLK - 2, NBLK - 1):
                turn_act(i - 2, i % 2)
                if i + 1 < NBLK:
                    turn_x(i + 1, (i + 1) % 2)
                hidden(i, i % 2)
                output(i - 2, i % 2)
            for i in (NBLK - 2, NBLK - 1):
                turn_act(i, i % 2)
                output(i, i % 2)

        @block.scalar
        def _(act):
            act.sem_inc(xT_ready, 2)
            act.sem_inc(actT_ready, 2)

            def turned_x(i, p):
                act.wait_ge(x_used, i + 3)
                act.wait_ge(h_done, i + 1)
                for c in range(DC):
                    ins = nc.scalar.activation(xT[:, p, c, :], x_ps[p][:, c * P:(c + 1) * P], ACT.Copy, scale=m["nw1"][:, c:c + 1])
                ins.then_inc(xT_ready, 1)

            def sigmoid(i, p):
                act.wait_ge(glu_ready, i + 1)
                nc.scalar.activation(sg[:, p, :], h[:, p, 0:D], ACT.Sigmoid, scale=1.702).then_inc(sig_ready, 1)

            def turned_act(i, p):
                act.wait_ge(t_done, i + 3)
                act.wait_ge(o_done, i + 1)
                nc.scalar.activation(actT[:, p, :, :], t_ps[p][:, 0:D], ACT.Copy).then_inc(actT_ready, 1)

            turned_x(0, 0)
            turned_x(1, 1)
            sigmoid(0, 0)
            turned_x(2, 0)
            sigmoid(1, 1)
            with act.Fori(LO // 2, HI // 2) as j:
                for p in range(2):
                    turned_act(j * 2 + (p - 2), p)
                    turned_x(j * 2 + (p + 1), 1 - p)
                    sigmoid(j * 2 + p, p)
            for i in (NBLK - 2, NBLK - 1):
                turned_act(i - 2, i % 2)
                if i + 1 < NBLK:
                    turned_x(i + 1, (i + 1) % 2)
                sigmoid(i, i % 2)
            for i in (NBLK - 2, NBLK - 1):
                turned_act(i, i % 2)

        @block.vector
        def _(v):
            v.sem_inc(h_out, 2)
            v.sem_inc(h_done, 2)
            v.sem_inc(o_done, 2)
            v.sem_inc(o_ready, 2)

            def swiglu(i, p):
                e = nc.vector.value_load(table[0:1, bass.ds(i, 1)], min_val=0, max_val=E8 - 1)
                v.wait_ge(h_done, i + 3)
                nc.vector.tensor_tensor(h[:, p, :], h_ps[p][:, :], b1[:, bass.ds(e, 1), :].rearrange("p a f -> p (a f)"), ALU.add).then_inc(h_out, 1)
                v.wait_ge(h_out, i + 3)
                nc.vector.tensor_scalar(h[:, p, 0:D], h[:, p, 0:D], 7.0, None, ALU.min).then_inc(glu_ready, 1)
                nc.vector.tensor_scalar(h[:, p, D:F1], h[:, p, D:F1], 7.0, -7.0, ALU.min, ALU.max).then_inc(dve, 1)
                v.wait_ge(sig_ready, i + 1)
                v.wait_ge(t_done, i + 1)
                nc.vector.tensor_tensor(sg[:, p, :], sg[:, p, :], h[:, p, 0:D], ALU.mult).then_inc(dve, 1)
                v.wait_ge(dve, i * 2 + 2)
                nc.vector.scalar_tensor_tensor(out=act_b[:, p, :], in0=h[:, p, D:F1], scalar=1.0, in1=sg[:, p, :], op0=ALU.add, op1=ALU.mult).then_inc(act_ready, 1)

            def finish(i, p):
                e = nc.vector.value_load(table[0:1, bass.ds(i, 1)], min_val=0, max_val=E8 - 1)
                v.wait_ge(o_done, i + 3)
                v.wait_ge(o_stored[p], (i - p) * 8 + 16)
                nc.vector.tensor_tensor(o[:, p, :], o_ps[p][:, 0:D], b2[:, bass.ds(e, 1), :].rearrange("p a f -> p (a f)"), ALU.add).then_inc(o_ready, 1)

            swiglu(0, 0)
            swiglu(1, 1)
            with v.Fori(LO // 2, HI // 2) as j:
                for p in range(2):
                    swiglu(j * 2 + p, p)
                    finish(j * 2 + (p - 2), p)
            for i in (NBLK - 2, NBLK - 1):
                swiglu(i, i % 2)
                finish(i - 2, i % 2)
            for i in (NBLK - 2, NBLK - 1):
                finish(i, i % 2)


def gather_rows(nc, pool, m, outs, nrows, got, loaded, used, slots):
    n = 0
    for i in range(T):
        for k in range(2):
            if n >= slots:
                pool.wait_ge(used, n - slots + 1)
            nc.gpsimd.indirect_dma_start(
                out=got[:, n % slots, :], out_offset=None, in_=outs[:, :],
                in_offset=bass.IndirectOffsetOnAxis(ap=m["gidx"][:, k, i:i + 1], axis=0),
                bounds_check=nrows - 1, oob_is_err=False).then_inc(loaded[n % slots], 16)
            n += 1


def combine1(nc, m, ctx):
    SL = 6
    got = m["sb"]("got", [P, SL, D], F32, ctx)
    loaded = [m["sem"](f"g_loaded{i}", ctx) for i in range(SL)]
    used = m["sem"]("g_used", ctx)
    H, w = m["H"], m["w"]
    with nc.Block() as block:
        @block.gpsimd
        def _(pool):
            gather_rows(nc, pool, m, m["outs1"], NBLK * P, got, loaded, used, SL)

        @block.vector
        def _(v):
            n = 0
            for i in range(T):
                for k in range(2):
                    v.wait_ge(loaded[n % SL], 16 * (n // SL + 1))
                    if k:
                        v.wait_ge(used, n)
                    nc.vector.scalar_tensor_tensor(out=H[:, i, :], in0=got[:, n % SL, :], scalar=w[:, k, i:i + 1], in1=H[:, i, :],
                                                   op0=ALU.mult, op1=ALU.add).then_inc(used, 1)
                    n += 1


def attention(nc, a, out, m, ctx):
    sb = lambda name, shape: m["sb"](name, shape, F32, ctx)
    m["uT"] = sb("auT", [P, DC, NPAD])
    m["qT"], m["kT"] = sb("qT", [P, DC, NPAD]), sb("kT", [P, DC, NPAD])
    m["aw"] = sb("aw", [48, NPAD])
    m["ctxT"] = sb("ctxT", [P, DC, NPAD])
    for part in (features, qk_project, windows, attention_core):
        with ExitStack() as c:
            part(nc, a, m, c)
    with ExitStack() as c:
        out_project(nc, m, c, m["ctxT"], DC, a["a_wo"])


def features(nc, a, m, ctx):
    sem = lambda name: m["sem"](name, ctx)
    H, uT, ident = m["H"], m["uT"], m["ident"]
    u = m["sb"]("fu", [P, 2, D], F32, ctx)
    bo = m["sb"]("bo", [P, D], F32, ctx)
    ut = [m["ps"](f"fut{i}", [P, 512], ctx) for i in range(2)]
    stats, dve, var_ready, std_ready, u_ready, ut_ready, ut_free, loaded, padded, added = map(
        sem, ("fstats", "fdve", "fvar", "fstd", "fu_ready", "fut_ready", "fut_free", "bo_loaded", "ct_padded", "bo_added"))
    with nc.Block() as block:
        @block.sync
        def _(sp):
            sp.dma_start(bo[:, :], a["a_bo_row"].partition_broadcast(P)).then_inc(loaded, 16)

        @block.vector
        def _(v):
            steps = Steps(v, dve)
            layer_stats(nc, v, steps, m, H, stats)
            v.sem_inc(var_ready, 1)
            v.wait_ge(std_ready, 1)
            steps.after(nc.vector.reciprocal(m["rstd"][:, :], m["std"][:, :]))
            with v.Fori(0, T // 2) as j:
                for p in range(2):
                    v.wait_ge(ut_ready, j * 2 + (p + 1))
                    normalise(nc, u[:, p, :], tile_of(H, j * 2 + p), m, j * 2 + p).then_inc(u_ready, 1)

        @block.gpsimd
        def _(pool):
            nc.gpsimd.memset(m["ctxT"][:, :, N:NPAD], 0.0).then_inc(padded, 1)
            pool.wait_ge(padded, 1)
            nc.gpsimd.memset(m["aw"][:, :], 0.0).then_inc(padded, 1)
            pool.wait_ge(loaded, 16)
            pool.wait_ge(u_ready, T)
            pool.wait_ge(padded, 2)
            nc.gpsimd.tensor_tensor(H[:, :, :], H[:, :, :], mid(bo[:, :], T), ALU.add).then_inc(added, 1)

        @block.scalar
        def _(act):
            act.wait_ge(var_ready, 1)
            nc.scalar.activation(m["std"][:, :], m["var"][:, :], ACT.Sqrt, bias=m["eps"][:, 0:1]).then_inc(std_ready, 1)
            act.sem_inc(ut_free, 2)
            with act.Fori(0, T // 2) as j:
                for p in range(2):
                    act.wait_ge(ut_ready, j * 2 + (p + 3))
                    nc.scalar.activation(cols(uT, (j * 2 + p) * P, P), ut[p][:, 0:D].rearrange("p (c q) -> p c q", q=P), ACT.Copy).then_inc(ut_free, 1)

        @block.tensor
        def _(pe):
            pe.sem_inc(ut_ready, 2)
            with pe.Fori(0, T // 2) as j:
                for p in range(2):
                    pe.wait_ge(u_ready, j * 2 + (p + 1))
                    pe.wait_ge(ut_free, j * 2 + (p + 1))
                    for c in range(DC):
                        ins = nc.tensor.transpose(ut[p][:, c * P:(c + 1) * P], u[:, p, c * P:(c + 1) * P], ident[:, :])
                    ins.then_inc(ut_ready, 1)


def qk_project(nc, a, m, ctx):
    sb = lambda name, shape: m["sb"](name, shape, F32, ctx)
    sem = lambda name: m["sem"](name, ctx)
    uT, qT, kT = m["uT"], m["qT"], m["kT"]
    wq, wk, bq, bk = sb("wq", [P, DC, D]), sb("wk", [P, DC, D]), sb("bq", [P, DC]), sb("bk", [P, DC])
    ps = [[m["ps"](f"qk_ps{i}{k}", [P, 512], ctx) for k in range(4)] for i in range(2)]
    loaded, done, q_out, k_out = map(sem, ("qk_loaded", "qk_done", "q_out", "k_out"))
    with nc.Block() as block:
        @block.sync
        def _(sp):
            for t, k in ((wq, "a_wq"), (wk, "a_wk")):
                sp.dma_start(t[:, :, :], a[k]).then_inc(loaded, 16)
            for t, k in ((bq, "a_bq"), (bk, "a_bk")):
                sp.dma_start(t[:, :], a[k]).then_inc(loaded, 16)

        @block.tensor
        def _(pe):
            pe.wait_ge(loaded, 64)
            with pe.Fori(0, NG // 2) as j:
                for p in range(2):
                    pe.wait_ge(q_out, j * 2 + (p + 1))
                    pe.wait_ge(k_out, j * 2 + (p + 1))
                    for n in range(4):
                        w = (wq, wk)[n // 2]
                        for c in range(DC):
                            mm = nc.tensor.matmul(ps[p][n][:, 0:G4], w[:, c, (n % 2) * P:(n % 2 + 1) * P], uT[:, c, bass.ds((j * 2 + p) * G4, G4)],
                                                  start=(c == 0), stop=(c == DC - 1))
                    mm.then_inc(done, 1)

        @block.scalar
        def _(act):
            act.sem_inc(q_out, 2)
            act.wait_ge(loaded, 64)
            with act.Fori(0, NG // 2) as j:
                for p in range(2):
                    act.wait_ge(done, j * 2 + (p + 1))
                    for n in range(2):
                        ins = nc.scalar.activation(qT[:, n, bass.ds((j * 2 + p) * G4, G4)], ps[p][n][:, 0:G4], ACT.Identity, bias=bq[:, n:n + 1])
                    ins.then_inc(q_out, 1)

        @block.vector
        def _(v):
            v.sem_inc(k_out, 2)
            v.wait_ge(loaded, 64)
            with v.Fori(0, NG // 2) as j:
                for p in range(2):
                    v.wait_ge(done, j * 2 + (p + 1))
                    for n in range(2):
                        ins = nc.vector.tensor_scalar(kT[:, n, bass.ds((j * 2 + p) * G4, G4)], ps[p][2 + n][:, 0:G4], bk[:, n:n + 1], None, ALU.add)
                    ins.then_inc(k_out, 1)


def windows(nc, a, m, ctx):
    sb = lambda name, shape: m["sb"](name, shape, F32, ctx)
    sem = lambda name: m["sem"](name, ctx)
    qT, aw = m["qT"], m["aw"]
    wfq, wfg = sb("wfq", [P, DC, D]), sb("wfg", [P, DC, D])
    up, uz, bfq, bfg = sb("up", [P, DC, NH]), sb("uz", [P, DC, NH]), sb("bfq", [P, DC]), sb("bfg", [P, DC])
    glo, gb = sb("glo", [P, DC, B]), sb("gbias", [P, DC, B])
    cT = sb("c_T", [P, 2, DC, G4])
    ep, ez = sb("ep", [NH, 2, G4]), sb("ez", [NH, 2, G4])
    ROOT2 = 2.0 ** 0.5
    c_ps = [m["ps"](f"c_ps{i}", [P, 2, 512], ctx) for i in range(2)]
    pz_ps = [m["ps"](f"pz_ps{i}", [P, 2, 512], ctx) for i in range(2)]
    loaded, dve, glo_ready, g_done, c_done, c_in, c_ready, pz_done, e_ready, aw_ready = map(
        sem, ("w_loaded", "w_dve", "glo_ready", "g_done", "c_done", "c_in", "c_ready", "pz_done", "e_ready", "aw_ready"))
    with nc.Block() as block:
        @block.sync
        def _(sp):
            for t, k in ((wfq, "a_wfq"), (wfg, "a_wfg"), (up, "a_up"), (uz, "a_uz")):
                sp.dma_start(t[:, :, :], a[k]).then_inc(loaded, 16)
            for t, k in ((bfq, "a_bfq"), (bfg, "a_bfg")):
                sp.dma_start(t[:, :], a[k]).then_inc(loaded, 16)

        @block.tensor
        def _(pe):
            pe.wait_ge(loaded, 96)
            pe.wait_ge(glo_ready, 1)
            for n in range(DC):
                for c in range(DC):
                    mm = nc.tensor.matmul(pz_ps[0][:, n, 0:B], wfg[:, c, n * P:(n + 1) * P], glo[:, c, :], start=(c == 0), stop=(c == DC - 1))
            mm.then_inc(g_done, 1)

            def c_args(i, p):
                pe.wait_ge(c_in, i + 1)
                for n in range(DC):
                    for c in range(DC):
                        mm = nc.tensor.matmul(c_ps[p][:, n, 0:G4], wfq[:, c, n * P:(n + 1) * P], qT[:, c, bass.ds(i * G4, G4)], start=(c == 0), stop=(c == DC - 1))
                mm.then_inc(c_done, 1)

            def pz(i, p):
                pe.wait_ge(c_ready, i + 1)
                pe.wait_ge(e_ready, i + 1)
                for n, u in enumerate((up, uz)):
                    for c in range(DC):
                        mm = nc.tensor.matmul(pz_ps[p][0:NH, n, 0:G4], u[:, c, :], cT[:, p, c, :], start=(c == 0), stop=(c == DC - 1))
                mm.then_inc(pz_done, 1)

            c_args(0, 0)
            with pe.Fori(0, NG // 2 - 1) as j:
                for p in range(2):
                    c_args(j * 2 + (p + 1), 1 - p)
                    pz(j * 2 + p, p)
            c_args(NG - 1, 1)
            pz(NG - 2, 0)
            pz(NG - 1, 1)

        @block.vector
        def _(v):
            steps = Steps(v, dve)
            v.sem_inc(c_in, 2)
            v.sem_inc(pz_done, 2)
            v.sem_inc(aw_ready, 2)
            for c in range(DC):
                ins = nc.vector.tensor_reduce(glo[:, c, :], qT[:, c, 0:N].rearrange("p (b s) -> p b s", s=S), AX.X, ALU.add)
            steps.after(ins)
            steps.after(nc.vector.tensor_scalar(glo[:, :, :], glo[:, :, :], 1.0 / S, None, ALU.mult))
            v.sem_inc(glo_ready, 1)
            v.wait_ge(loaded, 96)
            steps.after(nc.vector.tensor_tensor(bfq[:, :], bfq[:, :], bfg[:, :], ALU.add))
            v.wait_ge(g_done, 1)
            steps.after(nc.vector.tensor_tensor(gb[:, :, :], pz_ps[0][:, :, 0:B], last(bfq[:, :], B), ALU.add))
            v.sem_inc(e_ready, 2)
            base = steps.n

            def add_global(i, p):
                v.wait_ge(c_done, i + 1)
                v.wait_ge(pz_done, i + 1)
                g = gb[:, :, bass.ds(i * 4, 4)]
                for n in range(DC):
                    ins = nc.vector.tensor_tensor(cT[:, p, n, :].rearrange("p (b s) -> p b s", s=S), c_ps[p][:, n, 0:G4].rearrange("p (b s) -> p b s", s=S),
                                                  g[:, n, :].unsqueeze(2).broadcast_to([P, 4, S]), ALU.add)
                ins.then_inc(c_in, 1)

            def weights(i, p):
                v.wait_ge(e_ready, i + 3)
                nc.vector.tensor_scalar(ez[:, p, :], ez[:, p, :], 1.0, None, ALU.add).then_inc(dve, 1)
                nc.vector.tensor_scalar(ep[:, p, :], ep[:, p, :], 1.0, None, ALU.add).then_inc(dve, 1)
                v.wait_ge(dve, i * 3 + (base + 2))
                nc.vector.reciprocal(ep[:, p, :], ep[:, p, :]).then_inc(dve, 1)
                here = bass.ds(i * G4, G4)
                nc.vector.tensor_scalar(aw[0:NH, here], ez[:, p, :], ROOT2 / S, None, ALU.mult)
                v.wait_ge(dve, i * 3 + (base + 3))
                nc.vector.scalar_tensor_tensor(out=aw[32:32 + NH, here], in0=ez[:, p, :], scalar=ROOT2, in1=ep[:, p, :], op0=ALU.mult, op1=ALU.mult).then_inc(aw_ready, 1)

            add_global(0, 0)
            with v.Fori(0, NG // 2 - 1) as j:
                for p in range(2):
                    add_global(j * 2 + (p + 1), 1 - p)
                    weights(j * 2 + p, p)
            add_global(NG - 1, 1)
            weights(NG - 2, 0)
            weights(NG - 1, 1)

        @block.scalar
        def _(act):
            def tanh(i, p):
                act.wait_ge(c_in, i + 3)
                nc.scalar.activation(cT[:, p, :, :], cT[:, p, :, :], ACT.Tanh).then_inc(c_ready, 1)

            def exps(i, p):
                act.wait_ge(pz_done, i + 3)
                act.wait_ge(aw_ready, i + 1)
                nc.scalar.activation(ep[:, p, :], pz_ps[p][0:NH, 0, 0:G4], ACT.Exp, scale=-1.0)
                nc.scalar.activation(ez[:, p, :], pz_ps[p][0:NH, 1, 0:G4], ACT.Exp, scale=-1.0).then_inc(e_ready, 1)

            tanh(0, 0)
            with act.Fori(0, NG // 2 - 1) as j:
                for p in range(2):
                    tanh(j * 2 + (p + 1), 1 - p)
                    exps(j * 2 + p, p)
            tanh(NG - 1, 1)
            exps(NG - 2, 0)
            exps(NG - 1, 1)


def attention_core(nc, a, m, ctx):
    sb = lambda name, shape: m["sb"](name, shape, F32, ctx)
    sem = lambda name: m["sem"](name, ctx)
    uT, qT, kT, aw, ctxT, ident = m["uT"], m["qT"], m["kT"], m["aw"], m["ctxT"], m["ident"]
    UH = 4
    UPB = NH // UH
    UC = UH * S
    VW = AD + 1
    window, eo, bv, wv = sb("window", [48, NH * S]), sb("head_of_4", [P, UH]), sb("bv", [S, D]), sb("wv", [P, DC, D])
    us, qs, ks, ws = sb("aus", [P, 2, DC, S]), sb("qs", [P, 2, DC, S]), sb("ks", [P, 2, DC, UH, S]), sb("ws", [48, 2, S])
    vs = sb("vs", [S, 2, NH * VW])
    sq, ss, mx, pts, cx, rc = sb("sq", [S, 2, UC]), sb("ss", [S, 2, UC]), sb("mx", [S, 2, UH]), sb("pts", [S, 2, UC]), sb("cx", [S, 2, D]), sb("rc", [S, NH])
    pair = lambda name: [m["ps"](f"{name}{i}", [P, 512], ctx) for i in range(2)]
    s_ps, w_ps, p_ps = pair("s_ps"), pair("w_ps"), pair("p_ps")
    v_ps, c_ps = m["ps"]("v_ps", [P, 512], ctx), m["ps"]("cx_ps", [P, 512], ctx)
    consts, ones_set, copied, k_ready, v_done, v_out, su_done, sq_ready, ss_ready, mx_ready, sh_ready, pr_ready, pt_done, pt_out, c_done, c_out, rc_ready, ct_done, ct_out = map(
        sem, ("at_consts", "ones_set", "copied", "k_ready", "v_done", "v_out", "su_done", "sq_ready", "ss_ready", "mx_ready", "sh_ready", "pr_ready",
              "pt_done", "pt_out", "cx_done", "cx_out", "rc_ready", "ct_done", "ct_out"))

    def heads(x):
        return x.rearrange("p (h s) -> p h s", s=S)

    def steps_of(body):
        def run(eng):
            with eng.Fori(0, B // 2 - 1) as j:
                for r in range(2 * UPB):
                    body(j * (2 * UPB) + r, r, j * 2 + r // UPB, False)
            for r in range(2 * UPB):
                body((B - 2) * UPB + r, r, B - 2 + r // UPB, True)
        return run

    with nc.Block() as block:
        @block.sync
        def _(sp):
            sp.dma_start(window[:, :], a["window"].rearrange("r h s -> r (h s)")).then_inc(consts, 16)
            sp.dma_start(eo[:, :], a["head_of_4"]).then_inc(consts, 16)
            sp.dma_start(bv[:, :], a["a_bv_row"].partition_broadcast(S)).then_inc(consts, 16)
            sp.dma_start(wv[:, :, :], a["a_wv"]).then_inc(consts, 16)

        @block.tensor
        def _(pe):
            pe.sem_inc(su_done, 2 * UPB)
            pe.wait_ge(consts, 64)

            def values(b, q):
                pe.wait_ge(copied, b + 1)
                pe.wait_ge(ct_out, b + 1)
                for c in range(DC):
                    mm = nc.tensor.matmul(v_ps[0:S, 0:D], us[:, q, c, :], wv[:, c, :], start=(c == 0), stop=(c == DC - 1))
                mm.then_inc(v_done, 1)

            def begin(n, u, b, q, p):
                if u == 0:
                    values(b, q)
                    pe.wait_ge(k_ready, b + 1)
                pe.wait_ge(ss_ready, n + 1)
                o, n_in = (u % 2) * UH * AD, UH * AD
                nc.tensor.matmul(s_ps[p][0:S, 0:UC], qs[o:o + n_in, q, u // 2, :],
                                 ks[o:o + n_in, q, u // 2, :, :].rearrange("p a s -> p (a s)"), start=True, stop=True)
                pe.wait_ge(sq_ready, n + 1)
                nc.tensor.matmul(w_ps[p][0:S, 0:UC], ws[:, q, :], window[:, u * UC:(u + 1) * UC], start=True, stop=True).then_inc(su_done, 1)

            def turn(n, p):
                pe.wait_ge(pr_ready, n + 1)
                pe.wait_ge(pt_out, n + 1)
                for h in range(UH):
                    mm = nc.tensor.transpose(p_ps[p][0:S, h * S:(h + 1) * S], ss[:, p, h * S:(h + 1) * S], ident[0:S, 0:S])
                mm.then_inc(pt_done, 1)

            def context(n, u, b, q, p):
                if u == 0:
                    pe.wait_ge(v_out, b + 1)
                    pe.wait_ge(c_out, b + 1)
                pe.wait_ge(pt_out, n + 3)
                for h in range(UH):
                    g = u * UH + h
                    mm = nc.tensor.matmul(c_ps[0:S, g * VW:(g + 1) * VW], pts[:, p, h * S:(h + 1) * S], vs[:, q, g * VW:(g + 1) * VW], start=True, stop=True)
                if u == UPB - 1:
                    mm.then_inc(c_done, 1)

            def turn_context(b, q, end):
                pe.wait_ge(c_out, b + 2)
                if not end:
                    pe.wait_ge(v_out, b + 2)
                pe.wait_ge(ct_out, b + 2)
                for c in range(DC):
                    mm = nc.tensor.transpose(v_ps[:, D + c * S:D + (c + 1) * S], cx[:, q, c * P:(c + 1) * P], ident[0:S, 0:S])
                mm.then_inc(ct_done, 1)

            begin(0, 0, 0, 0, 0)
            begin(1, 1, 0, 0, 1)

            def step(n, r, b, end):
                p, q, u = r % 2, r // UPB, r % UPB
                turn(n, p)
                if not (end and r + 2 >= 2 * UPB):
                    r2 = (r + 2) % (2 * UPB)
                    begin(n + 2, r2 % UPB, b if u + 2 < UPB else b + 1, r2 // UPB, p)
                context(n, u, b, q, p)
                if u == UPB - 1:
                    turn_context(b, q, end and q == 1)

            steps_of(step)(pe)

        @block.scalar
        def _(act):
            act.sem_inc(sq_ready, 2)
            act.sem_inc(ct_out, 2)

            def copies(b, q):
                act.wait_ge(su_done, b * UPB + UPB)
                here = b * S
                nc.scalar.activation(us[:, q, :, :], cols(uT, here, S), ACT.Copy)
                nc.scalar.activation(qs[:, q, :, :], cols(qT, here, S), ACT.Copy, scale=0.25)
                nc.scalar.activation(ws[:, q, :], aw[:, bass.ds(here, S)], ACT.Copy).then_inc(copied, 1)

            def square(n, p):
                act.wait_ge(su_done, n + (1 + 2 * UPB))
                act.wait_ge(ss_ready, n + 1)
                nc.scalar.activation(sq[:, p, :], w_ps[p][0:S, 0:UC], ACT.Square).then_inc(sq_ready, 1)

            def exp(n, p):
                act.wait_ge(sh_ready, n + 1)
                nc.scalar.activation(ss[:, p, :], ss[:, p, :], ACT.Exp).then_inc(pr_ready, 1)

            copies(0, 0)
            square(0, 0)
            square(1, 1)
            exp(0, 0)

            def step(n, r, b, end):
                p, q, u = r % 2, r // UPB, r % UPB
                if u == 0 and not (end and q == 1):
                    copies(b + 1, 1 - q)
                if not (end and r + 2 >= 2 * UPB):
                    square(n + 2, p)
                if not (end and r + 1 >= 2 * UPB):
                    exp(n + 1, 1 - p)
                if u == UPB - 1:
                    act.wait_ge(ct_done, b + 1)
                    nc.scalar.activation(cols(ctxT, b * S, S), v_ps[:, D:D + DC * S].rearrange("p (c s) -> p c s", s=S), ACT.Copy).then_inc(ct_out, 1)

            steps_of(step)(act)

        @block.gpsimd
        def _(pool):
            def shift(n, p):
                pool.wait_ge(mx_ready, n + 1)
                nc.gpsimd.tensor_tensor(heads(ss[:, p, :]), heads(ss[:, p, :]), last(mx[:, p, :], S), ALU.subtract).then_inc(sh_ready, 1)

            with pool.Fori(0, B * UPB // 2) as j:
                for p in range(2):
                    shift(j * 2 + p, p)

        @block.vector
        def _(v):
            v.sem_inc(ss_ready, 2)
            v.sem_inc(pt_out, 2)
            v.sem_inc(c_out, 1)
            nc.vector.memset(vs[:, :, :], 1.0).then_inc(ones_set, 1)
            v.wait_ge(ones_set, 1)
            v.wait_ge(consts, 64)

            def keys(b, q):
                v.wait_ge(su_done, b * UPB + UPB)
                for e in range(UH):
                    ins = nc.vector.tensor_scalar(ks[:, q, :, e, :], cols(kT, b * S, S), eo[:, e:e + 1], None, ALU.mult)
                ins.then_inc(k_ready, 1)

            def values(b, q):
                v.wait_ge(v_done, b + 1)
                nc.vector.tensor_tensor(vs[:, q, :].rearrange("p (h w) -> p h w", w=VW)[:, :, 0:AD], v_ps[0:S, 0:D].rearrange("p (h w) -> p h w", w=AD),
                                        bv[:, :].rearrange("p (h w) -> p h w", w=AD), ALU.add).then_inc(v_out, 1)

            def scores(n, p):
                v.wait_ge(sq_ready, n + 3)
                nc.vector.tensor_tensor(ss[:, p, :], s_ps[p][0:S, 0:UC], sq[:, p, :], ALU.subtract).then_inc(ss_ready, 1)
                v.wait_ge(ss_ready, n + 3)
                nc.vector.tensor_reduce(mx[:, p, :], heads(ss[:, p, :]), AX.X, ALU.max).then_inc(mx_ready, 1)

            def turned(n, p):
                v.wait_ge(pt_done, n + 1)
                nc.vector.tensor_copy(pts[:, p, :], p_ps[p][0:S, 0:UC]).then_inc(pt_out, 1)

            def context(b, q):
                v.wait_ge(c_done, b + 1)
                c3 = c_ps[0:S, 0:NH * VW].rearrange("p (h w) -> p h w", w=VW)
                nc.vector.reciprocal(rc[:, :], c3[:, :, AD]).then_inc(rc_ready, 1)
                v.wait_ge(rc_ready, b + 1)
                nc.vector.tensor_tensor(cx[:, q, :].rearrange("p (h w) -> p h w", w=AD), c3[:, :, 0:AD], last(rc[:, :], AD), ALU.mult).then_inc(c_out, 1)

            keys(0, 0)
            values(0, 0)
            scores(0, 0)
            scores(1, 1)

            def step(n, r, b, end):
                p, q, u = r % 2, r // UPB, r % UPB
                if u == 0 and not (end and q == 1):
                    keys(b + 1, 1 - q)
                turned(n, p)
                if not (end and r + 2 >= 2 * UPB):
                    if u + 2 == UPB:
                        values(b + 1, 1 - q)
                    scores(n + 2, p)
                if u == UPB - 1:
                    context(b, q)

            steps_of(step)(v)


def moe2(nc, a, out, m, ctx):
    sb = lambda name, shape, dt=F32: m["sb"](name, shape, dt, ctx)
    m["R"] = m["A"]
    w1, w2 = sb("x_w1", [P, 2, DC, HID]), sb("x_w2", [P, 2, MC, D])
    w_loaded = [m["sem"](f"xw_loaded{p}", ctx) for p in range(2)]
    with ExitStack() as c:
        route_front(nc, a, m, c, False, None, a["r_gw"], a["r_gb"])
    with ExitStack() as c:
        capacity_routing(nc, a, m, c, w1, w2, w_loaded)
    with ExitStack() as c:
        moe2_experts(nc, a, m, c, w1, w2, w_loaded)
    with ExitStack() as c:
        combine2(nc, a, out, m, c)


def load_expert(sp, a, w1, w2, w_loaded, e, p):
    sp.dma_start(w1[:, p, :, :], a["x_w1"][bass.ds(e, 1)].rearrange("o p c n -> (o p) c n")).then_inc(w_loaded[p], 16)
    sp.dma_start(w2[:, p, :, :], a["x_w2"][bass.ds(e, 1)].rearrange("o p c n -> (o p) c n")).then_inc(w_loaded[p], 16)


def capacity_routing(nc, a, m, ctx, w1, w2, w_loaded):
    csb = lambda name, shape, dt=F32: m["sb"](name, shape, dt, ctx)
    t = routing_tensors(m, ctx)
    wt, hit, cnt = csb("wt", [P, ET]), csb("hit", [P, ET]), csb("cnt", [P, E8], BF16)
    thr, cand, bit, ge = (csb(n, [P, E8], U32) for n in ("thr", "cand", "bit", "ge"))
    room, taken = csb("room", [P, E8]), csb("taken", [P, 2, T])
    pb, pt, pc = (m["ps"](n, [P, 512], ctx) for n in ("ps_before", "ps_total", "ps_count"))
    dve, asked, counted, idx_ready, scattered, cnt_ready, cnt_done, srch = (m["sem"](n, ctx) for n in (
        "rt_dve", "asked", "counted", "idx_ready", "scattered", "cnt_ready", "cnt_done", "search"))
    BITS = 30
    PER = 5
    with nc.Block() as block:
        @block.sync
        def _(sp):
            for e in range(2):
                load_expert(sp, a, w1, w2, w_loaded, e, e)

        @block.scalar
        def _(act):
            act.wait_ge(t["gap_ready"], 1)
            nc.scalar.activation(m["w"][:, 1, :], m["w"][:, 1, :], ACT.Exp).then_inc(t["exp_ready"], 1)

        @block.tensor
        def _(pe):
            with pe.Fori(0, BITS) as i:
                pe.wait_ge(cnt_ready, i + 1)
                nc.tensor.matmul(pc[:, 0:E8], m["ones_bf"][:, :], cnt[:, :], start=True, stop=True).then_inc(cnt_done, 1)
            for n in range(3):
                count_matmuls(nc, pe, m, t, pb, pt, asked, counted, n + 1)

        @block.vector
        def _(v):
            steps = Steps(v, dve)
            top2(nc, v, steps, m, t)
            w, oh = m["w"], t["oh"]
            steps.after(nc.vector.tensor_tensor(by_tile(wt[:, :]), by_tile(oh[:, 0, :]), mid(w[:, 0, :], E8), ALU.mult))
            steps.after(nc.vector.tensor_tensor(by_tile(hit[:, :]), by_tile(oh[:, 1, :]), mid(w[:, 1, :], E8), ALU.mult))
            steps.after(nc.vector.tensor_tensor(wt[:, :], wt[:, :], hit[:, :], ALU.add))
            steps.after(nc.vector.memset(thr[:, :].bitcast(F32), 0.0))
            steps.after(nc.vector.memset(bit[:, :].bitcast(F32), 2.0 ** -63))
            with v.Fori(0, BITS) as i:
                nc.vector.tensor_tensor(cand[:, :], thr[:, :], bit[:, :], ALU.bitwise_or).then_inc(srch, 1)
                v.wait_ge(srch, i * PER + 1)
                nc.vector.tensor_tensor(by_tile(hit[:, :]), by_tile(wt[:, :]), last(cand[:, :].bitcast(F32), T), ALU.is_ge).then_inc(srch, 1)
                nc.vector.tensor_scalar(bit[:, :], bit[:, :], 1, None, ALU.logical_shift_right)
                v.wait_ge(srch, i * PER + 2)
                with nc.allow_low_precision(reason="counts up to 18 are exact in bfloat16"):
                    nc.vector.tensor_reduce(cnt[:, :], by_tile(hit[:, :]), AX.X, ALU.add).then_inc(cnt_ready, 1)
                v.wait_ge(cnt_done, i + 1)
                nc.vector.tensor_scalar(ge[:, :], pc[:, 0:E8], float(CAP), None, ALU.is_ge).then_inc(srch, 1)
                v.wait_ge(srch, i * PER + 3)
                nc.vector.copy_predicated(thr[:, :], ge[:, :], cand[:, :]).then_inc(srch, 2)
                v.wait_ge(srch, i * PER + 5)
            limit = last(thr[:, :].bitcast(F32), T)
            steps.after(nc.vector.tensor_tensor(by_tile(t["chosen"][:, :]), by_tile(wt[:, :]), limit, ALU.is_gt))
            positions(nc, v, steps, m, t, t["chosen"][:, :], pb, pt, asked, counted, 1)
            steps.after(nc.vector.tensor_scalar(room[:, :], by_tile(t["incl"][:, :])[:, :, T - 1], -1.0, float(CAP), ALU.mult, ALU.add))
            steps.after(nc.vector.tensor_tensor(by_tile(hit[:, :]), by_tile(wt[:, :]), limit, ALU.is_equal))
            steps.after(nc.vector.scalar_tensor_tensor(out=hit[:, :], in0=wt[:, :], scalar=0.0, in1=hit[:, :], op0=ALU.is_gt, op1=ALU.mult))
            positions(nc, v, steps, m, t, hit[:, :], pb, pt, asked, counted, 2)
            steps.after(nc.vector.tensor_tensor(by_tile(t["pos"][:, :]), by_tile(t["pos"][:, :]), last(room[:, :], T), ALU.is_lt))
            steps.after(nc.vector.tensor_tensor(hit[:, :], hit[:, :], t["pos"][:, :], ALU.mult))
            steps.after(nc.vector.tensor_tensor(t["chosen"][:, :], t["chosen"][:, :], hit[:, :], ALU.add))
            positions(nc, v, steps, m, t, t["chosen"][:, :], pb, pt, asked, counted, 3)
            steps.after(nc.vector.scalar_tensor_tensor(out=by_tile(t["pos"][:, :]), in0=last(m["iota8"][:, :], T), scalar=float(ROWS),
                                                       in1=by_tile(t["pos"][:, :]), op0=ALU.mult, op1=ALU.add))
            for k in range(2):
                steps.after(nc.vector.tensor_tensor(oh[:, k, :], oh[:, k, :], t["chosen"][:, :], ALU.mult))
                steps.after(nc.vector.tensor_reduce(taken[:, k, :], oh[:, k, :].rearrange("p (e t) -> p t e", t=T), AX.X, ALU.add))
            steps.after(nc.vector.tensor_tensor(w[:, :, :], w[:, :, :], taken[:, :, :], ALU.mult))
            row_indices(nc, steps, m, t, [taken[:, 0, :], taken[:, 1, :]])
            v.sem_inc(idx_ready, 1)

        @block.gpsimd
        def _(pool):
            pool.wait_ge(idx_ready, 1)
            scatter_rows(nc, pool, m, m["rows2"], E8 * ROWS, scattered)


def moe2_experts(nc, a, m, ctx, w1, w2, w_loaded):
    sb = lambda name, shape, dt=F32: m["sb"](name, shape, dt, ctx)
    sem = lambda name: m["sem"](name, ctx)
    ident = m["ident"]
    b1, b2 = sb("x_b1", [P, E8, MC]), sb("x_b2", [P, E8, DC])
    x = sb("xx", [XQ, 2, XG, D])
    xT = sb("xxT", [P, 2, DC, ROWS])
    hT = sb("xhT", [P, MC, ROWS])
    oT = sb("xoT", [P, DC, ROWS])
    r = sb("xr", [XQ, 2, XG, D])
    pair = lambda name: [m["ps"](f"{name}{i}", [P, 512], ctx) for i in range(2)]
    x_ps, h_ps, o_ps, r_ps = pair("xx_ps"), pair("xh_ps"), pair("xo_ps"), pair("xr_ps")
    biases, x_turned, xT_out, h_done, h_out, o_done, o_out, r_done, r_out = map(
        sem, ("x_biases", "x_turned", "xT_out", "xh_done", "xh_out", "xo_done", "xo_out", "xr_done", "xr_out"))
    x_loaded = [sem(f"xx_loaded{p}") for p in range(2)]
    stored = [sem(f"xr_stored{p}") for p in range(2)]

    def rows(dram, e):
        return dram[bass.ds(e * ROWS, ROWS), :].rearrange("(g q) d -> q g d", q=XQ)

    def for_experts(eng, step):
        step(0, 0, True, False)
        with eng.Fori(0, E8 // 2 - 1) as j:
            for p in range(2):
                step(j * 2 + (p + 1), 1 - p, False, False)
        step(E8 - 1, 1, False, True)

    with nc.Block() as block:
        @block.sync
        def _(sp):
            sp.dma_start(b1[:, :, :], a["x_b1"]).then_inc(biases, 16)
            sp.dma_start(b2[:, :, :], a["x_b2"]).then_inc(biases, 16)
            for p in range(2):
                sp.sem_inc(stored[p], 16)

            def load_x(e, p):
                sp.wait_ge(x_turned, e + 1)
                sp.dma_start(x[:, p, :, :], rows(m["rows2"], e)).then_inc(x_loaded[p], 16)

            def step(e, p, first, final):
                if not final:
                    if not first:
                        sp.wait_ge(o_done, e + 1)
                        load_expert(sp, a, w1, w2, w_loaded, e + 1, 1 - p)
                    load_x(e + 1, 1 - p)
                if not first:
                    sp.wait_ge(r_out, e + 1)
                    sp.dma_start(rows(m["outs2"], e - 1), r[:, 1 - p, :, :]).then_inc(stored[1 - p], 16)

            load_x(0, 0)
            for_experts(sp, step)
            sp.wait_ge(r_out, E8 + 1)
            sp.dma_start(rows(m["outs2"], E8 - 1), r[:, 1, :, :]).then_inc(stored[1], 16)
            for p in range(2):
                sp.wait_ge(stored[p], 16 * (E8 // 2 + 1))

        @block.tensor
        def _(pe):
            pe.sem_inc(x_turned, 2)

            def turn_x(e, p):
                pe.wait_ge(x_loaded[p], (e - p) * 8 + 16)
                for c in range(DC):
                    for g in range(XG):
                        mm = nc.tensor.transpose(x_ps[c][:, g * XQ:(g + 1) * XQ], x[:, p, g, c * P:(c + 1) * P], ident[0:XQ, 0:XQ])
                mm.then_inc(x_turned, 1)

            def turn_out(e, p):
                pe.wait_ge(o_out, e + 2)
                pe.wait_ge(r_out, e + 1)
                for g in range(XG):
                    for c in range(DC):
                        o = (g % 2) * D + c * P
                        mm = nc.tensor.transpose(r_ps[g // 2][0:XQ, o:o + P], oT[:, c, g * XQ:(g + 1) * XQ], ident[:, :])
                mm.then_inc(r_done, 1)

            def step(e, p, first, final):
                pe.wait_ge(w_loaded[p], (e - p) * 16 + 32)
                pe.wait_ge(xT_out, e + 1)
                for k in range(MC):
                    pe.wait_ge(h_out, e * MC + (k + 1))
                    for c in range(DC):
                        mm = nc.tensor.matmul(h_ps[k % 2][:, 0:ROWS], w1[:, p, c, k * P:(k + 1) * P], xT[:, p, c, :], start=(c == 0), stop=(c == DC - 1))
                    mm.then_inc(h_done, 1)
                if not first:
                    turn_out(e - 1, 1 - p)
                if not final:
                    turn_x(e + 1, 1 - p)
                pe.wait_ge(o_out, e + 1)
                for o in range(DC):
                    for k in range(MC):
                        if o == 0:
                            pe.wait_ge(h_out, e * MC + (k + 3))
                        mm = nc.tensor.matmul(o_ps[o][:, 0:ROWS], w2[:, p, k, o * P:(o + 1) * P], hT[:, k, :], start=(k == 0), stop=(k == MC - 1))
                mm.then_inc(o_done, 1)

            turn_x(0, 0)
            for_experts(pe, step)
            turn_out(E8 - 1, 1)

        @block.scalar
        def _(act):
            act.sem_inc(h_out, 2)
            act.sem_inc(o_done, 1)
            act.wait_ge(biases, 32)

            def turned(e, p):
                act.wait_ge(x_turned, e + 3)
                for c in range(DC):
                    ins = nc.scalar.activation(xT[:, p, c, :], x_ps[c][:, 0:ROWS], ACT.Copy)
                ins.then_inc(xT_out, 1)

            def step(e, p, first, final):
                for k in range(MC):
                    act.wait_ge(h_done, e * MC + (k + 1))
                    if k == 0:
                        act.wait_ge(o_done, e + 1)
                    nc.scalar.activation(hT[:, k, :], h_ps[k % 2][:, 0:ROWS], ACT.Gelu, bias=b1[:, bass.ds(e, 1), k]).then_inc(h_out, 1)
                if not final:
                    turned(e + 1, 1 - p)

            turned(0, 0)
            for_experts(act, step)

        @block.vector
        def _(v):
            v.sem_inc(o_out, 1)
            v.sem_inc(r_out, 1)
            v.sem_inc(r_done, 1)
            v.wait_ge(biases, 32)

            def turned_out(e, p):
                v.wait_ge(r_done, e + 2)
                v.wait_ge(stored[p], (e - p) * 8 + 16)
                for g in range(2):
                    ins = nc.vector.tensor_copy(r[:, p, 2 * g:2 * g + 2, :], r_ps[g][0:XQ, 0:2 * D].rearrange("p (g d) -> p g d", d=D))
                ins.then_inc(r_out, 1)

            def step(e, p, first, final):
                if not first:
                    turned_out(e - 1, 1 - p)
                v.wait_ge(o_done, e + 2)
                v.wait_ge(r_done, e + 1)
                for o in range(DC):
                    ins = nc.vector.tensor_scalar(oT[:, o, :], o_ps[o][:, 0:ROWS], b2[:, bass.ds(e, 1), o], None, ALU.add)
                ins.then_inc(o_out, 1)

            for_experts(v, step)
            turned_out(E8 - 1, 1)


def combine2(nc, a, out, m, ctx):
    SL = 6
    sb = lambda name, shape: m["sb"](name, shape, F32, ctx)
    sem = lambda name: m["sem"](name, ctx)
    H, A, w = m["H"], m["A"], m["w"]
    got, g, b, y = sb("got", [P, SL, D]), sb("lng", [P, D]), sb("lnb", [P, D]), sb("y", [P, 2, D])
    loaded = [sem(f"g_loaded{i}") for i in range(SL)]
    used, consts, summed, stats, dve, var_ready, std_ready, scaled, fin = map(
        sem, ("g_used", "ln_loaded", "h_plus_b", "cstats", "cdve", "cvar", "cstd", "scaled", "fin"))
    stored = sem("out_stored")
    rows = out.rearrange("b s d -> (b s) d")
    with nc.Block() as block:
        @block.sync
        def _(sp):
            sp.dma_start(g[:, :], a["ln_g"].partition_broadcast(P)).then_inc(consts, 16)
            sp.dma_start(b[:, :], a["ln_b"].partition_broadcast(P)).then_inc(consts, 16)
            with sp.Fori(0, T - 1) as i:
                sp.wait_ge(fin, i + 3)
                sp.dma_start(rows[bass.ds(i * P, P), :], tile_of(A, i)).then_inc(stored, 16)
            sp.wait_ge(fin, T + 2)
            sp.dma_start(rows[(T - 1) * P:N, :], A[0:LAST, T - 1, :]).then_inc(stored, 16)
            sp.wait_ge(stored, 16 * T)

        @block.gpsimd
        def _(pool):
            gather_rows(nc, pool, m, m["outs2"], E8 * ROWS, got, loaded, used, SL)
            pool.wait_ge(consts, 32)
            nc.gpsimd.tensor_tensor(H[:, :, :], H[:, :, :], mid(b[:, :], T), ALU.add).then_inc(summed, 1)

        @block.scalar
        def _(act):
            act.wait_ge(var_ready, 1)
            nc.scalar.activation(m["std"][:, :], m["var"][:, :], ACT.Sqrt, bias=m["eps"][:, 0:1]).then_inc(std_ready, 1)

        @block.vector
        def _(v):
            steps = Steps(v, dve)
            n = 0
            for i in range(T):
                v.wait_ge(loaded[n % SL], 16 * (n // SL + 1))
                nc.vector.tensor_scalar(A[:, i, :], got[:, n % SL, :], w[:, 0, i:i + 1], None, ALU.mult).then_inc(used, 1)
                n += 1
                v.wait_ge(loaded[n % SL], 16 * (n // SL + 1))
                v.wait_ge(used, n)
                nc.vector.scalar_tensor_tensor(out=A[:, i, :], in0=got[:, n % SL, :], scalar=w[:, 1, i:i + 1], in1=A[:, i, :],
                                               op0=ALU.mult, op1=ALU.add).then_inc(used, 1)
                n += 1
                v.wait_ge(used, n)
                nc.vector.bn_stats(m["st"][:, i, :], A[:, i, :]).then_inc(stats, 1)
            v.wait_ge(stats, T)
            mean_and_var(nc, steps, m["st"], m["mean"][:, :], m["var"][:, :], m["tmp"][:, :])
            v.sem_inc(var_ready, 1)
            v.wait_ge(std_ready, 1)
            steps.after(nc.vector.reciprocal(m["rstd"][:, :], m["std"][:, :]))
            v.wait_ge(consts, 32)
            v.wait_ge(summed, 1)
            v.sem_inc(fin, 2)
            with v.Fori(0, T // 2) as j:
                for p in range(2):
                    v.wait_ge(fin, j * 2 + (p + 1))
                    normalise(nc, y[:, p, :], tile_of(A, j * 2 + p), m, j * 2 + p).then_inc(scaled, 1)
                for p in range(2):
                    v.wait_ge(scaled, j * 4 + (p + 1))
                    nc.vector.tensor_tensor(y[:, p, :], y[:, p, :], g[:, :], ALU.mult).then_inc(scaled, 1)
                for p in range(2):
                    v.wait_ge(scaled, j * 4 + (p + 3))
                    nc.vector.tensor_tensor(tile_of(A, j * 2 + p), y[:, p, :], tile_of(H, j * 2 + p), ALU.add).then_inc(fin, 1)


def _laid_out(x):
    import numpy as np

    def chunks(w):
        c = w.shape[0] // P
        return w.reshape(c, P, -1).transpose(1, 0, 2)

    def column(v):
        return v.reshape(-1, P).T

    r = {k: np.asarray(v) for k, v in x.items()}
    o = {}
    px = r["x"].reshape(B, 3, 6, 16, 6, 16).transpose(1, 3, 5, 2, 4, 0).reshape(KC, P, PT, P)
    o["patches"] = px.transpose(2, 1, 0, 3)
    o["patch_w"] = chunks(r["L0_tok_W"].T)
    o["patch_b"] = r["L0_tok_b"]
    o["cls"] = r["L0_tok_class_token"].reshape(D)
    o["pos"] = r["L0_tok_pos_embedding"].reshape(1 + NPATCH, D)
    o["txt"] = r["txt"]
    o["m_gamma"], o["m_beta"] = column(r["L0_attn_ln_gamma"]), column(r["L0_attn_ln_beta"])
    o["m_win"] = chunks(r["L0_attn_W_in"])
    bi = r["L0_attn_b_in"]
    o["m_bz"] = column(bi[0:INNER])
    o["m_bx"] = bi[INNER:2 * INNER]
    o["m_bb"] = bi[2 * INNER:2 * INNER + NST].reshape(NST, 1)
    o["m_bc"] = bi[2 * INNER + NST:2 * INNER + 2 * NST].reshape(NST, 1)
    o["m_bdt"] = bi[2 * INNER + 2 * NST:].reshape(HM, 1)
    o["m_dtb"] = r["L0_attn_dt_bias"].reshape(HM, 1)
    o["m_alog"] = r["L0_attn_A_log"].reshape(HM, 1)
    o["m_d"] = r["L0_attn_D_skip"]
    o["m_wout"] = chunks(r["L0_attn_W_out"])
    o["m_bout"] = r["L0_attn_b_out"]
    o["f_norm"] = column(r["L0_ffn_norm_w"])
    o["f_gw"] = chunks(r["L0_ffn_gate_w"].T)
    o["f_gb"] = r["L0_ffn_gate_b"]
    w1 = r["L0_ffn_mlp1_w"].reshape(E8, 256, 2, DC, P)
    o["moe1_w1"] = w1.transpose(4, 0, 3, 2, 1).reshape(P, E8, DC, F1)
    o["moe1_b1"] = r["L0_ffn_mlp1_b"].reshape(E8, 256, 2).transpose(0, 2, 1).reshape(E8 * F1)
    o["moe1_w2"] = r["L0_ffn_mlp2_w"].reshape(E8, D, DC, P).transpose(3, 0, 2, 1)
    o["moe1_b2"] = r["L0_ffn_mlp2_b"].reshape(E8 * D)
    for k in ("q", "k", "v", "o", "fq", "fg"):
        o["a_w" + k] = chunks(r["L1_attn_w" + k])
        o["a_b" + k] = column(r["L1_attn_b" + k])
    o["a_bv_row"], o["a_bo_row"] = r["L1_attn_bv"], r["L1_attn_bo"]
    u = np.zeros((2, NH, AD, NH), r["L1_attn_up"].dtype)
    for i, k in enumerate(("up", "uz")):
        for h in range(NH):
            u[i, h, :, h] = r["L1_attn_" + k][h, 0]
    o["a_up"], o["a_uz"] = chunks(u[0].reshape(D, NH)), chunks(u[1].reshape(D, NH))
    o["r_gw"] = chunks(r["L1_ffn_router_w"])
    o["r_gb"] = r["L1_ffn_router_b"]
    o["x_w1"] = r["L1_ffn_w1"].reshape(E8, DC, P, HID).transpose(0, 2, 1, 3)
    o["x_w2"] = r["L1_ffn_w2"].reshape(E8, MC, P, D).transpose(0, 2, 1, 3)
    o["x_b1"] = r["L1_ffn_b1"].reshape(E8, MC, P).transpose(2, 0, 1)
    o["x_b2"] = r["L1_ffn_b2"].reshape(E8, DC, P).transpose(2, 0, 1)
    o["ln_g"], o["ln_b"] = r["L1_ffn_ln_g"], r["L1_ffn_ln_b"]
    f = np.float32
    n = np.arange(P)
    o["ident"] = np.eye(P, dtype=f)
    bf16_one = 0x3F80
    o["before"] = np.where(n[:, None] < n[None, :], bf16_one, 0).astype(np.uint16)
    o["ones_bf"] = np.full((P, P), bf16_one, np.uint16)
    win = np.zeros((48, NH, S), f)
    for h in range(NH):
        win[h, h] = np.arange(S)
        win[32 + h, h] = -1.0
    o["window"] = win
    keep = np.ones((P, E8, T), f)
    keep[:, :, 0] = 0.0
    o["keep"] = keep.reshape(P, ET)
    o["iota8"] = np.tile(np.arange(E8, dtype=f), (P, 1))
    o["iota_blk"] = np.repeat(np.arange(NBLK, dtype=f), E8).reshape(1, NBLK * E8)
    valid = np.ones((P, T), f)
    valid[LAST:, T - 1] = 0.0
    o["valid"] = valid
    o["head_of_4"] = ((n // AD)[:, None] % 4 == np.arange(4)[None, :]).astype(f)
    return {k: np.ascontiguousarray(v) for k, v in o.items()}


def kernel(**inputs):
    import numpy as _np
    import concourse.bacc as _bacc
    from concourse import mybir as _mybir
    from concourse.bass_utils import run_bass_kernel_spmd as _run

    nc = _bacc.Bacc("TRN2", target_bir_lowering=False, num_devices=1)
    arrays, args = {}, {}
    for name, v in _laid_out(inputs).items():
        arrays[f"in_{name}"] = v
        args[name] = nc.dram_tensor(f"in_{name}", v.shape, _mybir.dt.from_np(v.dtype), kind="ExternalInput").ap()
    out = nc.dram_tensor("out_0", (B, S, D), F32, kind="ExternalOutput").ap()
    build(nc, args, out)
    r = _run(nc, [arrays], core_ids=[0])
    return r.results[0]["out_0"]
```

```python
from contextlib import ExitStack

import concourse.bass as bass
from concourse import mybir

ALU = mybir.AluOpType
ACT = mybir.ActivationFunctionType
AX = mybir.AxisListType
F32 = mybir.dt.float32
BF16 = mybir.dt.bfloat16
U32 = mybir.dt.uint32
I32 = mybir.dt.int32

P = 128
B, NPATCH, NTXT = 32, 36, 32
S = 1 + NPATCH + NTXT
N = B * S
T = -(-N // P)
NPAD = T * P
LAST = N - (T - 1) * P
D = 256
DC = D // P
KP = 768
KC = KP // P
PT = B * NPATCH // P
POS = P // B
HM, HD, NST = 8, 64, 64
INNER = HM * HD
IC = INNER // P
PROJ = 2 * INNER + 2 * NST + HM
HS = HM * S
G4 = 4 * S
NG = N // G4
E8 = 8
ET = E8 * T
F1 = 512
NBLK = (2 * N + E8 * (P - 1)) // P
NH, AD = 16, 16
AS = NH * S
HID = 1024
MC = HID // P
CAP = max(int(N * 1.5 / E8), 2)
XG, XQ = 4, 104
ROWS = XG * XQ
GT = 3
ZC = 4
LN_EPS = 1e-5
RMS_EPS = 1.1920928955078125e-07
FAR = 1.0e6


def tile_of(x, i, n=1):
    return x[:, bass.ds(i, n), :].rearrange("p a b -> p (a b)")


def cols(x, start, n):
    return x[:, :, bass.ds(start, n)]


def bc(ap, shape):
    return ap.broadcast_to(shape)


def mid(ap2, n):
    p, k = ap2.shape
    return ap2.unsqueeze(1).broadcast_to([p, n, k])


def last(ap2, n):
    p, k = ap2.shape
    return ap2.unsqueeze(2).broadcast_to([p, k, n])


class Steps:

    def __init__(self, eng, sem):
        self.eng, self.sem, self.n = eng, sem, 0

    def after(self, ins):
        self.n += 1
        ins.then_inc(self.sem, 1)
        self.eng.wait_ge(self.sem, self.n)


def mean_and_var(nc, steps, st, mean, var, tmp):
    me, ve, mo, vo = st[:, :, 1], st[:, :, 2], st[:, :, 4], st[:, :, 5]
    steps.after(nc.vector.tensor_tensor(mean, me, mo, ALU.add))
    steps.after(nc.vector.tensor_scalar(mean, mean, 0.5, None, ALU.mult))
    steps.after(nc.vector.tensor_tensor(tmp, me, mo, ALU.subtract))
    steps.after(nc.vector.tensor_tensor(var, ve, vo, ALU.add))
    steps.after(nc.vector.scalar_tensor_tensor(out=tmp, in0=tmp, scalar=0.25, in1=tmp, op0=ALU.mult, op1=ALU.mult))
    steps.after(nc.vector.scalar_tensor_tensor(out=var, in0=var, scalar=1.0 / D, in1=tmp, op0=ALU.mult, op1=ALU.add))


def build(nc, a, out):
    with ExitStack() as top:
        named = {}

        def unique(name):
            named[name] = named.get(name, 0) + 1
            return name if named[name] == 1 else f"{name}_{named[name]}"

        def sb(name, shape, dt=F32, ctx=top):
            return ctx.enter_context(nc.sbuf_tensor(unique(name), shape, dt))

        phase_sems = []

        def sem(name, ctx=None):
            handle = nc.alloc_semaphore(name=unique(name))
            if ctx is not None:
                phase_sems.append(handle)
            return handle

        def scratch(name, shape):
            return nc.dram_tensor(name, shape, F32, kind="Internal").ap()

        m = {}
        m["sb"], m["sem"] = sb, sem
        m["ps"] = lambda name, shape, ctx, dt=F32: ctx.enter_context(nc.psum_tensor(unique(name), shape, dt))
        m["tokens"] = scratch("tokens", (N, D))
        m["bcast"] = scratch("bcast", (B, 2, HM, S))
        m["rows1"] = scratch("rows1", (NBLK * P, D))
        m["outs1"] = scratch("outs1", (NBLK * P, D))
        m["rows2"] = scratch("rows2", (E8 * ROWS, D))
        m["outs2"] = scratch("outs2", (E8 * ROWS, D))
        m["H"] = sb("H", [P, T, D])
        m["A"] = sb("A", [P, T, D])
        m["ident"] = sb("ident", [P, P])
        m["st"] = sb("st", [P, T, 6])
        for name in ("mean", "var", "rstd", "tmp", "std", "var2", "rstd2", "std2"):
            m[name] = sb(name, [P, T])
        m["eps"] = sb("eps", [P, 2])
        for name, shape, dt in (("before", [P, P], BF16), ("ones_bf", [P, P], BF16), ("keep", [P, ET], F32), ("iota8", [P, E8], F32), ("valid", [P, T], F32)):
            m[name] = sb(name, shape, dt)
        m["lg"], m["w"] = sb("lg", [P, T, E8]), sb("w", [P, 2, T])
        m["gidx"], m["sidx"] = sb("gidx", [P, 2, T], U32), sb("sidx", [P, 2, T], U32)
        m["w1"] = sb("moe1_w1", [P, E8, DC, F1])
        m["w2"] = sb("moe1_w2", [P, E8, DC, D])
        m["moe1_loaded"] = sem("moe1_loaded")
        m["zero"] = sb("zero", [P, ZC, D])
        m["zeros_stored1"], m["zeros_stored2"] = sem("zeros_stored1"), sem("zeros_stored2")
        for phase in (embed, mamba, moe1, attention, moe2):
            with ExitStack() as ctx:
                phase(nc, a, out, m, ctx)
            nc.clear_and_free_semaphores(phase_sems)
            nc.all_engine_barrier()
            phase_sems.clear()


def store_zeros(sp, m, rows, stored):
    r = rows.rearrange("(n p) d -> p n d", p=P)
    for c in range(0, r.shape[1], ZC):
        k = min(ZC, r.shape[1] - c)
        sp.dma_start(r[:, c:c + k, :], m["zero"][:, 0:k, :]).then_inc(stored, 16)


def zeros_count(nrows):
    return 16 * -(-(nrows // P) // ZC)


def embed(nc, a, out, m, ctx):
    sb = lambda name, shape, dt=F32: m["sb"](name, shape, dt, ctx)
    sem = lambda name: m["sem"](name, ctx)
    tokens, H, A = m["tokens"], m["H"], m["A"]
    rows = tokens.rearrange("(b s) d -> b s d", s=S)
    w = sb("patch_w", [P, KC, D])
    patches = sb("patches", [P, 3, KC, P])
    pos = sb("pos", [P, PT, D])
    bias = sb("patch_b", [P, D])
    cls = sb("cls", [B, 2, D])
    emb = sb("emb", [P, 3, D])
    zero = m["zero"]
    acc = [m["ps"](f"patch_acc{i}", [P, 512], ctx) for i in range(3)]
    w_loaded, consts, patches_free = map(sem, ("pw_loaded", "pc_loaded", "p_free"))
    patches_loaded = [sem(f"patches_loaded{p}") for p in range(3)]
    emb_stored = [sem(f"emb_stored{p}") for p in range(3)]
    pos_ready, acc_ready = map(sem, ("pos_ready", "acc_ready"))
    cls_ready, direct, zeroed, h_loaded, pad_ready = map(
        sem, ("cls_ready", "direct", "zeroed", "h_loaded", "pad_ready"))

    with nc.Block() as block:
        @block.sync
        def _(sp):
            sp.dma_start(w[:, :, :], a["patch_w"]).then_inc(w_loaded, 16)
            sp.dma_start(bias[:, :], a["patch_b"].partition_broadcast(P)).then_inc(consts, 16)
            for q in range(POS):
                src = a["pos"][1:, :].rearrange("(t q) d -> q t d", q=POS)[q]
                sp.dma_start(pos[q * B:(q + 1) * B, :, :], src.partition_broadcast(B)).then_inc(consts, 16)
            sp.dma_start(cls[:, 0, :], a["cls"].partition_broadcast(B)).then_inc(consts, 16)
            sp.dma_start(cls[:, 1, :], a["pos"][0].partition_broadcast(B)).then_inc(consts, 16)
            with sp.Fori(0, PT // 3) as j:
                for p in range(3):
                    sp.wait_ge(patches_free, j * 3 + (p + 1))
                    sp.dma_start(patches[:, p, :, :], a["patches"][bass.ds(j * 3 + p, 1)].rearrange("o p c q -> (o p) c q")).then_inc(patches_loaded[p], 16)
            for name in ("ident", "keep", "iota8", "valid"):
                sp.dma_start(m[name][:, :], a[name]).then_inc(h_loaded, 16)
            for name in ("before", "ones_bf"):
                sp.dma_start(m[name][:, :].bitcast(mybir.dt.uint16), a[name]).then_inc(h_loaded, 16)
            sp.dma_start(rows[:, 1 + NPATCH:, :], a["txt"]).then_inc(direct, 16)
            sp.wait_ge(cls_ready, 1)
            sp.dma_start(rows[:, 0, :], cls[:, 0, :]).then_inc(direct, 16)
            sp.wait_ge(direct, 32)
            for p in range(3):
                sp.wait_ge(emb_stored[p], 16 * POS * (PT // 3 + 1))
            sp.wait_ge(pad_ready, 1)
            full = (T - 1) * P
            sp.dma_start(H[:, 0:T - 1, :], tokens[0:full, :].rearrange("(t p) d -> p t d", p=P)).then_inc(h_loaded, 16)
            sp.dma_start(H[0:LAST, T - 1, :], tokens[full:N, :]).then_inc(h_loaded, 16)
            sp.dma_start(m["w1"][:, :, :, :], a["moe1_w1"]).then_inc(m["moe1_loaded"], 16)
            sp.dma_start(m["w2"][:, :, :, :], a["moe1_w2"]).then_inc(m["moe1_loaded"], 16)
            sp.wait_ge(h_loaded, 16 * 8)
            sp.wait_ge(zeroed, 1)

        @block.gpsimd
        def _(pool):
            nc.gpsimd.memset(zero[:, :, :], 0.0).then_inc(zeroed, 1)
            nc.gpsimd.memset(H[:, T - 1, :], 0.0).then_inc(pad_ready, 1)
            nc.gpsimd.memset(m["eps"][:, 0:1], LN_EPS)
            nc.gpsimd.memset(m["eps"][:, 1:2], RMS_EPS)

        @block.tensor
        def _(pe):
            pe.sem_inc(patches_free, 3)
            pe.wait_ge(w_loaded, 16)
            with pe.Fori(0, PT // 3) as j:
                for p in range(3):
                    pe.wait_ge(patches_loaded[p], j * 16 + 16)
                    pe.wait_ge(acc_ready, j * 3 + (p + 1))
                    for c in range(KC):
                        mm = nc.tensor.matmul(acc[p][:, 0:D], patches[:, p, c, :], w[:, c, :], start=(c == 0), stop=(c == KC - 1))
                    mm.then_inc(patches_free, 1)

        @block.vector
        def _(v):
            v.sem_inc(acc_ready, 3)
            v.wait_ge(consts, 16 * (3 + POS))
            nc.vector.tensor_tensor(cls[:, 0, :], cls[:, 0, :], cls[:, 1, :], ALU.add).then_inc(cls_ready, 1)
            nc.vector.tensor_tensor(pos[:, :, :], pos[:, :, :], mid(bias[:, :], PT), ALU.add).then_inc(pos_ready, 1)
            v.wait_ge(pos_ready, 1)
            with v.Fori(0, PT // 3) as j:
                for p in range(3):
                    v.wait_ge(patches_free, j * 3 + (p + 4))
                    v.wait_ge(emb_stored[p], j * (16 * POS) + 16 * POS)
                    nc.vector.tensor_tensor(emb[:, p, :], acc[p][:, 0:D], tile_of(pos, j * 3 + p), ALU.add).then_inc(acc_ready, 1)

        @block.scalar
        def _(act):
            for p in range(3):
                act.sem_inc(emb_stored[p], 16 * POS)
            with act.Fori(0, PT // 3) as j:
                for p in range(3):
                    act.wait_ge(acc_ready, j * 3 + (p + 4))
                    for q in range(POS):
                        dst = rows[:, bass.ds((j * 3 + p) * POS + (1 + q), 1), :].rearrange("b o d -> b (o d)")
                        act.dma_start(dst, emb[q * B:(q + 1) * B, p, :]).then_inc(emb_stored[p], 16)


def layer_stats(nc, v, steps, m, x, sem_name_done):
    with v.Fori(0, T // 3) as j:
        for p in range(3):
            nc.vector.bn_stats(m["st"][:, bass.ds(j * 3 + p, 1), :], x[:, bass.ds(j * 3 + p, 1), :]).then_inc(sem_name_done, 1)
    v.wait_ge(sem_name_done, T)


def moments(nc, v, steps, m, var_ready, second_eps=None):
    mean_and_var(nc, steps, m["st"], m["mean"][:, :], m["var"][:, :], m["tmp"][:, :])
    if second_eps is not None:
        steps.after(nc.vector.tensor_scalar(m["var2"][:, :], m["var"][:, :], 1.0 + second_eps, LN_EPS * second_eps, ALU.mult, ALU.add))
    v.sem_inc(var_ready, 1)


def roots(nc, act, m, var_ready, std_ready, second=False):
    act.wait_ge(var_ready, 1)
    ins = nc.scalar.activation(m["std"][:, :], m["var"][:, :], ACT.Sqrt, bias=m["eps"][:, 0:1])
    if second:
        ins = nc.scalar.activation(m["std2"][:, :], m["var2"][:, :], ACT.Sqrt)
    ins.then_inc(std_ready, 1)


def reciprocals(nc, v, steps, m, std_ready, second=False):
    v.wait_ge(std_ready, 1)
    if second:
        nc.vector.reciprocal(m["rstd2"][:, :], m["std2"][:, :])
    steps.after(nc.vector.reciprocal(m["rstd"][:, :], m["std"][:, :]))


def normalise(nc, dst, src, m, i, rstd="rstd"):
    return nc.vector.tensor_scalar(dst, src, m["mean"][:, bass.ds(i, 1)], m[rstd][:, bass.ds(i, 1)], ALU.subtract, ALU.mult)


NP = 3


def add_normed(nc, pool, m, normed, added):
    n = T // NP
    for c in range(NP):
        pool.wait_ge(normed, n * (c + 1))
        nc.gpsimd.tensor_tensor(m["H"][:, c * n:(c + 1) * n, :], m["H"][:, c * n:(c + 1) * n, :], m["A"][:, c * n:(c + 1) * n, :], ALU.add).then_inc(added, 1)


def pre_mamba(nc, a, out, m, ctx):
    sem = lambda name: m["sem"](name, ctx)
    H, A, uT, ident = m["H"], m["A"], m["uT"], m["ident"]
    gamma = m["sb"]("m_gamma", [P, DC], F32, ctx)
    beta = m["sb"]("m_beta", [P, DC], F32, ctx)
    u = m["sb"]("u", [P, 2, D], F32, ctx)
    ut = [m["ps"](f"ut{i}", [P, DC, P], ctx) for i in range(2)]
    stats1, var_ready, std_ready, dve, norm_ready, u_ready, ut_ready, ut_free, consts, summed = map(
        sem, ("stats1", "var_ready", "std_ready", "dve", "norm_ready", "u_ready", "ut_ready", "ut_free", "gb", "summed"))

    with nc.Block() as block:
        @block.sync
        def _(sp):
            sp.dma_start(gamma[:, :], a["m_gamma"]).then_inc(consts, 16)
            sp.dma_start(beta[:, :], a["m_beta"]).then_inc(consts, 16)

        @block.vector
        def _(v):
            steps = Steps(v, dve)
            layer_stats(nc, v, steps, m, H, stats1)
            moments(nc, v, steps, m, var_ready, LN_EPS)
            reciprocals(nc, v, steps, m, std_ready, True)
            with v.Fori(0, T // 2) as j:
                for p in range(2):
                    v.wait_ge(ut_ready, j * 2 + (p + 1))
                    normalise(nc, u[:, p, :], tile_of(H, j * 2 + p), m, j * 2 + p, "rstd2").then_inc(u_ready, 1)
                    normalise(nc, tile_of(A, j * 2 + p), tile_of(H, j * 2 + p), m, j * 2 + p).then_inc(norm_ready, 1)

        @block.gpsimd
        def _(pool):
            add_normed(nc, pool, m, norm_ready, summed)

        @block.scalar
        def _(act):
            roots(nc, act, m, var_ready, std_ready, True)
            act.wait_ge(consts, 32)
            act.sem_inc(ut_free, 2)
            with act.Fori(0, T // 2) as j:
                for p in range(2):
                    act.wait_ge(ut_ready, j * 2 + (p + 3))
                    for c in range(DC):
                        ins = nc.scalar.activation(uT[:, c, bass.ds((j * 2 + p) * P, P)], ut[p][:, c, :], ACT.Identity,
                                                   bias=beta[:, c:c + 1], scale=gamma[:, c:c + 1])
                    ins.then_inc(ut_free, 1)

        @block.tensor
        def _(pe):
            pe.sem_inc(ut_ready, 2)
            with pe.Fori(0, T // 2) as j:
                for p in range(2):
                    pe.wait_ge(u_ready, j * 2 + (p + 1))
                    pe.wait_ge(ut_free, j * 2 + (p + 1))
                    for c in range(DC):
                        ins = nc.tensor.transpose(ut[p][:, c, :], u[:, p, c * P:(c + 1) * P], ident[:, :])
                    ins.then_inc(ut_ready, 1)


def mamba(nc, a, out, m, ctx):
    sb = lambda name, shape: m["sb"](name, shape, F32, ctx)
    m["uT"] = sb("uT", [P, DC + 1, NPAD])
    pre_ctx = ExitStack()
    with pre_ctx:
        pre_mamba(nc, a, out, m, pre_ctx)
    m["cT"] = sb("cT", [NST, NPAD])
    m["gate"] = sb("gate", [P, IC, NPAD])
    m["win"] = sb("win", [P, DC, PROJ])
    for part in (mamba_project, mamba_core, mamba_out):
        with ExitStack() as c:
            part(nc, a, out, m, c)


def mamba_project(nc, a, out, m, ctx):
    sb = lambda name, shape: m["sb"](name, shape, F32, ctx)
    sem = lambda name: m["sem"](name, ctx)
    uT, cT, gate, win = m["uT"], m["cT"], m["gate"], m["win"]
    bz, bb, bcc = sb("bz", [P, IC]), sb("bb", [NST, 1]), sb("bcc", [NST, 1])
    bdt, dtb, alog = sb("bdt", [HM, 1]), sb("dtb", [HM, 1]), sb("alog", [HM, 1])
    dt, low, dec = sb("dt", [HM, N]), sb("low", [HM, N]), sb("dec", [HM, N])
    loaded, dve, dt_done, bc_done, psum_free, dt_raw, soft, decayed, stored, z_done, z_free, padded, prep = map(
        sem, ("pj_loaded", "pj_dve", "dt_done", "bc_done", "bc_free", "dt_raw", "soft", "decayed", "dt_stored", "z_done", "z_free", "padded", "prep"))
    OB, OC, ODT = 2 * INNER, 2 * INNER + NST, 2 * INNER + 2 * NST

    bout, bout_loaded = sb("m_bout", [P, D]), sem("bout_loaded")

    with ExitStack() as c1:
        acc = [[m["ps"](f"acc_{k}{i}", [P, 512], c1) for i in range(2)] for k in ("dt", "b", "c")]
        with nc.Block() as block:
            @block.sync
            def _(sp):
                sp.dma_start(win[:, :, :], a["m_win"]).then_inc(loaded, 16)
                for t, k in ((bz, "m_bz"), (bb, "m_bb"), (bcc, "m_bc"), (bdt, "m_bdt"), (dtb, "m_dtb"), (alog, "m_alog")):
                    sp.dma_start(t[:, :], a[k]).then_inc(loaded, 16)
                sp.dma_start(bout[:, :], a["m_bout"].partition_broadcast(P)).then_inc(bout_loaded, 16)
                sp.wait_ge(loaded, 7 * 16)
                store_zeros(sp, m, m["rows1"], m["zeros_stored1"])

            @block.gpsimd
            def _(pool):
                nc.gpsimd.memset(uT[NST:P, DC, :], 0.0).then_inc(padded, 1)
                pool.wait_ge(padded, 1)
                nc.gpsimd.memset(gate[:, :, N:NPAD], 0.0).then_inc(padded, 1)
                pool.wait_ge(bout_loaded, 16)
                pool.wait_ge(padded, 2)
                nc.gpsimd.tensor_tensor(m["H"][:, :, :], m["H"][:, :, :], mid(bout[:, :], T), ALU.add).then_inc(padded, 1)

            @block.tensor
            def _(pe):
                pe.wait_ge(loaded, 7 * 16)
                with pe.Fori(0, NG // 2) as j:
                    for p in range(2):
                        pe.wait_ge(psum_free, j * 2 + (p + 1))
                        for k, (o, n) in enumerate(((ODT, HM), (OB, NST), (OC, NST))):
                            for c in range(DC):
                                mm = nc.tensor.matmul(acc[k][p][0:n, 0:G4], win[:, c, o:o + n], uT[:, c, bass.ds((j * 2 + p) * G4, G4)],
                                                      start=(c == 0), stop=(c == DC - 1))
                        mm.then_inc(bc_done, 1)

            @block.vector
            def _(v):
                steps = Steps(v, dve)
                v.sem_inc(psum_free, 2)
                v.wait_ge(loaded, 7 * 16)
                steps.after(nc.vector.tensor_tensor(bdt[:, :], bdt[:, :], dtb[:, :], ALU.add))
                with v.Fori(0, NG // 2) as j:
                    for p in range(2):
                        v.wait_ge(bc_done, j * 2 + (p + 1))
                        here = bass.ds((j * 2 + p) * G4, G4)
                        nc.vector.tensor_scalar(dt[:, here], acc[0][p][0:HM, 0:G4], bdt[:, 0:1], None, ALU.add)
                        nc.vector.tensor_scalar(uT[0:NST, DC, here], acc[1][p][0:NST, 0:G4], bb[:, 0:1], None, ALU.add)
                        nc.vector.tensor_scalar(cT[:, here], acc[2][p][0:NST, 0:G4], bcc[:, 0:1], None, ALU.add).then_inc(psum_free, 1)

    zacc = [[m["ps"](f"zacc{i}{k}", [P, 512], ctx) for k in range(IC)] for i in range(2)]
    rows = m["bcast"]
    with nc.Block() as block:
        @block.vector
        def _(v):
            nc.vector.tensor_scalar(low[:, :], dt[:, :], -1.0, None, ALU.mult).then_inc(dt_raw, 1)
            v.wait_ge(dt_raw, 1)
            nc.vector.tensor_tensor(low[:, :], low[:, :], dt[:, :], ALU.min).then_inc(dt_raw, 1)
            v.wait_ge(soft, 2)
            nc.vector.scalar_tensor_tensor(out=dt[:, :], in0=dt[:, :], scalar=0.0, in1=low[:, :], op0=ALU.max, op1=ALU.add).then_inc(dt_raw, 1)
            v.wait_ge(decayed, 2)
            nc.vector.memset(dec[:, :].rearrange("h (b s) -> h b s", s=S)[:, :, 0:1], 0.0).then_inc(dt_raw, 1)

        @block.scalar
        def _(act):
            act.wait_ge(dt_raw, 2)
            nc.scalar.activation(low[:, :], low[:, :], ACT.Exp).then_inc(soft, 1)
            act.wait_ge(soft, 1)
            nc.scalar.activation(low[:, :], low[:, :], ACT.Ln, bias=1.0).then_inc(soft, 1)
            nc.scalar.activation(alog[:, :], alog[:, :], ACT.Exp).then_inc(decayed, 1)
            act.wait_ge(decayed, 1)
            act.wait_ge(dt_raw, 3)
            nc.scalar.activation(dec[:, :], dt[:, :], ACT.Copy, scale=alog[:, 0:1]).then_inc(prep, 1)
            act.wait_ge(prep, 1)
            nc.scalar.activation(dec[:, :], dec[:, :], ACT.Exp, scale=-1.0).then_inc(decayed, 1)
            act.sem_inc(z_free, 2)
            with act.Fori(0, NG // 2) as j:
                for p in range(2):
                    act.wait_ge(z_done, j * 2 + (p + 1))
                    for k in range(IC):
                        ins = nc.scalar.activation(gate[:, k, bass.ds((j * 2 + p) * G4, G4)], zacc[p][k][:, 0:G4], ACT.Silu, bias=bz[:, k:k + 1])
                    ins.then_inc(z_free, 1)

        @block.sync
        def _(sp):
            sp.wait_ge(dt_raw, 4)
            sp.dma_start(rows[:, 0].rearrange("b h s -> h b s"), dec[:, :].rearrange("h (b s) -> h b s", s=S)).then_inc(stored, 16)
            sp.dma_start(rows[:, 1].rearrange("b h s -> h b s"), dt[:, :].rearrange("h (b s) -> h b s", s=S)).then_inc(stored, 16)
            sp.wait_ge(stored, 32)

        @block.tensor
        def _(pe):
            with pe.Fori(0, NG // 2) as j:
                for p in range(2):
                    pe.wait_ge(z_free, j * 2 + (p + 1))
                    for k in range(IC):
                        for c in range(DC):
                            mm = nc.tensor.matmul(zacc[p][k][:, 0:G4], win[:, c, k * P:(k + 1) * P], uT[:, c, bass.ds((j * 2 + p) * G4, G4)],
                                                  start=(c == 0), stop=(c == DC - 1))
                    mm.then_inc(z_done, 1)


def mamba_core(nc, a, out, m, ctx):
    sb = lambda name, shape: m["sb"](name, shape, F32, ctx)
    sem = lambda name: m["sem"](name, ctx)
    uT, cT, gate, win, ident = m["uT"], m["cT"], m["gate"], m["win"], m["ident"]
    KB = 80
    us = sb("us", [P, 2, DC + 1, S])
    rows = sb("rows_b", [KB, 2, 2, HS])
    xs = sb("xs", [S, 2, INNER])
    inj = sb("inj", [S, 2, HS])
    sc = sb("sc", [S, 2, HS])
    bx = sb("bx", [S, INNER])
    dd = sb("dd", [S, HM])
    dI = sb("dI", [S, HS])
    x_ps = [m["ps"](f"x_ps{i}", [P, 512], ctx) for i in range(2)]
    g_ps = [m["ps"](f"g_ps{i}", [P, 512], ctx) for i in range(2)]
    y_ps = [m["ps"](f"y_ps{i}", [P, IC, P], ctx) for i in range(2)]
    consts, d_ready, us_ready, xg_done, x_ready, inj_ready, scanned, mult, m_ready, y_done, y_out = map(
        sem, ("mc_consts", "d_ready", "us_ready", "xg_done", "x_ready", "inj_ready", "scanned", "mult", "m_ready", "y_done", "y_out"))
    rows_loaded = [sem(f"rows_loaded{p}") for p in range(2)]
    S3 = [S, HM, S]

    def v3(x):
        return x.rearrange("p (h s) -> p h s", s=S)

    with nc.Block() as block:
        @block.sync
        def _(sp):
            sp.dma_start(bx[:, :], a["m_bx"].partition_broadcast(S)).then_inc(consts, 16)
            sp.dma_start(dd[:, :], a["m_d"].partition_broadcast(S)).then_inc(consts, 16)
            with sp.Fori(0, B // 2) as j:
                for p in range(2):
                    sp.wait_ge(scanned, j * 2 + (p + 1))
                    sp.dma_start(rows[:, p, :, :], m["bcast"][bass.ds(j * 2 + p, 1)].rearrange("o k h s -> (o k) (h s)").partition_broadcast(KB)).then_inc(rows_loaded[p], 16)

        @block.scalar
        def _(act):
            with act.Fori(0, B // 2) as j:
                for p in range(2):
                    act.wait_ge(xg_done, j * 2 + (p + 1))
                    nc.scalar.activation(us[:, p, :, :], cols(uT, (j * 2 + p) * S, S), ACT.Copy).then_inc(us_ready, 1)

        @block.gpsimd
        def _(pool):
            pool.wait_ge(consts, 32)
            nc.gpsimd.tensor_tensor(v3(dI[:, :]), mid(ident[0:S, 0:S], HM), last(dd[:, :], S), ALU.mult).then_inc(d_ready, 1)

            def inject(i, p):
                pool.wait_ge(rows_loaded[p], (i - p) * 8 + 16)
                pool.wait_ge(scanned, i + 1)
                nc.gpsimd.tensor_tensor(v3(inj[:, p, :]), mid(ident[0:S, 0:S], HM), v3(rows[0:S, p, 1, :]), ALU.mult).then_inc(inj_ready, 1)

            def skip(i, p):
                pool.wait_ge(mult, i + 3)
                nc.gpsimd.tensor_tensor(sc[:, p, :], sc[:, p, :], dI[:, :], ALU.add).then_inc(m_ready, 1)

            inject(0, 0)
            pool.wait_ge(d_ready, 1)
            with pool.Fori(0, B // 2 - 1) as j:
                for p in range(2):
                    inject(j * 2 + (p + 1), 1 - p)
                    skip(j * 2 + p, p)
            inject(B - 1, 1)
            skip(B - 2, 0)
            skip(B - 1, 1)

        @block.tensor
        def _(pe):
            pe.sem_inc(xg_done, 2)

            def front(i, p):
                pe.wait_ge(us_ready, i + 1)
                pe.wait_ge(x_ready, i + 1)
                for c in range(DC):
                    nc.tensor.matmul(x_ps[p][0:S, 0:INNER], us[:, p, c, :], win[:, c, INNER:2 * INNER], start=(c == 0), stop=(c == DC - 1))
                pe.wait_ge(mult, i + 1)
                nc.tensor.matmul(g_ps[p][0:S, 0:S], us[0:NST, p, DC, :], cT[:, bass.ds(i * S, S)], start=True, stop=True).then_inc(xg_done, 1)

            def back(i, p):
                pe.wait_ge(m_ready, i + 1)
                pe.wait_ge(y_out, i + 1)
                for h in range(HM):
                    o = (h % 2) * HD
                    mm = nc.tensor.matmul(y_ps[p][o:o + HD, h // 2, 0:S], xs[:, p, h * HD:(h + 1) * HD], sc[:, p, h * S:(h + 1) * S], start=True, stop=True)
                mm.then_inc(y_done, 1)

            front(0, 0)
            front(1, 1)
            with pe.Fori(0, B // 2 - 1) as j:
                for p in range(2):
                    back(j * 2 + p, p)
                    front(j * 2 + (p + 2), p)
            back(B - 2, 0)
            back(B - 1, 1)

        @block.vector
        def _(v):
            v.sem_inc(x_ready, 2)
            v.sem_inc(scanned, 2)
            v.sem_inc(mult, 2)
            v.sem_inc(y_done, 2)
            v.sem_inc(y_out, 2)
            v.wait_ge(consts, 32)

            def front(i, p):
                v.wait_ge(xg_done, i + 3)
                v.wait_ge(y_done, i + 1)
                nc.vector.tensor_tensor(xs[:, p, :], x_ps[p][0:S, 0:INNER], bx[:, :], ALU.add).then_inc(x_ready, 1)
                v.wait_ge(inj_ready, i + 1)
                nc.vector.tensor_tensor_scan(sc[:, p, :], rows[0:S, p, 0, :], inj[:, p, :], 0.0, ALU.mult, ALU.add).then_inc(scanned, 1)
                v.wait_ge(scanned, i + 3)
                nc.vector.tensor_tensor(v3(sc[:, p, :]), v3(sc[:, p, :]), mid(g_ps[p][0:S, 0:S], HM), ALU.mult).then_inc(mult, 1)

            def back(i, p):
                v.wait_ge(y_done, i + 3)
                g = cols(gate, i * S, S)
                nc.vector.tensor_tensor(g, y_ps[p][:, :, 0:S], g, ALU.mult).then_inc(y_out, 1)

            front(0, 0)
            with v.Fori(0, B // 2 - 1) as j:
                for p in range(2):
                    front(j * 2 + (p + 1), 1 - p)
                    back(j * 2 + p, p)
            front(B - 1, 1)
            back(B - 2, 0)
            back(B - 1, 1)


def mamba_out(nc, a, out, m, ctx):
    out_project(nc, m, ctx, m["gate"], IC, a["m_wout"])


def out_project(nc, m, ctx, src, chunks, w_dram):
    H = m["H"]
    w = m["sb"]("w_out", [P, chunks, D], F32, ctx)
    lhs = m["sb"]("lhs", [P, 2, chunks, P], F32, ctx)
    ps = [m["ps"](f"o_ps{i}", [P, 512], ctx) for i in range(2)]
    loaded, lhs_ready, done, added = (m["sem"](n, ctx) for n in ("wo_loaded", "lhs_ready", "o_done", "added"))
    with nc.Block() as block:
        @block.sync
        def _(sp):
            sp.dma_start(w[:, :, :], w_dram).then_inc(loaded, 16)

        @block.scalar
        def _(act):
            with act.Fori(0, T // 2) as j:
                for p in range(2):
                    act.wait_ge(done, j * 2 + (p + 1))
                    nc.scalar.activation(lhs[:, p, :, :], cols(src, (j * 2 + p) * P, P), ACT.Copy).then_inc(lhs_ready, 1)

        @block.tensor
        def _(pe):
            pe.sem_inc(done, 2)
            pe.wait_ge(loaded, 16)
            with pe.Fori(0, T // 2) as j:
                for p in range(2):
                    pe.wait_ge(lhs_ready, j * 2 + (p + 1))
                    pe.wait_ge(added, j * 2 + (p + 1))
                    for c in range(chunks):
                        mm = nc.tensor.matmul(ps[p][:, 0:D], lhs[:, p, c, :], w[:, c, :], start=(c == 0), stop=(c == chunks - 1))
                    mm.then_inc(done, 1)

        @block.vector
        def _(v):
            v.sem_inc(added, 2)
            with v.Fori(0, T // 2) as j:
                for p in range(2):
                    v.wait_ge(done, j * 2 + (p + 3))
                    h = tile_of(H, j * 2 + p)
                    nc.vector.tensor_tensor(h, ps[p][:, 0:D], h, ALU.add).then_inc(added, 1)
                    v.wait_ge(added, j * 2 + (p + 3))
                    nc.vector.bn_stats(m["st"][:, bass.ds(j * 2 + p, 1), :], H[:, bass.ds(j * 2 + p, 1), :])


def route_front(nc, a, m, ctx, rms, norm, gw_dram, gb_dram):
    sb = lambda name, shape, dt=F32: m["sb"](name, shape, dt, ctx)
    sem = lambda name: m["sem"](name, ctx)
    H, A, ident, lg = m["H"], m["A"], m["ident"], m["lg"]
    R = m["R"]
    gw, gb, nw = sb("gw", [P, DC, E8]), sb("gb", [P, E8]), sb("nw", [P, DC])
    x = sb("rx", [P, 2, D])
    xT = sb("rxT", [P, 2, DC, P])
    t_ps = [m["ps"](f"rt_ps{i}", [P, DC, P], ctx) for i in range(2)]
    l_ps = [m["ps"](f"rl_ps{i}", [P, 512], ctx) for i in range(2)]
    loaded, dve, var_ready, std_ready, norm_ready, r_ready, x_ready, t_done, t_out, l_done, l_out, summed = map(
        sem, ("rf_loaded", "rdve", "rvar", "rstd_", "rnorm", "r_ready", "rx_ready", "rt_done", "rt_out", "rl_done", "rl_out", "rsum"))
    with nc.Block() as block:
        @block.sync
        def _(sp):
            sp.dma_start(gw[:, :, :], gw_dram).then_inc(loaded, 16)
            sp.dma_start(gb[:, :], gb_dram.partition_broadcast(P)).then_inc(loaded, 16)
            if norm is not None:
                sp.dma_start(nw[:, :], norm).then_inc(loaded, 16)
            sp.wait_ge(loaded, 48 if rms else 32)

        @block.vector
        def _(v):
            steps = Steps(v, dve)
            v.sem_inc(l_out, 2)
            moments(nc, v, steps, m, var_ready, RMS_EPS if rms else None)
            reciprocals(nc, v, steps, m, std_ready, rms)
            with v.Fori(0, T // 2) as j:
                for p in range(2):
                    normalise(nc, tile_of(R, j * 2 + p), tile_of(H, j * 2 + p), m, j * 2 + p, "rstd2" if rms else "rstd").then_inc(r_ready, 1)
            if rms:
                with v.Fori(0, T // 2) as j:
                    for p in range(2):
                        normalise(nc, tile_of(A, j * 2 + p), tile_of(H, j * 2 + p), m, j * 2 + p).then_inc(norm_ready, 1)
            v.wait_ge(loaded, 48 if rms else 32)
            with v.Fori(0, T // 2) as j:
                for p in range(2):
                    v.wait_ge(l_done, j * 2 + (p + 3))
                    nc.vector.tensor_tensor(tile_of(lg, j * 2 + p), l_ps[p][:, 0:E8], gb[:, :], ALU.add).then_inc(l_out, 1)

        @block.gpsimd
        def _(pool):
            if rms:
                add_normed(nc, pool, m, norm_ready, summed)

        @block.scalar
        def _(act):
            roots(nc, act, m, var_ready, std_ready, rms)
            act.wait_ge(loaded, 48 if rms else 32)

            def fetch(i, p):
                act.wait_ge(r_ready, i + 1)
                act.wait_ge(t_done, i + 1)
                nc.scalar.activation(x[:, p, :], tile_of(R, i), ACT.Copy).then_inc(x_ready, 1)

            def turned(i, p):
                act.wait_ge(t_done, i + 3)
                act.wait_ge(l_done, i + 1)
                for c in range(DC):
                    if norm is not None:
                        ins = nc.scalar.activation(xT[:, p, c, :], t_ps[p][:, c, :], ACT.Copy, scale=nw[:, c:c + 1])
                    else:
                        ins = nc.scalar.activation(xT[:, p, c, :], t_ps[p][:, c, :], ACT.Copy)
                ins.then_inc(t_out, 1)

            fetch(0, 0)
            with act.Fori(0, T // 2 - 1) as j:
                for p in range(2):
                    fetch(j * 2 + (p + 1), 1 - p)
                    turned(j * 2 + p, p)
            fetch(T - 1, 1)
            turned(T - 2, 0)
            turned(T - 1, 1)

        @block.tensor
        def _(pe):
            pe.sem_inc(t_done, 2)
            pe.sem_inc(l_done, 2)
            pe.sem_inc(t_out, 2)
            pe.wait_ge(loaded, 48 if rms else 32)

            def turn(i, p):
                pe.wait_ge(x_ready, i + 1)
                pe.wait_ge(t_out, i + 1)
                for c in range(DC):
                    ins = nc.tensor.transpose(t_ps[p][:, c, :], x[:, p, c * P:(c + 1) * P], ident[:, :])
                ins.then_inc(t_done, 1)

            def logits(i, p):
                pe.wait_ge(t_out, i + 3)
                pe.wait_ge(l_out, i + 1)
                for c in range(DC):
                    ins = nc.tensor.matmul(l_ps[p][:, 0:E8], xT[:, p, c, :], gw[:, c, :], start=(c == 0), stop=(c == DC - 1))
                ins.then_inc(l_done, 1)

            turn(0, 0)
            with pe.Fori(0, T // 2 - 1) as j:
                for p in range(2):
                    turn(j * 2 + (p + 1), 1 - p)
                    logits(j * 2 + p, p)
            turn(T - 1, 1)
            logits(T - 2, 0)
            logits(T - 1, 1)


def by_tile(x):
    return x.rearrange("p (e t) -> p e t", t=T)


def top2(nc, v, steps, m, t):
    lg, m8, ix8, ixf, oh, w = m["lg"], t["m8"], t["ix8"], t["ixf"], t["oh"], m["w"]
    for i in range(T):
        ins = nc.vector.max(m8[:, i, :], lg[:, i, :])
    steps.after(ins)
    for i in range(T):
        ins = nc.vector.max_index(ix8[:, i, :], m8[:, i, :], lg[:, i, :])
    steps.after(ins)
    steps.after(nc.vector.tensor_tensor(w[:, 1, :], m8[:, :, 1], m8[:, :, 0], ALU.subtract))
    v.sem_inc(t["gap_ready"], 1)
    for k in range(2):
        ins = nc.vector.tensor_copy(ixf[:, k, :], ix8[:, :, k])
    steps.after(ins)
    for k in range(2):
        ins = nc.vector.tensor_tensor(by_tile(oh[:, k, :]), mid(ixf[:, k, :], E8), last(m["iota8"][:, :], T), ALU.is_equal)
    steps.after(ins)
    for k in range(2):
        ins = nc.vector.tensor_tensor(by_tile(oh[:, k, :]), by_tile(oh[:, k, :]), mid(m["valid"][:, :], E8), ALU.mult)
    steps.after(ins)
    v.wait_ge(t["exp_ready"], 1)
    steps.after(nc.vector.tensor_scalar(w[:, 0, :], w[:, 1, :], 1.0, None, ALU.add))
    steps.after(nc.vector.reciprocal(w[:, 0, :], w[:, 0, :]))
    steps.after(nc.vector.tensor_tensor(w[:, 1, :], w[:, 1, :], w[:, 0, :], ALU.mult))


def positions(nc, v, steps, m, t, chosen, ps_before, ps_total, asked, counted, n):
    steps.after(nc.vector.tensor_copy(t["chosen_bf"][:, :], chosen))
    v.sem_inc(asked, 1)
    v.wait_ge(counted, n)
    steps.after(nc.vector.tensor_tensor_scan(t["incl"][:, :], m["keep"][:, :], ps_total[:, 0:ET], 0.0, ALU.mult, ALU.add))
    steps.after(nc.vector.tensor_tensor(t["pos"][:, :], t["incl"][:, :], ps_total[:, 0:ET], ALU.subtract))
    steps.after(nc.vector.tensor_tensor(t["pos"][:, :], ps_before[:, 0:ET], t["pos"][:, :], ALU.add))


def count_matmuls(nc, pe, m, t, ps_before, ps_total, asked, counted, n):
    pe.wait_ge(asked, n)
    nc.tensor.matmul(ps_before[:, 0:ET], m["before"][:, :], t["chosen_bf"][:, :], start=True, stop=True)
    nc.tensor.matmul(ps_total[:, 0:ET], m["ones_bf"][:, :], t["chosen_bf"][:, :], start=True, stop=True).then_inc(counted, 1)


def row_indices(nc, steps, m, t, taken):
    for k in range(2):
        steps.after(nc.vector.tensor_tensor(t["incl"][:, :], t["oh"][:, k, :], t["pos"][:, :], ALU.mult))
        steps.after(nc.vector.tensor_reduce(t["row"][:, k, :], t["incl"][:, :].rearrange("p (e t) -> p t e", t=T), AX.X, ALU.add))
        steps.after(nc.vector.tensor_copy(m["gidx"][:, k, :], t["row"][:, k, :]))
        steps.after(nc.vector.tensor_scalar(t["ixf"][:, k, :], taken[k], -FAR, FAR, ALU.mult, ALU.add))
        steps.after(nc.vector.tensor_tensor(m["sidx"][:, k, :], t["row"][:, k, :], t["ixf"][:, k, :], ALU.add))


def routing_tensors(m, ctx):
    sb = lambda name, shape, dt=F32: m["sb"](name, shape, dt, ctx)
    t = {"m8": sb("m8", [P, T, 8]), "ix8": sb("ix8", [P, T, 8], U32), "ixf": sb("ixf", [P, 2, T]),
         "oh": sb("oh", [P, 2, ET]), "chosen": sb("chosen", [P, ET]), "chosen_bf": sb("chosen_bf", [P, ET], BF16),
         "incl": sb("incl", [P, ET]), "pos": sb("pos_e", [P, ET]), "row": sb("row", [P, 2, T])}
    for n in ("gap_ready", "exp_ready"):
        t[n] = m["sem"](n, ctx)
    return t


def scatter_rows(nc, pool, m, rows, nrows, sem):
    for k in range(2):
        for i in range(T):
            nc.gpsimd.indirect_dma_start(
                out=rows[:, :], out_offset=bass.IndirectOffsetOnAxis(ap=m["sidx"][:, k, i:i + 1], axis=0),
                in_=m["R"][:, i, :], in_offset=None, bounds_check=nrows - 1, oob_is_err=False).then_inc(sem, 16)
    pool.wait_ge(sem, 16 * 2 * T)


def moe1(nc, a, out, m, ctx):
    sb = lambda name, shape, dt=F32: m["sb"](name, shape, dt, ctx)
    sem = lambda name: m["sem"](name, ctx)
    m["R"] = sb("R", [P, T, D])
    m["nw1"] = sb("nw1", [P, DC])
    b1, b2 = sb("b1", [P, E8, F1]), sb("b2", [P, E8, D])
    table = sb("table", [1, NBLK], I32)
    nw_loaded = sem("nw_loaded")
    with ExitStack() as c:
        route_front(nc, a, m, c, True, a["f_norm"], a["f_gw"], a["f_gb"])
    with ExitStack() as c:
        t = routing_tensors(m, c)
        csb = lambda name, shape, dt=F32: m["sb"](name, shape, dt, c)
        iota_blk, full, nb, nbi = csb("iota_blk", [1, NBLK * E8]), csb("full", [1, NBLK * E8]), csb("nb", [P, E8]), csb("nbi", [P, E8], I32)
        ends, ones8, cntf = csb("ends", [P, E8]), csb("ones8", [P, E8]), csb("cntf", [1, NBLK])
        pb, pt = (m["ps"](n, [P, 512], c) for n in ("ps_before", "ps_total"))
        dve, asked, counted, idx_ready, scattered, iota_loaded = (m["sem"](n, c) for n in (
            "rt_dve", "asked", "counted", "idx_ready", "scattered", "iota_loaded"))
        with nc.Block() as block:
            @block.sync
            def _(sp):
                sp.dma_start(iota_blk[:, :], a["iota_blk"]).then_inc(iota_loaded, 16)
                sp.dma_start(b1[:, :, :], a["moe1_b1"].rearrange("(e f) -> e f", e=E8).partition_broadcast(P)).then_inc(nw_loaded, 16)
                sp.dma_start(b2[:, :, :], a["moe1_b2"].rearrange("(e f) -> e f", e=E8).partition_broadcast(P)).then_inc(nw_loaded, 16)
                sp.dma_start(m["nw1"][:, :], a["f_norm"]).then_inc(nw_loaded, 16)
                sp.wait_ge(nw_loaded, 48)

            @block.scalar
            def _(act):
                act.wait_ge(t["gap_ready"], 1)
                nc.scalar.activation(m["w"][:, 1, :], m["w"][:, 1, :], ACT.Exp).then_inc(t["exp_ready"], 1)

            @block.vector
            def _(v):
                steps = Steps(v, dve)
                top2(nc, v, steps, m, t)
                steps.after(nc.vector.tensor_tensor(t["chosen"][:, :], t["oh"][:, 0, :], t["oh"][:, 1, :], ALU.add))
                positions(nc, v, steps, m, t, t["chosen"][:, :], pb, pt, asked, counted, 1)
                steps.after(nc.vector.tensor_scalar(nbi[:, :], by_tile(t["incl"][:, :])[:, :, T - 1], float(P - 1), None, ALU.add))
                steps.after(nc.vector.tensor_scalar(nbi[:, :], nbi[:, :], 7, None, ALU.logical_shift_right))
                steps.after(nc.vector.tensor_copy(nb[:, :], nbi[:, :]))
                steps.after(nc.vector.memset(ones8[:, :], 1.0))
                steps.after(nc.vector.tensor_tensor_scan(ends[:, :], ones8[:, :], nb[:, :], 0.0, ALU.mult, ALU.add))
                steps.after(nc.vector.tensor_tensor(nb[:, :], ends[:, :], nb[:, :], ALU.subtract))
                steps.after(nc.vector.scalar_tensor_tensor(out=by_tile(t["pos"][:, :]), in0=last(nb[:, :], T), scalar=float(P),
                                                           in1=by_tile(t["pos"][:, :]), op0=ALU.mult, op1=ALU.add))
                row_indices(nc, steps, m, t, [m["valid"][:, :], m["valid"][:, :]])
                v.sem_inc(idx_ready, 1)
                v.wait_ge(iota_loaded, 16)
                steps.after(nc.vector.tensor_tensor(full[:, :].rearrange("p (n e) -> p n e", e=E8), iota_blk[:, :].rearrange("p (n e) -> p n e", e=E8),
                                                    mid(ends[0:1, :], NBLK), ALU.is_ge))
                steps.after(nc.vector.tensor_reduce(cntf[:, :], full[:, :].rearrange("p (n e) -> p n e", e=E8), AX.X, ALU.add))
                steps.after(nc.vector.tensor_scalar(table[:, :], cntf[:, :], float(E8 - 1), None, ALU.min))

            @block.tensor
            def _(pe):
                count_matmuls(nc, pe, m, t, pb, pt, asked, counted, 1)

            @block.gpsimd
            def _(pool):
                pool.wait_ge(m["zeros_stored1"], zeros_count(NBLK * P))
                pool.wait_ge(idx_ready, 1)
                scatter_rows(nc, pool, m, m["rows1"], NBLK * P, scattered)

    with ExitStack() as c:
        moe1_experts(nc, a, m, c, b1, b2, table)


def moe1_experts(nc, a, m, ctx, b1, b2, table):
    sb = lambda name, shape, dt=F32: m["sb"](name, shape, dt, ctx)
    sem = lambda name: m["sem"](name, ctx)
    ident, w1, w2 = m["ident"], m["w1"], m["w2"]
    XS = 4
    x = sb("ex", [P, XS, D])
    xT = sb("exT", [P, 2, DC, P])
    h = sb("eh", [P, 2, F1])
    sg = sb("esg", [P, 2, D])
    act_b = sb("eact", [P, 2, D])
    actT = sb("eactT", [P, 2, DC, P])
    o = sb("eo", [P, 2, D])
    psum = lambda name: [m["ps"](f"{name}{i}", [P, 512], ctx) for i in range(2)]
    x_ps, h_ps, t_ps, o_ps = psum("ex_ps"), psum("eh_ps"), psum("et_ps"), psum("eo_ps")
    x_used, xT_ready, h_done, h_out, glu_ready, sig_ready, act_ready, t_done, actT_ready, o_done, o_ready, dve = map(
        sem, ("x_used", "xT_ready", "h_done", "h_out", "glu_ready", "sig_ready", "act_ready", "et_done", "actT_ready", "eo_done", "o_ready", "e_dve"))
    x_loaded = [sem(f"x_loaded{q}") for q in range(XS)]
    o_stored = [sem(f"o_stored{p}") for p in range(2)]

    def middle_blocks(eng, step):
        for i in range(2, XS):
            step(i, i)
        with eng.Fori(1, NBLK // XS) as j:
            for q in range(XS):
                step(j * XS + q, q)
        for i in range(NBLK // XS * XS, NBLK - 1):
            step(i, i % XS)

    with nc.Block() as block:
        @block.sync
        def _(sp):
            def load(i, q):
                sp.wait_ge(x_used, i + 1)
                sp.dma_start(x[:, q, :], m["rows1"][bass.ds(i * P, P), :]).then_inc(x_loaded[q], 16)

            for i in range(XS):
                load(i, i)
            with sp.Fori(1, NBLK // XS) as j:
                for q in range(XS):
                    load(j * XS + q, q)
            for i in range(NBLK // XS * XS, NBLK):
                load(i, i % XS)

        @block.tensor
        def _(pe):
            pe.sem_inc(x_used, XS)
            pe.sem_inc(t_done, 2)
            pe.wait_ge(m["moe1_loaded"], 32)

            def turn_x(i, q):
                pe.wait_ge(x_loaded[q], (i - q) * (16 // XS) + 16)
                pe.wait_ge(xT_ready, i + 1)
                for c in range(DC):
                    mm = nc.tensor.transpose(x_ps[q % 2][:, c * P:(c + 1) * P], x[:, q, c * P:(c + 1) * P], ident[:, :])
                mm.then_inc(x_used, 1)

            def hidden(i, p):
                e = nc.tensor.value_load(table[0:1, bass.ds(i, 1)], min_val=0, max_val=E8 - 1)
                pe.wait_ge(xT_ready, i + 3)
                pe.wait_ge(h_out, i + 1)
                for c in range(DC):
                    mm = nc.tensor.matmul(h_ps[p][:, :], xT[:, p, c, :], w1[:, bass.ds(e, 1), c, :].rearrange("p a f -> p (a f)"),
                                          start=(c == 0), stop=(c == DC - 1))
                mm.then_inc(h_done, 1)

            def turn_act(i, p):
                pe.wait_ge(act_ready, i + 1)
                pe.wait_ge(actT_ready, i + 1)
                for c in range(DC):
                    mm = nc.tensor.transpose(t_ps[p][:, c * P:(c + 1) * P], act_b[:, p, c * P:(c + 1) * P], ident[:, :])
                mm.then_inc(t_done, 1)

            def output(i, p):
                e = nc.tensor.value_load(table[0:1, bass.ds(i, 1)], min_val=0, max_val=E8 - 1)
                pe.wait_ge(actT_ready, i + 3)
                pe.wait_ge(o_ready, i + 1)
                for c in range(DC):
                    mm = nc.tensor.matmul(o_ps[p][:, 0:D], actT[:, p, c, :], w2[:, bass.ds(e, 1), c, :].rearrange("p a f -> p (a f)"),
                                          start=(c == 0), stop=(c == DC - 1))
                mm.then_inc(o_done, 1)

            turn_x(0, 0)
            turn_x(1, 1)
            hidden(0, 0)
            turn_x(2, 2)
            hidden(1, 1)

            def step(i, q):
                turn_act(i - 2, q % 2)
                turn_x(i + 1, (q + 1) % XS)
                hidden(i, q % 2)
                output(i - 2, q % 2)

            middle_blocks(pe, step)
            i = NBLK - 1
            turn_act(i - 2, i % 2)
            hidden(i, i % 2)
            output(i - 2, i % 2)
            for i in (NBLK - 2, NBLK - 1):
                turn_act(i, i % 2)
                output(i, i % 2)

        @block.scalar
        def _(act):
            act.sem_inc(xT_ready, 2)
            act.sem_inc(actT_ready, 2)

            for p in range(2):
                act.sem_inc(o_stored[p], 16)

            def store(i, p):
                act.wait_ge(o_ready, i + 3)
                act.dma_start(m["outs1"][bass.ds(i * P, P), :], o[:, p, :]).then_inc(o_stored[p], 16)

            def turned_x(i, p):
                act.wait_ge(x_used, i + (1 + XS))
                act.wait_ge(h_done, i + 1)
                for c in range(DC):
                    ins = nc.scalar.activation(xT[:, p, c, :], x_ps[p][:, c * P:(c + 1) * P], ACT.Copy, scale=m["nw1"][:, c:c + 1])
                ins.then_inc(xT_ready, 1)

            def sigmoid(i, p):
                act.wait_ge(glu_ready, i + 1)
                nc.scalar.activation(sg[:, p, :], h[:, p, 0:D], ACT.Sigmoid, scale=1.702).then_inc(sig_ready, 1)

            def turned_act(i, p):
                act.wait_ge(t_done, i + 3)
                act.wait_ge(o_done, i + 1)
                nc.scalar.activation(actT[:, p, :, :], t_ps[p][:, 0:D], ACT.Copy).then_inc(actT_ready, 1)

            turned_x(0, 0)
            turned_x(1, 1)
            sigmoid(0, 0)
            turned_x(2, 0)
            sigmoid(1, 1)

            def step(i, q):
                turned_act(i - 2, q % 2)
                turned_x(i + 1, (q + 1) % 2)
                sigmoid(i, q % 2)
                if not (isinstance(i, int) and i < 3):
                    store(i - 3, (q + 1) % 2)

            middle_blocks(act, step)
            i = NBLK - 1
            turned_act(i - 2, i % 2)
            sigmoid(i, i % 2)
            store(i - 3, (i + 1) % 2)
            for i in (NBLK - 2, NBLK - 1):
                turned_act(i, i % 2)
                store(i - 1, (i + 1) % 2)
            store(NBLK - 1, (NBLK - 1) % 2)
            for p in range(2):
                act.wait_ge(o_stored[p], 16 * (NBLK // 2 + 1))

        @block.vector
        def _(v):
            v.sem_inc(h_out, 2)
            v.sem_inc(h_done, 2)
            v.sem_inc(o_done, 2)
            v.sem_inc(o_ready, 2)

            def swiglu(i, p):
                e = nc.vector.value_load(table[0:1, bass.ds(i, 1)], min_val=0, max_val=E8 - 1)
                v.wait_ge(h_done, i + 3)
                nc.vector.tensor_tensor(h[:, p, :], h_ps[p][:, :], b1[:, bass.ds(e, 1), :].rearrange("p a f -> p (a f)"), ALU.add).then_inc(h_out, 1)
                v.wait_ge(h_out, i + 3)
                nc.vector.tensor_scalar(h[:, p, 0:D], h[:, p, 0:D], 7.0, None, ALU.min).then_inc(glu_ready, 1)
                nc.vector.tensor_scalar(h[:, p, D:F1], h[:, p, D:F1], 7.0, -7.0, ALU.min, ALU.max).then_inc(dve, 1)
                v.wait_ge(sig_ready, i + 1)
                v.wait_ge(t_done, i + 1)
                nc.vector.tensor_tensor(sg[:, p, :], sg[:, p, :], h[:, p, 0:D], ALU.mult).then_inc(dve, 1)
                v.wait_ge(dve, i * 2 + 2)
                nc.vector.scalar_tensor_tensor(out=act_b[:, p, :], in0=h[:, p, D:F1], scalar=1.0, in1=sg[:, p, :], op0=ALU.add, op1=ALU.mult).then_inc(act_ready, 1)

            def finish(i, p):
                e = nc.vector.value_load(table[0:1, bass.ds(i, 1)], min_val=0, max_val=E8 - 1)
                v.wait_ge(o_done, i + 3)
                v.wait_ge(o_stored[p], (i - p) * 8 + 16)
                nc.vector.tensor_tensor(o[:, p, :], o_ps[p][:, 0:D], b2[:, bass.ds(e, 1), :].rearrange("p a f -> p (a f)"), ALU.add).then_inc(o_ready, 1)

            swiglu(0, 0)
            swiglu(1, 1)

            def step(i, q):
                swiglu(i, q % 2)
                finish(i - 2, q % 2)

            middle_blocks(v, step)
            step(NBLK - 1, (NBLK - 1) % XS)
            for i in (NBLK - 2, NBLK - 1):
                finish(i, i % 2)


def gather_rows(nc, pool, m, outs, nrows, got, loaded, used, slots):
    n = 0
    for i in range(T):
        for k in range(2):
            if n >= slots:
                pool.wait_ge(used, n - slots + 1)
            nc.gpsimd.indirect_dma_start(
                out=got[:, n % slots, :], out_offset=None, in_=outs[:, :],
                in_offset=bass.IndirectOffsetOnAxis(ap=m["gidx"][:, k, i:i + 1], axis=0),
                bounds_check=nrows - 1, oob_is_err=False).then_inc(loaded[n % slots], 16)
            n += 1


def attention(nc, a, out, m, ctx):
    sb = lambda name, shape: m["sb"](name, shape, F32, ctx)
    m["uT"] = sb("auT", [P, DC, NPAD])
    m["qT"], m["kT"] = sb("qT", [P, DC, NPAD]), sb("kT", [P, DC, NPAD])
    m["aw"] = sb("aw", [S, B, 2 * NH])
    m["ctxT"] = sb("ctxT", [P, DC, NPAD])
    for part in (combine1_and_project, windows, attention_core):
        with ExitStack() as c:
            part(nc, a, m, c)
    with ExitStack() as c:
        out_project(nc, m, c, m["ctxT"], DC, a["a_wo"])


def collect(nc, v, steps, m, tiles, got, loaded, used, stats, var_ready, into, first_alone):
    w, slots = m["w"], len(loaded)
    for i in tiles:
        for k in range(2):
            n = 2 * i + k
            v.wait_ge(loaded[n % slots], 16 * (n // slots + 1))
            if k:
                v.wait_ge(used, n)
            if first_alone and k == 0:
                ins = nc.vector.tensor_scalar(into[:, i, :], got[:, n % slots, :], w[:, 0, i:i + 1], None, ALU.mult)
            else:
                ins = nc.vector.scalar_tensor_tensor(out=into[:, i, :], in0=got[:, n % slots, :], scalar=w[:, k, i:i + 1], in1=into[:, i, :],
                                                     op0=ALU.mult, op1=ALU.add)
            ins.then_inc(used, 1)
        v.wait_ge(used, 2 * i + 2)
        nc.vector.bn_stats(m["st"][:, i, :], into[:, i, :]).then_inc(stats, 1)
    v.wait_ge(stats, tiles[-1] + 1)
    here = slice(tiles[0], tiles[-1] + 1)
    mean_and_var(nc, steps, m["st"][:, here, :], m["mean"][:, here], m["var"][:, here], m["tmp"][:, here])
    v.sem_inc(var_ready, 1)


def group_tiles(k):
    return range(k * GT, (k + 1) * GT)


def group_root(nc, act, m, k, var_ready, std_ready):
    here = slice(k * GT, (k + 1) * GT)
    act.wait_ge(var_ready, k + 1)
    nc.scalar.activation(m["std"][:, here], m["var"][:, here], ACT.Sqrt, bias=m["eps"][:, 0:1]).then_inc(std_ready, 1)


def combine1_and_project(nc, a, m, ctx):
    SL, US, QB = 6, 6, 6
    NQ = 4
    GN = GT * P
    sb = lambda name, shape: m["sb"](name, shape, F32, ctx)
    sem = lambda name: m["sem"](name, ctx)
    H, uT, ident = m["H"], m["uT"], m["ident"]
    got, u = sb("got", [P, SL, D]), sb("fu", [P, US, D])
    wq, wk, bq, bk = sb("wq", [P, DC, D]), sb("wk", [P, DC, D]), sb("bq", [P, DC]), sb("bk", [P, DC])
    ut = [m["ps"](f"fut{i}", [P, 512], ctx) for i in range(2)]
    ps = [m["ps"](f"qk_ps{i}", [P, 512], ctx) for i in range(QB)]
    loaded = [sem(f"g_loaded{i}") for i in range(SL)]
    used, stats, dve, var_ready, std_ready, u_ready, ut_done, ut_out, w_loaded, qk_done, qk_out, padded = map(
        sem, ("g_used", "fstats", "fdve", "fvar", "fstd", "fu_ready", "fut_done", "fut_out", "qk_loaded", "qk_done", "qk_out", "ct_padded"))
    with nc.Block() as block:
        @block.sync
        def _(sp):
            for t, k in ((wq, "a_wq"), (wk, "a_wk")):
                sp.dma_start(t[:, :, :], a[k]).then_inc(w_loaded, 16)
            for t, k in ((bq, "a_bq"), (bk, "a_bk")):
                sp.dma_start(t[:, :], a[k]).then_inc(w_loaded, 16)

        @block.gpsimd
        def _(pool):
            gather_rows(nc, pool, m, m["outs1"], NBLK * P, got, loaded, used, SL)
            nc.gpsimd.memset(m["ctxT"][:, :, N:NPAD], 0.0).then_inc(padded, 1)

        @block.vector
        def _(v):
            steps = Steps(v, dve)

            def norm(k):
                here = slice(k * GT, (k + 1) * GT)
                v.wait_ge(std_ready, k + 1)
                steps.after(nc.vector.reciprocal(m["rstd"][:, here], m["std"][:, here]))
                for i in group_tiles(k):
                    if i >= US:
                        v.wait_ge(ut_done, i - US + 1)
                    nc.vector.tensor_scalar(u[:, i % US, :], H[:, i, :], m["mean"][:, i:i + 1], m["rstd"][:, i:i + 1], ALU.subtract, ALU.mult).then_inc(u_ready, 1)

            for k in range(T // GT):
                collect(nc, v, steps, m, group_tiles(k), got, loaded, used, stats, var_ready, H, False)
                norm(k)

        @block.scalar
        def _(act):
            act.wait_ge(w_loaded, 64)

            def turned(k):
                for i in group_tiles(k):
                    act.wait_ge(ut_done, i + 1)
                    nc.scalar.activation(uT[:, :, i * P:(i + 1) * P], ut[i % 2][:, 0:D].rearrange("p (c q) -> p c q", q=P), ACT.Copy).then_inc(ut_out, 1)

            def projected(k):
                for n in range(NQ):
                    b, to, bias = k * NQ + n, (m["qT"], m["kT"])[n // DC], (bq, bk)[n // DC]
                    act.wait_ge(qk_done, b + 1)
                    nc.scalar.activation(to[:, n % DC, k * GN:(k + 1) * GN], ps[b % QB][:, 0:GN], ACT.Identity, bias=bias[:, n % DC:n % DC + 1]).then_inc(qk_out, 1)

            for k in range(T // GT):
                group_root(nc, act, m, k, var_ready, std_ready)
                turned(k)
                if k:
                    projected(k - 1)
            projected(T // GT - 1)

        @block.tensor
        def _(pe):
            pe.wait_ge(w_loaded, 64)
            for k in range(T // GT):
                for i in group_tiles(k):
                    pe.wait_ge(u_ready, i + 1)
                    if i >= 2:
                        pe.wait_ge(ut_out, i - 1)
                    for c in range(DC):
                        mm = nc.tensor.transpose(ut[i % 2][:, c * P:(c + 1) * P], u[:, i % US, c * P:(c + 1) * P], ident[:, :])
                    mm.then_inc(ut_done, 1)
                pe.wait_ge(ut_out, (k + 1) * GT)
                for n in range(NQ):
                    b, w = k * NQ + n, (wq, wk)[n // DC]
                    if b >= QB:
                        pe.wait_ge(qk_out, b - QB + 1)
                    for c in range(DC):
                        mm = nc.tensor.matmul(ps[b % QB][:, 0:GN], w[:, c, (n % DC) * P:(n % DC + 1) * P], uT[:, c, k * GN:(k + 1) * GN],
                                              start=(c == 0), stop=(c == DC - 1))
                    mm.then_inc(qk_done, 1)


def windows(nc, a, m, ctx):
    sb = lambda name, shape: m["sb"](name, shape, F32, ctx)
    sem = lambda name: m["sem"](name, ctx)
    qT, aw = m["qT"], m["aw"]
    wfq, wfg = sb("wfq", [P, DC, D]), sb("wfg", [P, DC, D])
    upz, bfq, bfg = sb("upz", [P, DC, 2 * NH]), sb("bfq", [P, DC]), sb("bfg", [P, DC])
    glo, gb = sb("glo", [P, DC, B]), sb("gbias", [P, DC, B])
    cT = sb("c_T", [P, 2, DC, G4])
    e = sb("epz", [S, 2, 4, 2 * NH])
    rp = sb("rp", [S, 2, 4, NH])
    bo = sb("bo", [P, D])
    bo_loaded, bo_added = sem("bo_loaded"), sem("bo_added")
    ROOT2 = 2.0 ** 0.5
    c_ps = [m["ps"](f"c_ps{i}", [P, 2, 512], ctx) for i in range(2)]
    pz_ps = [m["ps"](f"pz_ps{i}", [P, 2, 512], ctx) for i in range(2)]
    loaded, dve, glo_ready, g_done, c_done, c_in, c_ready, pz_done, e_ready, aw_ready = map(
        sem, ("w_loaded", "w_dve", "glo_ready", "g_done", "c_done", "c_in", "c_ready", "pz_done", "e_ready", "aw_ready"))
    with nc.Block() as block:
        @block.sync
        def _(sp):
            for t, k in ((wfq, "a_wfq"), (wfg, "a_wfg"), (upz, "a_upz")):
                sp.dma_start(t[:, :, :], a[k]).then_inc(loaded, 16)
            for t, k in ((bfq, "a_bfq"), (bfg, "a_bfg")):
                sp.dma_start(t[:, :], a[k]).then_inc(loaded, 16)
            sp.dma_start(bo[:, :], a["a_bo_row"].partition_broadcast(P)).then_inc(bo_loaded, 16)

        @block.gpsimd
        def _(pool):
            pool.wait_ge(bo_loaded, 16)
            nc.gpsimd.tensor_tensor(m["H"][:, :, :], m["H"][:, :, :], mid(bo[:, :], T), ALU.add).then_inc(bo_added, 1)

        @block.tensor
        def _(pe):
            pe.wait_ge(loaded, 80)
            pe.wait_ge(glo_ready, 1)
            for n in range(DC):
                for c in range(DC):
                    mm = nc.tensor.matmul(pz_ps[0][:, n, 0:B], wfg[:, c, n * P:(n + 1) * P], glo[:, c, :], start=(c == 0), stop=(c == DC - 1))
            mm.then_inc(g_done, 1)

            def c_args(i, p):
                pe.wait_ge(c_in, i + 1)
                for n in range(DC):
                    for c in range(DC):
                        mm = nc.tensor.matmul(c_ps[p][:, n, 0:G4], wfq[:, c, n * P:(n + 1) * P], qT[:, c, bass.ds(i * G4, G4)], start=(c == 0), stop=(c == DC - 1))
                mm.then_inc(c_done, 1)

            def pz(i, p):
                pe.wait_ge(c_ready, i + 1)
                pe.wait_ge(e_ready, i + 1)
                for k in range(4):
                    for c in range(DC):
                        mm = nc.tensor.matmul(pz_ps[p][0:S, 0, k * 2 * NH:(k + 1) * 2 * NH], cT[:, p, c, k * S:(k + 1) * S], upz[:, c, :], start=(c == 0), stop=(c == DC - 1))
                mm.then_inc(pz_done, 1)

            c_args(0, 0)
            with pe.Fori(0, NG // 2 - 1) as j:
                for p in range(2):
                    c_args(j * 2 + (p + 1), 1 - p)
                    pz(j * 2 + p, p)
            c_args(NG - 1, 1)
            pz(NG - 2, 0)
            pz(NG - 1, 1)

        @block.vector
        def _(v):
            steps = Steps(v, dve)
            v.sem_inc(c_in, 2)
            v.sem_inc(pz_done, 2)
            v.sem_inc(aw_ready, 2)
            for c in range(DC):
                ins = nc.vector.tensor_reduce(glo[:, c, :], qT[:, c, 0:N].rearrange("p (b s) -> p b s", s=S), AX.X, ALU.add)
            steps.after(ins)
            steps.after(nc.vector.tensor_scalar(glo[:, :, :], glo[:, :, :], 1.0 / S, None, ALU.mult))
            v.sem_inc(glo_ready, 1)
            v.wait_ge(loaded, 80)
            steps.after(nc.vector.tensor_tensor(bfq[:, :], bfq[:, :], bfg[:, :], ALU.add))
            v.wait_ge(g_done, 1)
            steps.after(nc.vector.tensor_tensor(gb[:, :, :], pz_ps[0][:, :, 0:B], last(bfq[:, :], B), ALU.add))
            v.sem_inc(e_ready, 2)
            base = steps.n

            def add_global(i, p):
                v.wait_ge(c_done, i + 1)
                v.wait_ge(pz_done, i + 1)
                g = gb[:, :, bass.ds(i * 4, 4)]
                for n in range(DC):
                    ins = nc.vector.tensor_tensor(cT[:, p, n, :].rearrange("p (b s) -> p b s", s=S), c_ps[p][:, n, 0:G4].rearrange("p (b s) -> p b s", s=S),
                                                  g[:, n, :].unsqueeze(2).broadcast_to([P, 4, S]), ALU.add)
                ins.then_inc(c_in, 1)

            def weights(i, p):
                v.wait_ge(e_ready, i + 3)
                ep, ez = e[:, p, :, 0:NH], e[:, p, :, NH:2 * NH]
                nc.vector.tensor_scalar(e[:, p, :, :], e[:, p, :, :], 1.0, None, ALU.add).then_inc(dve, 1)
                v.wait_ge(dve, i * 2 + (base + 1))
                nc.vector.reciprocal(rp[:, p, :, :], ep).then_inc(dve, 1)
                here = aw[0:S, bass.ds(i * 4, 4), :]
                nc.vector.tensor_scalar(here[:, :, 0:NH], ez, ROOT2 / S, None, ALU.mult)
                v.wait_ge(dve, i * 2 + (base + 2))
                nc.vector.scalar_tensor_tensor(out=here[:, :, NH:2 * NH], in0=ez, scalar=-ROOT2, in1=rp[:, p, :, :], op0=ALU.mult, op1=ALU.mult).then_inc(aw_ready, 1)

            add_global(0, 0)
            with v.Fori(0, NG // 2 - 1) as j:
                for p in range(2):
                    add_global(j * 2 + (p + 1), 1 - p)
                    weights(j * 2 + p, p)
            add_global(NG - 1, 1)
            weights(NG - 2, 0)
            weights(NG - 1, 1)

        @block.scalar
        def _(act):
            def tanh(i, p):
                act.wait_ge(c_in, i + 3)
                nc.scalar.activation(cT[:, p, :, :], cT[:, p, :, :], ACT.Tanh).then_inc(c_ready, 1)

            def exps(i, p):
                act.wait_ge(pz_done, i + 3)
                act.wait_ge(aw_ready, i + 1)
                nc.scalar.activation(e[:, p, :, :].rearrange("p k n -> p (k n)"), pz_ps[p][0:S, 0, 0:8 * NH], ACT.Exp, scale=-1.0).then_inc(e_ready, 1)

            tanh(0, 0)
            with act.Fori(0, NG // 2 - 1) as j:
                for p in range(2):
                    tanh(j * 2 + (p + 1), 1 - p)
                    exps(j * 2 + p, p)
            tanh(NG - 1, 1)
            exps(NG - 2, 0)
            exps(NG - 1, 1)


def attention_core(nc, a, m, ctx):
    sb = lambda name, shape: m["sb"](name, shape, F32, ctx)
    sem = lambda name: m["sem"](name, ctx)
    uT, qT, kT, aw, ctxT, ident = m["uT"], m["qT"], m["kT"], m["aw"], m["ctxT"], m["ident"]
    UH = 4
    UPB = NH // UH
    UC = UH * S
    CH = P // AD
    VW = AD + 1
    AHEAD = 3
    SQC = UPB + 1
    place, eo, bv, wv = sb("place", [S, S]), sb("head_of", [P, CH]), sb("bv", [S, D]), sb("wv", [P, DC, D])
    us, qs, ks, ws = sb("aus", [P, 2, DC, S]), sb("qs", [P, 2, DC, S]), sb("ks", [P, 2, DC, CH, S]), sb("ws", [S, 2, 2 * NH])
    vs = sb("vs", [P, 2, NH * VW])
    sq, ss, mx = sb("sq", [S, UPB, UC]), sb("ss", [P, UPB, UC]), sb("mx", [S, UPB, UH])
    pts, cx, rc = sb("pts", [P, 2, UC]), sb("cx", [S, 2, D]), sb("rc", [S, NH])
    s_ps = [m["ps"](f"s_ps{i}", [P, 512], ctx) for i in range(UPB)]
    p_ps = [m["ps"](f"p_ps{i}", [P, 512], ctx) for i in range(2)]
    v_ps, c_ps = m["ps"]("v_ps", [P, 512], ctx), m["ps"]("cx_ps", [P, 512], ctx)
    consts, ones_set, copied, k_ready, v_done, v_out, s_done, sq_ready, ss_ready, mx_ready, sh_ready, pr_ready, pt_done, pt_out, c_done, c_out, rc_ready, ct_done, ct_out = map(
        sem, ("at_consts", "ones_set", "copied", "k_ready", "v_done", "v_out", "s_done", "sq_ready", "ss_ready", "mx_ready", "sh_ready", "pr_ready",
              "pt_done", "pt_out", "cx_done", "cx_out", "rc_ready", "ct_done", "ct_out"))

    def heads(x):
        return x.rearrange("p (h s) -> p h s", s=S)

    def units(step):
        def run(eng):
            for u in range(UPB):
                step(u, u, 0, 0, True, B - 1)
            with eng.Fori(0, B // 2 - 2) as j:
                for r in range(2 * UPB):
                    k, u = r // UPB, r % UPB
                    step(j * (2 * UPB) + (UPB + r), u, j * 2 + (k + 1), 1 - k, False, 3)
            for b in range(B - 3, B):
                for u in range(UPB):
                    step(b * UPB + u, u, b, b % 2, False, B - 1 - b)
        return run

    with nc.Block() as block:
        @block.sync
        def _(sp):
            sp.dma_start(place[:, :], a["place"].partition_broadcast(S)).then_inc(consts, 16)
            sp.dma_start(eo[:, :], a["head_of"]).then_inc(consts, 16)
            sp.dma_start(bv[:, :], a["a_bv_row"].partition_broadcast(S)).then_inc(consts, 16)
            sp.dma_start(wv[:, :, :], a["a_wv"]).then_inc(consts, 16)
            store_zeros(sp, m, m["rows2"], m["zeros_stored2"])

        @block.tensor
        def _(pe):
            pe.sem_inc(s_done, 2 * UPB)
            pe.sem_inc(v_done, 2)
            pe.wait_ge(consts, 64)

            def values(b, q):
                pe.wait_ge(copied, b + 1)
                pe.wait_ge(ct_out, b + 1)
                for c in range(DC):
                    mm = nc.tensor.matmul(v_ps[0:S, 0:D], us[:, q, c, :], wv[:, c, :], start=(c == 0), stop=(c == DC - 1))
                mm.then_inc(v_done, 1)

            def scores(n, u, b, q):
                if u == 0:
                    pe.wait_ge(copied, b + 1)
                    pe.wait_ge(k_ready, b + 1)
                pe.wait_ge(ss_ready, n + 1)
                h = u % 2 * UH
                nc.tensor.matmul(s_ps[u][0:S, 0:UC], qs[:, q, u // 2, :],
                                 ks[:, q, u // 2, h:h + UH, :].rearrange("p a s -> p (a s)"), start=True, stop=True).then_inc(s_done, 1)

            def turn(n, u):
                pe.wait_ge(pr_ready, n + 1)
                pe.wait_ge(pt_out, n + 1)
                for h in range(UH):
                    mm = nc.tensor.transpose(p_ps[u % 2][0:S, h * S:(h + 1) * S], ss[0:S, u, h * S:(h + 1) * S], ident[0:S, 0:S])
                mm.then_inc(pt_done, 1)

            def context(n, u, b, q):
                if u == 0:
                    pe.wait_ge(v_out, b + 1)
                    pe.wait_ge(c_out, b + 1)
                pe.wait_ge(pt_out, n + 3)
                for h in range(UH):
                    g = u * UH + h
                    mm = nc.tensor.matmul(c_ps[0:S, g * VW:(g + 1) * VW], pts[:, u % 2, h * S:(h + 1) * S], vs[:, q, g * VW:(g + 1) * VW], start=True, stop=True)
                if u == UPB - 1:
                    mm.then_inc(c_done, 1)

            def turn_context(b, q, final=False):
                pe.wait_ge(c_out, b + 2)
                if not final:
                    pe.wait_ge(v_out, b + 2)
                pe.wait_ge(ct_out, b + 2)
                for c in range(DC):
                    mm = nc.tensor.transpose(v_ps[:, D + c * S:D + (c + 1) * S], cx[:, q, c * P:(c + 1) * P], ident[0:S, 0:S])
                mm.then_inc(ct_done, 1)

            values(0, 0)
            for u in range(AHEAD):
                scores(u, u, 0, 0)

            def step(n, u, b, q, first, left):
                u3 = (u + AHEAD) % UPB
                if u3 > u:
                    scores(n + AHEAD, u3, b, q)
                elif left:
                    scores(n + AHEAD, u3, b + 1, 1 - q)
                turn(n, u)
                if u > 0:
                    context(n - 1, u - 1, b, q)
                elif not first:
                    context(n - 1, UPB - 1, b - 1, 1 - q)
                if u == 1 and not first:
                    turn_context(b - 1, 1 - q)
                if u == UPB - 1 and left:
                    values(b + 1, 1 - q)

            units(step)(pe)
            context(B * UPB - 1, UPB - 1, B - 1, 1)
            turn_context(B - 1, 1, True)

        @block.scalar
        def _(act):
            act.sem_inc(sq_ready, SQC)
            act.sem_inc(ct_out, 2)
            act.wait_ge(consts, 64)

            def square(n, u, b, q):
                if u == 0:
                    act.wait_ge(copied, b + 1)
                act.wait_ge(ss_ready, n + 1)
                for h in range(UH):
                    g = u * UH + h
                    ins = nc.scalar.activation(sq[:, u, h * S:(h + 1) * S], place[:, :], ACT.Square, scale=ws[:, q, g:g + 1], bias=ws[:, q, NH + g:NH + g + 1])
                ins.then_inc(sq_ready, 1)

            def exp(n, u):
                act.wait_ge(sh_ready, n + 1)
                nc.scalar.activation(ss[0:S, u, :], ss[0:S, u, :], ACT.Exp).then_inc(pr_ready, 1)

            def context_out(b):
                act.wait_ge(ct_done, b + 1)
                nc.scalar.activation(cols(ctxT, b * S, S), v_ps[:, D:D + DC * S].rearrange("p (c s) -> p c s", s=S), ACT.Copy).then_inc(ct_out, 1)

            for u in range(UPB):
                square(u, u, 0, 0)
            exp(0, 0)

            def step(n, u, b, q, first, left):
                if left or u < UPB - 1:
                    exp(n + 1, (u + 1) % UPB)
                if left:
                    square(n + UPB, u, b + 1, 1 - q)
                if u == 2 and not first:
                    context_out(b - 1)

            units(step)(act)
            context_out(B - 1)

        @block.gpsimd
        def _(pool):
            def copies(b, q):
                pool.wait_ge(s_done, b * UPB + UPB)
                pool.wait_ge(v_done, b + 1)
                pool.wait_ge(sq_ready, b * UPB + 1)
                here = b * S
                nc.gpsimd.tensor_copy(us[:, q, :, :], cols(uT, here, S))
                nc.gpsimd.tensor_copy(qs[:, q, :, :], cols(qT, here, S))
                nc.gpsimd.tensor_copy(ws[:, q, :], tile_of(aw, b)[0:S, :]).then_inc(copied, 1)

            for b in range(2):
                copies(b, b)

            def step(n, u, b, q, first, left):
                pool.wait_ge(mx_ready, n + 1)
                nc.gpsimd.tensor_tensor(heads(ss[0:S, u, :]), heads(ss[0:S, u, :]), last(mx[:, u, :], S), ALU.subtract).then_inc(sh_ready, 1)
                if u == 2 and left >= 2:
                    copies(b + 2, q)

            units(step)(pool)

        @block.vector
        def _(v):
            v.sem_inc(ss_ready, UPB)
            v.sem_inc(pt_out, 2)
            v.sem_inc(c_out, 1)
            for t in (vs, ss, pts):
                nc.vector.memset(t[:, :, :], 0.0).then_inc(ones_set, 1)
            v.wait_ge(ones_set, 3)
            nc.vector.memset(vs[0:S, :, :], 1.0).then_inc(ones_set, 1)
            v.wait_ge(ones_set, 4)
            v.wait_ge(consts, 64)

            def keys(b, q):
                v.wait_ge(s_done, b * UPB + UPB)
                for e in range(CH):
                    ins = nc.vector.tensor_scalar(ks[:, q, :, e, :], cols(kT, b * S, S), eo[:, e:e + 1], 0.25, ALU.mult, ALU.mult)
                ins.then_inc(k_ready, 1)

            def values(b, q):
                v.wait_ge(v_done, b + 3)
                nc.vector.tensor_tensor(vs[0:S, q, :].rearrange("p (h w) -> p h w", w=VW)[:, :, 0:AD], v_ps[0:S, 0:D].rearrange("p (h w) -> p h w", w=AD),
                                        bv[:, :].rearrange("p (h w) -> p h w", w=AD), ALU.add).then_inc(v_out, 1)

            def scores(n, u):
                v.wait_ge(s_done, n + (1 + 2 * UPB))
                v.wait_ge(sq_ready, n + (1 + SQC))
                nc.vector.tensor_tensor(ss[0:S, u, :], s_ps[u][0:S, 0:UC], sq[:, u, :], ALU.subtract).then_inc(ss_ready, 1)
                v.wait_ge(ss_ready, n + (1 + UPB))
                nc.vector.tensor_reduce(mx[:, u, :], heads(ss[0:S, u, :]), AX.X, ALU.max).then_inc(mx_ready, 1)

            def turned(n, u):
                v.wait_ge(pt_done, n + 1)
                nc.vector.tensor_copy(pts[0:S, u % 2, :], p_ps[u % 2][0:S, 0:UC]).then_inc(pt_out, 1)

            def context(b, q):
                v.wait_ge(c_done, b + 1)
                c3 = c_ps[0:S, 0:NH * VW].rearrange("p (h w) -> p h w", w=VW)
                nc.vector.reciprocal(rc[:, :], c3[:, :, AD]).then_inc(rc_ready, 1)
                v.wait_ge(rc_ready, b + 1)
                nc.vector.tensor_tensor(cx[:, q, :].rearrange("p (h w) -> p h w", w=AD), c3[:, :, 0:AD], last(rc[:, :], AD), ALU.mult).then_inc(c_out, 1)

            for b in range(2):
                keys(b, b)
            values(0, 0)
            for u in range(AHEAD):
                scores(u, u)

            def step(n, u, b, q, first, left):
                if left or u == 0:
                    scores(n + AHEAD, (u + AHEAD) % UPB)
                turned(n, u)
                if u == 0 and not first:
                    context(b - 1, 1 - q)
                if u == 2 and left >= 2:
                    keys(b + 2, q)
                if u == UPB - 1 and left:
                    values(b + 1, 1 - q)

            units(step)(v)
            context(B - 1, 1)


def moe2(nc, a, out, m, ctx):
    sb = lambda name, shape, dt=F32: m["sb"](name, shape, dt, ctx)
    m["R"] = m["A"]
    w1, w2 = sb("x_w1", [P, 2, DC, HID]), sb("x_w2", [P, 2, MC, D])
    m["ln_g"], m["ln_b"] = sb("lng", [P, D]), sb("lnb", [P, D])
    w_loaded = [m["sem"](f"xw_loaded{p}", ctx) for p in range(2)]
    with ExitStack() as c:
        route_front(nc, a, m, c, False, None, a["r_gw"], a["r_gb"])
    with ExitStack() as c:
        capacity_routing(nc, a, m, c, w1, w2, w_loaded)
    with ExitStack() as c:
        moe2_experts(nc, a, m, c, w1, w2, w_loaded)
    with ExitStack() as c:
        combine2(nc, a, out, m, c)


def load_expert(sp, a, w1, w2, w_loaded, e, p):
    sp.dma_start(w1[:, p, :, :], a["x_w1"][bass.ds(e, 1)].rearrange("o p c n -> (o p) c n")).then_inc(w_loaded[p], 16)
    sp.dma_start(w2[:, p, :, :], a["x_w2"][bass.ds(e, 1)].rearrange("o p c n -> (o p) c n")).then_inc(w_loaded[p], 16)


def capacity_routing(nc, a, m, ctx, w1, w2, w_loaded):
    csb = lambda name, shape, dt=F32: m["sb"](name, shape, dt, ctx)
    t = routing_tensors(m, ctx)
    C3 = 3
    wt, hit, hits, cnt = csb("wt", [P, ET]), csb("hit", [P, ET]), csb("hits", [P, C3, ET]), csb("cnt", [P, C3, E8], BF16)
    thr, cand, bits = csb("thr", [P, E8], U32), csb("cand", [P, C3, E8], U32), csb("bits", [P, C3, E8], U32)
    best = csb("best", [P, C3 + 1, E8])
    room, taken = csb("room", [P, E8]), csb("taken", [P, 2, T])
    pb, pt, pc = (m["ps"](n, [P, 512], ctx) for n in ("ps_before", "ps_total", "ps_count"))
    dve, asked, counted, idx_ready, scattered, cnt_ready, cnt_done, srch = (m["sem"](n, ctx) for n in (
        "rt_dve", "asked", "counted", "idx_ready", "scattered", "cnt_ready", "cnt_done", "search"))
    ROUNDS = 15
    PER = 5
    with nc.Block() as block:
        @block.sync
        def _(sp):
            for e in range(2):
                load_expert(sp, a, w1, w2, w_loaded, e, e)

        @block.scalar
        def _(act):
            act.wait_ge(t["gap_ready"], 1)
            nc.scalar.activation(m["w"][:, 1, :], m["w"][:, 1, :], ACT.Exp).then_inc(t["exp_ready"], 1)

        @block.tensor
        def _(pe):
            with pe.Fori(0, ROUNDS) as i:
                pe.wait_ge(cnt_ready, i + 1)
                nc.tensor.matmul(pc[:, 0:C3 * E8], m["ones_bf"][:, :], cnt[:, :, :].rearrange("p c e -> p (c e)"), start=True, stop=True).then_inc(cnt_done, 1)
            for n in range(3):
                count_matmuls(nc, pe, m, t, pb, pt, asked, counted, n + 1)

        @block.vector
        def _(v):
            steps = Steps(v, dve)
            top2(nc, v, steps, m, t)
            w, oh = m["w"], t["oh"]
            steps.after(nc.vector.tensor_tensor(by_tile(wt[:, :]), by_tile(oh[:, 0, :]), mid(w[:, 0, :], E8), ALU.mult))
            steps.after(nc.vector.tensor_tensor(by_tile(hit[:, :]), by_tile(oh[:, 1, :]), mid(w[:, 1, :], E8), ALU.mult))
            steps.after(nc.vector.tensor_tensor(wt[:, :], wt[:, :], hit[:, :], ALU.add))
            steps.after(nc.vector.memset(thr[:, :].bitcast(F32), 0.0))
            for c in range(C3):
                steps.after(nc.vector.memset(bits[:, c, :].bitcast(F32), (2.0 ** -95, 2.0 ** -63, 2.0 ** -31)[c]))
            steps.after(nc.vector.memset(best[:, C3, :], 0.0))
            with v.Fori(0, ROUNDS) as i:
                nc.vector.tensor_tensor(cand[:, :, :], mid(thr[:, :], C3), bits[:, :, :], ALU.bitwise_or).then_inc(srch, 1)
                v.wait_ge(srch, i * PER + 1)
                nc.vector.tensor_tensor(hits[:, :, :].rearrange("p c (e t) -> p c e t", t=T), by_tile(wt[:, :]).unsqueeze(1).broadcast_to([P, C3, E8, T]),
                                        cand[:, :, :].bitcast(F32).unsqueeze(3).broadcast_to([P, C3, E8, T]), ALU.is_ge).then_inc(srch, 1)
                nc.vector.tensor_scalar(bits[:, :, :], bits[:, :, :], 2, None, ALU.logical_shift_right)
                v.wait_ge(srch, i * PER + 2)
                with nc.allow_low_precision(reason="counts up to 18 are exact in bfloat16"):
                    nc.vector.tensor_reduce(cnt[:, :, :], hits[:, :, :].rearrange("p c (e t) -> p c e t", t=T), AX.X, ALU.add).then_inc(cnt_ready, 1)
                v.wait_ge(cnt_done, i + 1)
                nc.vector.scalar_tensor_tensor(out=best[:, 0:C3, :], in0=pc[:, 0:C3 * E8].rearrange("p (c e) -> p c e", e=E8), scalar=float(CAP),
                                               in1=cand[:, :, :].bitcast(F32), op0=ALU.is_ge, op1=ALU.mult).then_inc(srch, 1)
                v.wait_ge(srch, i * PER + 3)
                nc.vector.tensor_reduce(thr[:, :].bitcast(F32), best[:, :, :].rearrange("p c e -> p e c"), AX.X, ALU.max).then_inc(srch, 1)
                v.wait_ge(srch, i * PER + 4)
                nc.vector.tensor_copy(best[:, C3, :], thr[:, :].bitcast(F32)).then_inc(srch, 1)
                v.wait_ge(srch, i * PER + 5)
            limit = last(thr[:, :].bitcast(F32), T)
            steps.after(nc.vector.tensor_tensor(by_tile(t["chosen"][:, :]), by_tile(wt[:, :]), limit, ALU.is_gt))
            positions(nc, v, steps, m, t, t["chosen"][:, :], pb, pt, asked, counted, 1)
            steps.after(nc.vector.tensor_scalar(room[:, :], by_tile(t["incl"][:, :])[:, :, T - 1], -1.0, float(CAP), ALU.mult, ALU.add))
            steps.after(nc.vector.tensor_tensor(by_tile(hit[:, :]), by_tile(wt[:, :]), limit, ALU.is_equal))
            steps.after(nc.vector.scalar_tensor_tensor(out=hit[:, :], in0=wt[:, :], scalar=0.0, in1=hit[:, :], op0=ALU.is_gt, op1=ALU.mult))
            positions(nc, v, steps, m, t, hit[:, :], pb, pt, asked, counted, 2)
            steps.after(nc.vector.tensor_tensor(by_tile(t["pos"][:, :]), by_tile(t["pos"][:, :]), last(room[:, :], T), ALU.is_lt))
            steps.after(nc.vector.tensor_tensor(hit[:, :], hit[:, :], t["pos"][:, :], ALU.mult))
            steps.after(nc.vector.tensor_tensor(t["chosen"][:, :], t["chosen"][:, :], hit[:, :], ALU.add))
            positions(nc, v, steps, m, t, t["chosen"][:, :], pb, pt, asked, counted, 3)
            steps.after(nc.vector.scalar_tensor_tensor(out=by_tile(t["pos"][:, :]), in0=last(m["iota8"][:, :], T), scalar=float(ROWS),
                                                       in1=by_tile(t["pos"][:, :]), op0=ALU.mult, op1=ALU.add))
            for k in range(2):
                steps.after(nc.vector.tensor_tensor(oh[:, k, :], oh[:, k, :], t["chosen"][:, :], ALU.mult))
                steps.after(nc.vector.tensor_reduce(taken[:, k, :], oh[:, k, :].rearrange("p (e t) -> p t e", t=T), AX.X, ALU.add))
            steps.after(nc.vector.tensor_tensor(w[:, :, :], w[:, :, :], taken[:, :, :], ALU.mult))
            row_indices(nc, steps, m, t, [taken[:, 0, :], taken[:, 1, :]])
            v.sem_inc(idx_ready, 1)

        @block.gpsimd
        def _(pool):
            pool.wait_ge(m["zeros_stored2"], zeros_count(E8 * ROWS))
            pool.wait_ge(idx_ready, 1)
            scatter_rows(nc, pool, m, m["rows2"], E8 * ROWS, scattered)


def moe2_experts(nc, a, m, ctx, w1, w2, w_loaded):
    sb = lambda name, shape, dt=F32: m["sb"](name, shape, dt, ctx)
    sem = lambda name: m["sem"](name, ctx)
    ident = m["ident"]
    b1, b2 = sb("x_b1", [P, E8, MC]), sb("x_b2", [P, E8, DC])
    x = sb("xx", [XQ, 2, XG, D])
    xT = sb("xxT", [P, 2, DC, ROWS])
    hT = sb("xhT", [P, MC, ROWS])
    oT = sb("xoT", [P, DC, ROWS])
    r = sb("xr", [XQ, 2, XG, D])
    pair = lambda name: [m["ps"](f"{name}{i}", [P, 512], ctx) for i in range(2)]
    x_ps, h_ps, o_ps, r_ps = pair("xx_ps"), pair("xh_ps"), pair("xo_ps"), pair("xr_ps")
    biases, x_turned, xT_out, h_done, h_out, o_done, o_out, r_done, r_out = map(
        sem, ("x_biases", "x_turned", "xT_out", "xh_done", "xh_out", "xo_done", "xo_out", "xr_done", "xr_out"))
    x_loaded = [sem(f"xx_loaded{p}") for p in range(2)]
    stored = [sem(f"xr_stored{p}") for p in range(2)]
    ln_loaded, h_plus_b = sem("ln_loaded"), sem("h_plus_b")

    def rows(dram, e):
        return dram[bass.ds(e * ROWS, ROWS), :].rearrange("(g q) d -> q g d", q=XQ)

    def for_experts(eng, step):
        step(0, 0, True, False)
        with eng.Fori(0, E8 // 2 - 1) as j:
            for p in range(2):
                step(j * 2 + (p + 1), 1 - p, False, False)
        step(E8 - 1, 1, False, True)

    with nc.Block() as block:
        @block.sync
        def _(sp):
            sp.dma_start(b1[:, :, :], a["x_b1"]).then_inc(biases, 16)
            sp.dma_start(b2[:, :, :], a["x_b2"]).then_inc(biases, 16)
            sp.dma_start(m["ln_b"][:, :], a["ln_b"].partition_broadcast(P)).then_inc(ln_loaded, 16)
            sp.dma_start(m["ln_g"][:, :], a["ln_g"].partition_broadcast(P)).then_inc(ln_loaded, 16)
            for p in range(2):
                sp.sem_inc(stored[p], 16)

            def load_x(e, p):
                sp.wait_ge(x_turned, e + 1)
                sp.dma_start(x[:, p, :, :], rows(m["rows2"], e)).then_inc(x_loaded[p], 16)

            def step(e, p, first, final):
                if not final:
                    if not first:
                        sp.wait_ge(o_done, e + 1)
                        load_expert(sp, a, w1, w2, w_loaded, e + 1, 1 - p)
                    load_x(e + 1, 1 - p)
                if not first:
                    sp.wait_ge(r_out, e + 1)
                    sp.dma_start(rows(m["outs2"], e - 1), r[:, 1 - p, :, :]).then_inc(stored[1 - p], 16)

            load_x(0, 0)
            for_experts(sp, step)
            sp.wait_ge(r_out, E8 + 1)
            sp.dma_start(rows(m["outs2"], E8 - 1), r[:, 1, :, :]).then_inc(stored[1], 16)
            for p in range(2):
                sp.wait_ge(stored[p], 16 * (E8 // 2 + 1))

        @block.gpsimd
        def _(pool):
            pool.wait_ge(ln_loaded, 32)
            nc.gpsimd.tensor_tensor(m["H"][:, :, :], m["H"][:, :, :], mid(m["ln_b"][:, :], T), ALU.add).then_inc(h_plus_b, 1)

        @block.tensor
        def _(pe):
            pe.sem_inc(x_turned, 2)

            def turn_x(e, p):
                pe.wait_ge(x_loaded[p], (e - p) * 8 + 16)
                for c in range(DC):
                    for g in range(XG):
                        mm = nc.tensor.transpose(x_ps[c][:, g * XQ:(g + 1) * XQ], x[:, p, g, c * P:(c + 1) * P], ident[0:XQ, 0:XQ])
                mm.then_inc(x_turned, 1)

            def turn_out(e, p):
                pe.wait_ge(o_out, e + 2)
                pe.wait_ge(r_out, e + 1)
                for g in range(XG):
                    for c in range(DC):
                        o = (g % 2) * D + c * P
                        mm = nc.tensor.transpose(r_ps[g // 2][0:XQ, o:o + P], oT[:, c, g * XQ:(g + 1) * XQ], ident[:, :])
                mm.then_inc(r_done, 1)

            def step(e, p, first, final):
                pe.wait_ge(w_loaded[p], (e - p) * 16 + 32)
                pe.wait_ge(xT_out, e + 1)
                for k in range(MC):
                    pe.wait_ge(h_out, e * MC + (k + 1))
                    for c in range(DC):
                        mm = nc.tensor.matmul(h_ps[k % 2][:, 0:ROWS], w1[:, p, c, k * P:(k + 1) * P], xT[:, p, c, :], start=(c == 0), stop=(c == DC - 1))
                    mm.then_inc(h_done, 1)
                if not first:
                    turn_out(e - 1, 1 - p)
                if not final:
                    turn_x(e + 1, 1 - p)
                pe.wait_ge(o_out, e + 1)
                for o in range(DC):
                    for k in range(MC):
                        if o == 0:
                            pe.wait_ge(h_out, e * MC + (k + 3))
                        mm = nc.tensor.matmul(o_ps[o][:, 0:ROWS], w2[:, p, k, o * P:(o + 1) * P], hT[:, k, :], start=(k == 0), stop=(k == MC - 1))
                mm.then_inc(o_done, 1)

            turn_x(0, 0)
            for_experts(pe, step)
            turn_out(E8 - 1, 1)

        @block.scalar
        def _(act):
            act.sem_inc(h_out, 2)
            act.sem_inc(o_done, 1)
            act.wait_ge(biases, 32)

            def turned(e, p):
                act.wait_ge(x_turned, e + 3)
                for c in range(DC):
                    ins = nc.scalar.activation(xT[:, p, c, :], x_ps[c][:, 0:ROWS], ACT.Copy)
                ins.then_inc(xT_out, 1)

            def step(e, p, first, final):
                for k in range(MC):
                    act.wait_ge(h_done, e * MC + (k + 1))
                    if k == 0:
                        act.wait_ge(o_done, e + 1)
                    nc.scalar.activation(hT[:, k, :], h_ps[k % 2][:, 0:ROWS], ACT.Gelu, bias=b1[:, bass.ds(e, 1), k]).then_inc(h_out, 1)
                if not final:
                    turned(e + 1, 1 - p)

            turned(0, 0)
            for_experts(act, step)

        @block.vector
        def _(v):
            v.sem_inc(o_out, 1)
            v.sem_inc(r_out, 1)
            v.sem_inc(r_done, 1)
            v.wait_ge(biases, 32)

            def turned_out(e, p):
                v.wait_ge(r_done, e + 2)
                v.wait_ge(stored[p], (e - p) * 8 + 16)
                for g in range(2):
                    ins = nc.vector.tensor_copy(r[:, p, 2 * g:2 * g + 2, :], r_ps[g][0:XQ, 0:2 * D].rearrange("p (g d) -> p g d", d=D))
                ins.then_inc(r_out, 1)

            def step(e, p, first, final):
                if not first:
                    turned_out(e - 1, 1 - p)
                v.wait_ge(o_done, e + 2)
                v.wait_ge(r_done, e + 1)
                for o in range(DC):
                    ins = nc.vector.tensor_scalar(oT[:, o, :], o_ps[o][:, 0:ROWS], b2[:, bass.ds(e, 1), o], None, ALU.add)
                ins.then_inc(o_out, 1)

            for_experts(v, step)
            turned_out(E8 - 1, 1)


def combine2(nc, a, out, m, ctx):
    SL = 6
    sb = lambda name, shape: m["sb"](name, shape, F32, ctx)
    sem = lambda name: m["sem"](name, ctx)
    H, A, g = m["H"], m["A"], m["ln_g"]
    got = sb("got", [P, SL, D])
    loaded = [sem(f"g_loaded{i}") for i in range(SL)]
    used, stats, dve, var_ready, std_ready, scaled, fin, stored = map(
        sem, ("g_used", "cstats", "cdve", "cvar", "cstd", "scaled", "fin", "out_stored"))
    rows = out.rearrange("b s d -> (b s) d")
    with nc.Block() as block:
        @block.sync
        def _(sp):
            with sp.Fori(0, T - 1) as i:
                sp.wait_ge(fin, i + 1)
                sp.dma_start(rows[bass.ds(i * P, P), :], tile_of(A, i)).then_inc(stored, 16)
            sp.wait_ge(fin, T)
            sp.dma_start(rows[(T - 1) * P:N, :], A[0:LAST, T - 1, :]).then_inc(stored, 16)
            sp.wait_ge(stored, 16 * T)

        @block.gpsimd
        def _(pool):
            gather_rows(nc, pool, m, m["outs2"], E8 * ROWS, got, loaded, used, SL)

        @block.scalar
        def _(act):
            for k in range(T // GT):
                group_root(nc, act, m, k, var_ready, std_ready)

        @block.vector
        def _(v):
            steps = Steps(v, dve)

            def norm(k):
                here = slice(k * GT, (k + 1) * GT)
                v.wait_ge(std_ready, k + 1)
                steps.after(nc.vector.reciprocal(m["rstd"][:, here], m["std"][:, here]))
                for i in range(k * GT, (k + 1) * GT):
                    nc.vector.scalar_tensor_tensor(out=A[:, i, :], in0=A[:, i, :], scalar=m["mean"][:, i:i + 1], in1=g[:, :],
                                                   op0=ALU.subtract, op1=ALU.mult).then_inc(scaled, 1)
                for i in range(k * GT, (k + 1) * GT):
                    v.wait_ge(scaled, i + 1)
                    nc.vector.scalar_tensor_tensor(out=A[:, i, :], in0=A[:, i, :], scalar=m["rstd"][:, i:i + 1], in1=H[:, i, :],
                                                   op0=ALU.mult, op1=ALU.add).then_inc(fin, 1)

            for k in range(T // GT):
                collect(nc, v, steps, m, group_tiles(k), got, loaded, used, stats, var_ready, A, True)
                if k:
                    norm(k - 1)
            norm(T // GT - 1)


def _laid_out(x):
    import numpy as np

    def chunks(w):
        c = w.shape[0] // P
        return w.reshape(c, P, -1).transpose(1, 0, 2)

    def column(v):
        return v.reshape(-1, P).T

    r = {k: np.asarray(v) for k, v in x.items()}
    o = {}
    px = r["x"].reshape(B, 3, 6, 16, 6, 16).transpose(1, 3, 5, 2, 4, 0).reshape(KC, P, PT, P)
    o["patches"] = px.transpose(2, 1, 0, 3)
    o["patch_w"] = chunks(r["L0_tok_W"].T)
    o["patch_b"] = r["L0_tok_b"]
    o["cls"] = r["L0_tok_class_token"].reshape(D)
    o["pos"] = r["L0_tok_pos_embedding"].reshape(1 + NPATCH, D)
    o["txt"] = r["txt"]
    o["m_gamma"], o["m_beta"] = column(r["L0_attn_ln_gamma"]), column(r["L0_attn_ln_beta"])
    o["m_win"] = chunks(r["L0_attn_W_in"])
    bi = r["L0_attn_b_in"]
    o["m_bz"] = column(bi[0:INNER])
    o["m_bx"] = bi[INNER:2 * INNER]
    o["m_bb"] = bi[2 * INNER:2 * INNER + NST].reshape(NST, 1)
    o["m_bc"] = bi[2 * INNER + NST:2 * INNER + 2 * NST].reshape(NST, 1)
    o["m_bdt"] = bi[2 * INNER + 2 * NST:].reshape(HM, 1)
    o["m_dtb"] = r["L0_attn_dt_bias"].reshape(HM, 1)
    o["m_alog"] = r["L0_attn_A_log"].reshape(HM, 1)
    o["m_d"] = r["L0_attn_D_skip"]
    o["m_wout"] = chunks(r["L0_attn_W_out"])
    o["m_bout"] = r["L0_attn_b_out"]
    o["f_norm"] = column(r["L0_ffn_norm_w"])
    o["f_gw"] = chunks(r["L0_ffn_gate_w"].T)
    o["f_gb"] = r["L0_ffn_gate_b"]
    w1 = r["L0_ffn_mlp1_w"].reshape(E8, 256, 2, DC, P)
    o["moe1_w1"] = w1.transpose(4, 0, 3, 2, 1).reshape(P, E8, DC, F1)
    o["moe1_b1"] = r["L0_ffn_mlp1_b"].reshape(E8, 256, 2).transpose(0, 2, 1).reshape(E8 * F1)
    o["moe1_w2"] = r["L0_ffn_mlp2_w"].reshape(E8, D, DC, P).transpose(3, 0, 2, 1)
    o["moe1_b2"] = r["L0_ffn_mlp2_b"].reshape(E8 * D)
    for k in ("q", "k", "v", "o", "fq", "fg"):
        o["a_w" + k] = chunks(r["L1_attn_w" + k])
        o["a_b" + k] = column(r["L1_attn_b" + k])
    o["a_bv_row"], o["a_bo_row"] = r["L1_attn_bv"], r["L1_attn_bo"]
    u = np.zeros((2, NH, AD, NH), r["L1_attn_up"].dtype)
    for i, k in enumerate(("up", "uz")):
        for h in range(NH):
            u[i, h, :, h] = r["L1_attn_" + k][h, 0]
    o["a_upz"] = chunks(np.concatenate((u[0].reshape(D, NH), u[1].reshape(D, NH)), axis=1))
    o["r_gw"] = chunks(r["L1_ffn_router_w"])
    o["r_gb"] = r["L1_ffn_router_b"]
    o["x_w1"] = r["L1_ffn_w1"].reshape(E8, DC, P, HID).transpose(0, 2, 1, 3)
    o["x_w2"] = r["L1_ffn_w2"].reshape(E8, MC, P, D).transpose(0, 2, 1, 3)
    o["x_b1"] = r["L1_ffn_b1"].reshape(E8, MC, P).transpose(2, 0, 1)
    o["x_b2"] = r["L1_ffn_b2"].reshape(E8, DC, P).transpose(2, 0, 1)
    o["ln_g"], o["ln_b"] = r["L1_ffn_ln_g"], r["L1_ffn_ln_b"]
    f = np.float32
    n = np.arange(P)
    o["ident"] = np.eye(P, dtype=f)
    bf16_one = 0x3F80
    o["before"] = np.where(n[:, None] < n[None, :], bf16_one, 0).astype(np.uint16)
    o["ones_bf"] = np.full((P, P), bf16_one, np.uint16)
    o["place"] = np.arange(S, dtype=f)
    keep = np.ones((P, E8, T), f)
    keep[:, :, 0] = 0.0
    o["keep"] = keep.reshape(P, ET)
    o["iota8"] = np.tile(np.arange(E8, dtype=f), (P, 1))
    o["iota_blk"] = np.repeat(np.arange(NBLK, dtype=f), E8).reshape(1, NBLK * E8)
    valid = np.ones((P, T), f)
    valid[LAST:, T - 1] = 0.0
    o["valid"] = valid
    o["head_of"] = ((n // AD)[:, None] == np.arange(P // AD)[None, :]).astype(f)
    return {k: np.ascontiguousarray(v) for k, v in o.items()}


def kernel(**inputs):
    import numpy as _np
    import concourse.bacc as _bacc
    from concourse import mybir as _mybir
    from concourse.bass_utils import run_bass_kernel_spmd as _run

    nc = _bacc.Bacc("TRN2", target_bir_lowering=False, num_devices=1)
    arrays, args = {}, {}
    for name, v in _laid_out(inputs).items():
        arrays[f"in_{name}"] = v
        args[name] = nc.dram_tensor(f"in_{name}", v.shape, _mybir.dt.from_np(v.dtype), kind="ExternalInput").ap()
    out = nc.dram_tensor("out_0", (B, S, D), F32, kind="ExternalOutput").ap()
    build(nc, args, out)
    r = _run(nc, [arrays], core_ids=[0])
    return r.results[0]["out_0"]
```

```python
from contextlib import ExitStack

import concourse.bass as bass
from concourse import mybir

ALU = mybir.AluOpType
ACT = mybir.ActivationFunctionType
AX = mybir.AxisListType
F32 = mybir.dt.float32
BF16 = mybir.dt.bfloat16
U32 = mybir.dt.uint32
I32 = mybir.dt.int32

P = 128
B, NPATCH, NTXT = 32, 36, 32
S = 1 + NPATCH + NTXT
N = B * S
T = -(-N // P)
NPAD = T * P
LAST = N - (T - 1) * P
D = 256
DC = D // P
KP = 768
KC = KP // P
PT = B * NPATCH // P
POS = P // B
HM, HD, NST = 8, 64, 64
INNER = HM * HD
IC = INNER // P
PROJ = 2 * INNER + 2 * NST + HM
HS = HM * S
G4 = 4 * S
NG = N // G4
E8 = 8
ET = E8 * T
F1 = 512
NBLK = (2 * N + E8 * (P - 1)) // P
NH, AD = 16, 16
AS = NH * S
HID = 1024
MC = HID // P
CAP = max(int(N * 1.5 / E8), 2)
XG, XQ = 4, 104
ROWS = XG * XQ
GT = 3
ZC = 4
LN_EPS = 1e-5
RMS_EPS = 1.1920928955078125e-07
FAR = 1.0e6


def tile_of(x, i, n=1):
    return x[:, bass.ds(i, n), :].rearrange("p a b -> p (a b)")


def cols(x, start, n):
    return x[:, :, bass.ds(start, n)]


def bc(ap, shape):
    return ap.broadcast_to(shape)


def mid(ap2, n):
    p, k = ap2.shape
    return ap2.unsqueeze(1).broadcast_to([p, n, k])


def last(ap2, n):
    p, k = ap2.shape
    return ap2.unsqueeze(2).broadcast_to([p, k, n])


class Steps:

    def __init__(self, eng, sem):
        self.eng, self.sem, self.n = eng, sem, 0

    def after(self, ins):
        self.n += 1
        ins.then_inc(self.sem, 1)
        self.eng.wait_ge(self.sem, self.n)


def mean_and_var(nc, steps, st, mean, var, tmp):
    me, ve, mo, vo = st[:, :, 1], st[:, :, 2], st[:, :, 4], st[:, :, 5]
    steps.after(nc.vector.tensor_tensor(mean, me, mo, ALU.add))
    steps.after(nc.vector.tensor_scalar(mean, mean, 0.5, None, ALU.mult))
    steps.after(nc.vector.tensor_tensor(tmp, me, mo, ALU.subtract))
    steps.after(nc.vector.tensor_tensor(var, ve, vo, ALU.add))
    steps.after(nc.vector.scalar_tensor_tensor(out=tmp, in0=tmp, scalar=0.25, in1=tmp, op0=ALU.mult, op1=ALU.mult))
    steps.after(nc.vector.scalar_tensor_tensor(out=var, in0=var, scalar=1.0 / D, in1=tmp, op0=ALU.mult, op1=ALU.add))


def build(nc, a, out):
    with ExitStack() as top:
        named = {}

        def unique(name):
            named[name] = named.get(name, 0) + 1
            return name if named[name] == 1 else f"{name}_{named[name]}"

        def sb(name, shape, dt=F32, ctx=top):
            return ctx.enter_context(nc.sbuf_tensor(unique(name), shape, dt))

        phase_sems = []

        def sem(name, ctx=None):
            handle = nc.alloc_semaphore(name=unique(name))
            if ctx is not None:
                phase_sems.append(handle)
            return handle

        def scratch(name, shape):
            return nc.dram_tensor(name, shape, F32, kind="Internal").ap()

        m = {}
        m["sb"], m["sem"] = sb, sem
        m["ps"] = lambda name, shape, ctx, dt=F32: ctx.enter_context(nc.psum_tensor(unique(name), shape, dt))
        m["tokens"] = scratch("tokens", (N, D))
        m["bcast"] = scratch("bcast", (B, 2, HM, S))
        m["rows1"] = scratch("rows1", (NBLK * P, D))
        m["outs1"] = scratch("outs1", (NBLK * P, D))
        m["rows2"] = scratch("rows2", (E8 * ROWS, D))
        m["outs2"] = scratch("outs2", (E8 * ROWS, D))
        m["H"] = sb("H", [P, T, D])
        m["A"] = sb("A", [P, T, D])
        m["R"] = m["A"]
        m["ident"] = sb("ident", [P, P])
        m["st"] = sb("st", [P, T, 6])
        for name in ("mean", "var", "rstd", "tmp", "std", "var2", "rstd2", "std2"):
            m[name] = sb(name, [P, T])
        m["eps"] = sb("eps", [P, 2])
        for name, shape, dt in (("before", [P, P], BF16), ("ones_bf", [P, P], BF16), ("keep", [P, ET], F32), ("iota8", [P, E8], F32), ("valid", [P, T], F32)):
            m[name] = sb(name, shape, dt)
        m["lg"], m["w"] = sb("lg", [P, T, E8]), sb("w", [P, 2, T])
        m["gidx"], m["sidx"] = sb("gidx", [P, 2, T], U32), sb("sidx", [P, 2, T], U32)
        m["w1"] = sb("moe1_w1", [P, E8, DC, F1])
        m["w2"] = sb("moe1_w2", [P, E8, DC, D])
        m["moe1_loaded"] = sem("moe1_loaded")
        m["zero"] = sb("zero", [P, ZC, D])
        m["zeros_stored1"], m["zeros_stored2"] = sem("zeros_stored1"), sem("zeros_stored2")
        for phase in (embed, mamba, moe1, attention, moe2):
            with ExitStack() as ctx:
                phase(nc, a, out, m, ctx)
            nc.clear_and_free_semaphores(phase_sems)
            nc.all_engine_barrier()
            phase_sems.clear()


def store_zeros(sp, m, rows, stored):
    r = rows.rearrange("(n p) d -> p n d", p=P)
    for c in range(0, r.shape[1], ZC):
        k = min(ZC, r.shape[1] - c)
        sp.dma_start(r[:, c:c + k, :], m["zero"][:, 0:k, :]).then_inc(stored, 16)


def zeros_count(nrows):
    return 16 * -(-(nrows // P) // ZC)


def embed(nc, a, out, m, ctx):
    sb = lambda name, shape, dt=F32: m["sb"](name, shape, dt, ctx)
    sem = lambda name: m["sem"](name, ctx)
    tokens, H, A = m["tokens"], m["H"], m["A"]
    rows = tokens.rearrange("(b s) d -> b s d", s=S)
    w = sb("patch_w", [P, KC, D])
    patches = sb("patches", [P, 3, KC, P])
    pos = sb("pos", [P, PT, D])
    bias = sb("patch_b", [P, D])
    cls = sb("cls", [B, 2, D])
    emb = sb("emb", [P, 3, D])
    zero = m["zero"]
    acc = [m["ps"](f"patch_acc{i}", [P, 512], ctx) for i in range(3)]
    w_loaded, consts, patches_free = map(sem, ("pw_loaded", "pc_loaded", "p_free"))
    patches_loaded = [sem(f"patches_loaded{p}") for p in range(3)]
    emb_stored = [sem(f"emb_stored{p}") for p in range(3)]
    pos_ready, acc_ready = map(sem, ("pos_ready", "acc_ready"))
    cls_ready, direct, zeroed, h_loaded, pad_ready = map(
        sem, ("cls_ready", "direct", "zeroed", "h_loaded", "pad_ready"))

    with nc.Block() as block:
        @block.sync
        def _(sp):
            sp.dma_start(w[:, :, :], a["patch_w"]).then_inc(w_loaded, 16)
            sp.dma_start(bias[:, :], a["patch_b"].partition_broadcast(P)).then_inc(consts, 16)
            for q in range(POS):
                src = a["pos"][1:, :].rearrange("(t q) d -> q t d", q=POS)[q]
                sp.dma_start(pos[q * B:(q + 1) * B, :, :], src.partition_broadcast(B)).then_inc(consts, 16)
            sp.dma_start(cls[:, 0, :], a["cls"].partition_broadcast(B)).then_inc(consts, 16)
            sp.dma_start(cls[:, 1, :], a["pos"][0].partition_broadcast(B)).then_inc(consts, 16)
            with sp.Fori(0, PT // 3) as j:
                for p in range(3):
                    sp.wait_ge(patches_free, j * 3 + (p + 1))
                    sp.dma_start(patches[:, p, :, :], a["patches"][bass.ds(j * 3 + p, 1)].rearrange("o p c q -> (o p) c q")).then_inc(patches_loaded[p], 16)
            for name in ("ident", "keep", "iota8", "valid"):
                sp.dma_start(m[name][:, :], a[name]).then_inc(h_loaded, 16)
            for name in ("before", "ones_bf"):
                sp.dma_start(m[name][:, :].bitcast(mybir.dt.uint16), a[name]).then_inc(h_loaded, 16)
            sp.dma_start(rows[:, 1 + NPATCH:, :], a["txt"]).then_inc(direct, 16)
            sp.wait_ge(cls_ready, 1)
            sp.dma_start(rows[:, 0, :], cls[:, 0, :]).then_inc(direct, 16)
            sp.wait_ge(direct, 32)
            for p in range(3):
                sp.wait_ge(emb_stored[p], 16 * POS * (PT // 3 + 1))
            sp.wait_ge(pad_ready, 1)
            full = (T - 1) * P
            sp.dma_start(H[:, 0:T - 1, :], tokens[0:full, :].rearrange("(t p) d -> p t d", p=P)).then_inc(h_loaded, 16)
            sp.dma_start(H[0:LAST, T - 1, :], tokens[full:N, :]).then_inc(h_loaded, 16)
            sp.dma_start(m["w1"][:, :, :, :], a["moe1_w1"]).then_inc(m["moe1_loaded"], 16)
            sp.dma_start(m["w2"][:, :, :, :], a["moe1_w2"]).then_inc(m["moe1_loaded"], 16)
            sp.wait_ge(h_loaded, 16 * 8)
            sp.wait_ge(zeroed, 1)

        @block.gpsimd
        def _(pool):
            nc.gpsimd.memset(zero[:, :, :], 0.0).then_inc(zeroed, 1)
            nc.gpsimd.memset(H[:, T - 1, :], 0.0).then_inc(pad_ready, 1)
            nc.gpsimd.memset(m["eps"][:, 0:1], LN_EPS)
            nc.gpsimd.memset(m["eps"][:, 1:2], RMS_EPS)

        @block.tensor
        def _(pe):
            pe.sem_inc(patches_free, 3)
            pe.wait_ge(w_loaded, 16)
            with pe.Fori(0, PT // 3) as j:
                for p in range(3):
                    pe.wait_ge(patches_loaded[p], j * 16 + 16)
                    pe.wait_ge(acc_ready, j * 3 + (p + 1))
                    for c in range(KC):
                        mm = nc.tensor.matmul(acc[p][:, 0:D], patches[:, p, c, :], w[:, c, :], start=(c == 0), stop=(c == KC - 1))
                    mm.then_inc(patches_free, 1)

        @block.vector
        def _(v):
            v.sem_inc(acc_ready, 3)
            v.wait_ge(consts, 16 * (3 + POS))
            nc.vector.tensor_tensor(cls[:, 0, :], cls[:, 0, :], cls[:, 1, :], ALU.add).then_inc(cls_ready, 1)
            nc.vector.tensor_tensor(pos[:, :, :], pos[:, :, :], mid(bias[:, :], PT), ALU.add).then_inc(pos_ready, 1)
            v.wait_ge(pos_ready, 1)
            with v.Fori(0, PT // 3) as j:
                for p in range(3):
                    v.wait_ge(patches_free, j * 3 + (p + 4))
                    v.wait_ge(emb_stored[p], j * (16 * POS) + 16 * POS)
                    nc.vector.tensor_tensor(emb[:, p, :], acc[p][:, 0:D], tile_of(pos, j * 3 + p), ALU.add).then_inc(acc_ready, 1)

        @block.scalar
        def _(act):
            for p in range(3):
                act.sem_inc(emb_stored[p], 16 * POS)
            with act.Fori(0, PT // 3) as j:
                for p in range(3):
                    act.wait_ge(acc_ready, j * 3 + (p + 4))
                    for q in range(POS):
                        dst = rows[:, bass.ds((j * 3 + p) * POS + (1 + q), 1), :].rearrange("b o d -> b (o d)")
                        act.dma_start(dst, emb[q * B:(q + 1) * B, p, :]).then_inc(emb_stored[p], 16)


def layer_stats(nc, v, steps, m, x, sem_name_done):
    with v.Fori(0, T // 3) as j:
        for p in range(3):
            nc.vector.bn_stats(m["st"][:, bass.ds(j * 3 + p, 1), :], x[:, bass.ds(j * 3 + p, 1), :]).then_inc(sem_name_done, 1)
    v.wait_ge(sem_name_done, T)


def both_norms(nc, m, tiles, second_eps):
    return nc.vector.tensor_scalar(m["var2"][:, tiles], m["var"][:, tiles], 1.0 + second_eps, LN_EPS * second_eps, ALU.mult, ALU.add)


def group_tiles(k):
    return range(k * GT, (k + 1) * GT)


def group_root(nc, act, m, k, var_ready, std_ready, second=False):
    here = slice(k * GT, (k + 1) * GT)
    act.wait_ge(var_ready, k + 1)
    ins = nc.scalar.activation(m["std"][:, here], m["var"][:, here], ACT.Sqrt, bias=m["eps"][:, 0:1])
    if second:
        ins = nc.scalar.activation(m["std2"][:, here], m["var2"][:, here], ACT.Sqrt)
    ins.then_inc(std_ready, 1)


def normalise(nc, dst, src, m, i, rstd="rstd"):
    return nc.vector.tensor_scalar(dst, src, m["mean"][:, bass.ds(i, 1)], m[rstd][:, bass.ds(i, 1)], ALU.subtract, ALU.mult)


NP = 3


def add_normed(nc, pool, m, normed, added):
    n = T // NP
    for c in range(NP):
        pool.wait_ge(normed, n * (c + 1))
        nc.gpsimd.tensor_tensor(m["H"][:, c * n:(c + 1) * n, :], m["H"][:, c * n:(c + 1) * n, :], m["A"][:, c * n:(c + 1) * n, :], ALU.add).then_inc(added, 1)


def pre_mamba(nc, a, out, m, ctx):
    sem = lambda name: m["sem"](name, ctx)
    H, A, uT, ident = m["H"], m["A"], m["uT"], m["ident"]
    gamma = m["sb"]("m_gamma", [P, DC], F32, ctx)
    beta = m["sb"]("m_beta", [P, DC], F32, ctx)
    u = m["sb"]("u", [P, 2, D], F32, ctx)
    ut = [m["ps"](f"ut{i}", [P, DC, P], ctx) for i in range(2)]
    stats1, var_ready, std_ready, dve, norm_ready, u_ready, ut_ready, ut_free, consts, summed = map(
        sem, ("stats1", "var_ready", "std_ready", "dve", "norm_ready", "u_ready", "ut_ready", "ut_free", "gb", "summed"))

    with nc.Block() as block:
        @block.sync
        def _(sp):
            sp.dma_start(gamma[:, :], a["m_gamma"]).then_inc(consts, 16)
            sp.dma_start(beta[:, :], a["m_beta"]).then_inc(consts, 16)

        @block.vector
        def _(v):
            steps = Steps(v, dve)
            layer_stats(nc, v, steps, m, H, stats1)
            mean_and_var(nc, steps, m["st"], m["mean"][:, :], m["var"][:, :], m["tmp"][:, :])
            steps.after(both_norms(nc, m, slice(0, T), LN_EPS))
            v.sem_inc(var_ready, 1)
            v.wait_ge(std_ready, 1)
            nc.vector.reciprocal(m["rstd2"][:, :], m["std2"][:, :])
            steps.after(nc.vector.reciprocal(m["rstd"][:, :], m["std"][:, :]))
            with v.Fori(0, T // 2) as j:
                for p in range(2):
                    v.wait_ge(ut_ready, j * 2 + (p + 1))
                    normalise(nc, u[:, p, :], tile_of(H, j * 2 + p), m, j * 2 + p, "rstd2").then_inc(u_ready, 1)
                    normalise(nc, tile_of(A, j * 2 + p), tile_of(H, j * 2 + p), m, j * 2 + p).then_inc(norm_ready, 1)

        @block.gpsimd
        def _(pool):
            add_normed(nc, pool, m, norm_ready, summed)

        @block.scalar
        def _(act):
            act.wait_ge(var_ready, 1)
            nc.scalar.activation(m["std"][:, :], m["var"][:, :], ACT.Sqrt, bias=m["eps"][:, 0:1])
            nc.scalar.activation(m["std2"][:, :], m["var2"][:, :], ACT.Sqrt).then_inc(std_ready, 1)
            act.wait_ge(consts, 32)
            act.sem_inc(ut_free, 2)
            with act.Fori(0, T // 2) as j:
                for p in range(2):
                    act.wait_ge(ut_ready, j * 2 + (p + 3))
                    for c in range(DC):
                        ins = nc.scalar.activation(uT[:, c, bass.ds((j * 2 + p) * P, P)], ut[p][:, c, :], ACT.Identity,
                                                   bias=beta[:, c:c + 1], scale=gamma[:, c:c + 1])
                    ins.then_inc(ut_free, 1)

        @block.tensor
        def _(pe):
            pe.sem_inc(ut_ready, 2)
            with pe.Fori(0, T // 2) as j:
                for p in range(2):
                    pe.wait_ge(u_ready, j * 2 + (p + 1))
                    pe.wait_ge(ut_free, j * 2 + (p + 1))
                    for c in range(DC):
                        ins = nc.tensor.transpose(ut[p][:, c, :], u[:, p, c * P:(c + 1) * P], ident[:, :])
                    ins.then_inc(ut_ready, 1)


def mamba(nc, a, out, m, ctx):
    sb = lambda name, shape: m["sb"](name, shape, F32, ctx)
    m["uT"] = sb("uT", [P, DC + 1, NPAD])
    pre_ctx = ExitStack()
    with pre_ctx:
        pre_mamba(nc, a, out, m, pre_ctx)
    m["cT"] = sb("cT", [NST, NPAD])
    m["gate"] = sb("gate", [P, IC, NPAD])
    m["win"] = sb("win", [P, DC, PROJ])
    for part in (mamba_project, mamba_core, mamba_out):
        with ExitStack() as c:
            part(nc, a, out, m, c)


def mamba_project(nc, a, out, m, ctx):
    sb = lambda name, shape: m["sb"](name, shape, F32, ctx)
    sem = lambda name: m["sem"](name, ctx)
    uT, cT, gate, win = m["uT"], m["cT"], m["gate"], m["win"]
    bz, bb, bcc = sb("bz", [P, IC]), sb("bb", [NST, 1]), sb("bcc", [NST, 1])
    bdt, dtb, alog = sb("bdt", [HM, 1]), sb("dtb", [HM, 1]), sb("alog", [HM, 1])
    dt, low, dec = sb("dt", [HM, N]), sb("low", [HM, N]), sb("dec", [HM, N])
    loaded, dve, dt_free, dt_done, bc_done, psum_free, dt_raw, soft, decayed, stored, z_done, z_free, padded, prep = map(
        sem, ("pj_loaded", "pj_dve", "dt_free", "dt_done", "bc_done", "bc_free", "dt_raw", "soft", "decayed", "dt_stored", "z_done", "z_free", "padded", "prep"))
    OB, OC, ODT = 2 * INNER, 2 * INNER + NST, 2 * INNER + 2 * NST

    bout, bout_loaded = sb("m_bout", [P, D]), sem("bout_loaded")

    with ExitStack() as c1:
        acc = [[m["ps"](f"acc_{k}{i}", [P, 512], c1) for i in range(2)] for k in ("dt", "b", "c")]
        with nc.Block() as block:
            @block.sync
            def _(sp):
                sp.dma_start(win[:, :, :], a["m_win"]).then_inc(loaded, 16)
                for t, k in ((bz, "m_bz"), (bb, "m_bb"), (bcc, "m_bc"), (bdt, "m_bdt"), (dtb, "m_dtb"), (alog, "m_alog")):
                    sp.dma_start(t[:, :], a[k]).then_inc(loaded, 16)
                sp.dma_start(bout[:, :], a["m_bout"].partition_broadcast(P)).then_inc(bout_loaded, 16)
                sp.wait_ge(loaded, 7 * 16)
                store_zeros(sp, m, m["rows1"], m["zeros_stored1"])

            @block.gpsimd
            def _(pool):
                nc.gpsimd.memset(uT[NST:P, DC, :], 0.0).then_inc(padded, 1)
                pool.wait_ge(padded, 1)
                nc.gpsimd.memset(gate[:, :, N:NPAD], 0.0).then_inc(padded, 1)
                pool.wait_ge(bout_loaded, 16)
                pool.wait_ge(padded, 2)
                nc.gpsimd.tensor_tensor(m["H"][:, :, :], m["H"][:, :, :], mid(bout[:, :], T), ALU.add).then_inc(padded, 1)

            @block.tensor
            def _(pe):
                pe.wait_ge(loaded, 7 * 16)

                def project(i, p, parts, free, done):
                    pe.wait_ge(free, i + 1)
                    for k, o, n in parts:
                        for c in range(DC):
                            mm = nc.tensor.matmul(acc[k][p][0:n, 0:G4], win[:, c, o:o + n], uT[:, c, bass.ds(i * G4, G4)],
                                                  start=(c == 0), stop=(c == DC - 1))
                    mm.then_inc(done, 1)

                with pe.Fori(0, NG // 2) as j:
                    for p in range(2):
                        project(j * 2 + p, p, ((0, ODT, HM),), dt_free, dt_done)
                with pe.Fori(0, NG // 2) as j:
                    for p in range(2):
                        project(j * 2 + p, p, ((1, OB, NST), (2, OC, NST)), psum_free, bc_done)

            @block.vector
            def _(v):
                steps = Steps(v, dve)
                v.sem_inc(psum_free, 2)
                v.sem_inc(dt_free, 2)
                v.wait_ge(loaded, 7 * 16)
                steps.after(nc.vector.tensor_tensor(bdt[:, :], bdt[:, :], dtb[:, :], ALU.add))
                with v.Fori(0, NG // 2) as j:
                    for p in range(2):
                        v.wait_ge(dt_done, j * 2 + (p + 1))
                        nc.vector.tensor_scalar(dt[:, bass.ds((j * 2 + p) * G4, G4)], acc[0][p][0:HM, 0:G4], bdt[:, 0:1], None, ALU.add).then_inc(dt_free, 1)
                v.wait_ge(dt_free, NG + 2)

                def bc_out(lo, hi):
                    with v.Fori(lo // 2, hi // 2) as j:
                        for p in range(2):
                            v.wait_ge(bc_done, j * 2 + (p + 1))
                            here = bass.ds((j * 2 + p) * G4, G4)
                            nc.vector.tensor_scalar(uT[0:NST, DC, here], acc[1][p][0:NST, 0:G4], bb[:, 0:1], None, ALU.add)
                            nc.vector.tensor_scalar(cT[:, here], acc[2][p][0:NST, 0:G4], bcc[:, 0:1], None, ALU.add).then_inc(psum_free, 1)

                nc.vector.tensor_scalar(low[:, :], dt[:, :], -1.0, None, ALU.mult).then_inc(dt_raw, 1)
                v.wait_ge(dt_raw, 1)
                nc.vector.tensor_tensor(low[:, :], low[:, :], dt[:, :], ALU.min).then_inc(dt_raw, 1)
                bc_out(0, NG // 2)
                v.wait_ge(soft, 2)
                nc.vector.scalar_tensor_tensor(out=dt[:, :], in0=dt[:, :], scalar=0.0, in1=low[:, :], op0=ALU.max, op1=ALU.add).then_inc(dt_raw, 1)
                bc_out(NG // 2, NG)
                v.wait_ge(decayed, 2)
                nc.vector.memset(dec[:, :].rearrange("h (b s) -> h b s", s=S)[:, :, 0:1], 0.0).then_inc(dt_raw, 1)

            @block.scalar
            def _(act):
                act.wait_ge(dt_raw, 2)
                nc.scalar.activation(low[:, :], low[:, :], ACT.Exp).then_inc(soft, 1)
                act.wait_ge(soft, 1)
                nc.scalar.activation(low[:, :], low[:, :], ACT.Ln, bias=1.0).then_inc(soft, 1)
                nc.scalar.activation(alog[:, :], alog[:, :], ACT.Exp).then_inc(decayed, 1)
                act.wait_ge(decayed, 1)
                act.wait_ge(dt_raw, 3)
                nc.scalar.activation(dec[:, :], dt[:, :], ACT.Copy, scale=alog[:, 0:1]).then_inc(prep, 1)
                act.wait_ge(prep, 1)
                nc.scalar.activation(dec[:, :], dec[:, :], ACT.Exp, scale=-1.0).then_inc(decayed, 1)

    zacc = [[m["ps"](f"zacc{i}{k}", [P, 512], ctx) for k in range(IC)] for i in range(2)]
    rows = m["bcast"]
    with nc.Block() as block:
        @block.scalar
        def _(act):
            act.sem_inc(z_free, 2)
            with act.Fori(0, NG // 2) as j:
                for p in range(2):
                    act.wait_ge(z_done, j * 2 + (p + 1))
                    for k in range(IC):
                        ins = nc.scalar.activation(gate[:, k, bass.ds((j * 2 + p) * G4, G4)], zacc[p][k][:, 0:G4], ACT.Silu, bias=bz[:, k:k + 1])
                    ins.then_inc(z_free, 1)

        @block.sync
        def _(sp):
            sp.dma_start(rows[:, 0].rearrange("b h s -> h b s"), dec[:, :].rearrange("h (b s) -> h b s", s=S)).then_inc(stored, 16)
            sp.dma_start(rows[:, 1].rearrange("b h s -> h b s"), dt[:, :].rearrange("h (b s) -> h b s", s=S)).then_inc(stored, 16)
            sp.wait_ge(stored, 32)

        @block.tensor
        def _(pe):
            with pe.Fori(0, NG // 2) as j:
                for p in range(2):
                    pe.wait_ge(z_free, j * 2 + (p + 1))
                    for k in range(IC):
                        for c in range(DC):
                            mm = nc.tensor.matmul(zacc[p][k][:, 0:G4], win[:, c, k * P:(k + 1) * P], uT[:, c, bass.ds((j * 2 + p) * G4, G4)],
                                                  start=(c == 0), stop=(c == DC - 1))
                    mm.then_inc(z_done, 1)


def mamba_core(nc, a, out, m, ctx):
    sb = lambda name, shape: m["sb"](name, shape, F32, ctx)
    sem = lambda name: m["sem"](name, ctx)
    uT, cT, gate, win, ident = m["uT"], m["cT"], m["gate"], m["win"], m["ident"]
    KB = 80
    RS = 4
    us = sb("us", [P, 2, DC + 1, S])
    rows = m["A"][0:KB, :, :].rearrange("p t d -> p (t d)")[:, 0:RS * 2 * HS].rearrange("p (q k x) -> p q k x", q=RS, k=2)
    xs = sb("xs", [S, RS, INNER])
    inj = sb("inj", [S, 2, HS])
    sc = sb("sc", [S, RS, HS])
    bx = sb("bx", [S, INNER])
    dd = sb("dd", [S, HM])
    dI = sb("dI", [S, HS])
    x_ps = [m["ps"](f"x_ps{i}", [P, 512], ctx) for i in range(2)]
    g_ps = [m["ps"](f"g_ps{i}", [P, 512], ctx) for i in range(2)]
    y_ps = [m["ps"](f"y_ps{i}", [P, IC, P], ctx) for i in range(2)]
    consts, d_ready, us_ready, xg_done, x_ready, inj_ready, scanned, mult, m_ready, y_done, y_out = map(
        sem, ("mc_consts", "d_ready", "us_ready", "xg_done", "x_ready", "inj_ready", "scanned", "mult", "m_ready", "y_done", "y_out"))
    rows_loaded = [sem(f"rows_loaded{q}") for q in range(RS)]

    def batches(eng, step):
        with eng.Fori(0, B // RS - 1) as j:
            for q in range(RS):
                step(j * RS + q, q, True)
        for i in range(B - RS, B):
            step(i, i % RS, i + 2 < B)

    def v3(x):
        return x.rearrange("p (h s) -> p h s", s=S)

    with nc.Block() as block:
        @block.sync
        def _(sp):
            sp.dma_start(bx[:, :], a["m_bx"].partition_broadcast(S)).then_inc(consts, 16)
            sp.dma_start(dd[:, :], a["m_d"].partition_broadcast(S)).then_inc(consts, 16)
            with sp.Fori(0, B // RS) as j:
                for q in range(RS):
                    sp.wait_ge(scanned, j * RS + (q + 1))
                    sp.dma_start(rows[:, q, :, :], m["bcast"][bass.ds(j * RS + q, 1)].rearrange("o k h s -> (o k) (h s)").partition_broadcast(KB)).then_inc(rows_loaded[q], 16)

        @block.scalar
        def _(act):
            with act.Fori(0, B // 2) as j:
                for p in range(2):
                    act.wait_ge(xg_done, j * 2 + (p + 1))
                    nc.scalar.activation(us[:, p, :, :], cols(uT, (j * 2 + p) * S, S), ACT.Copy).then_inc(us_ready, 1)

        @block.gpsimd
        def _(pool):
            pool.wait_ge(consts, 32)
            nc.gpsimd.tensor_tensor(v3(dI[:, :]), mid(ident[0:S, 0:S], HM), last(dd[:, :], S), ALU.mult).then_inc(d_ready, 1)

            def inject(i, q):
                pool.wait_ge(rows_loaded[q], (i - q) * (16 // RS) + 16)
                pool.wait_ge(scanned, i + 3)
                nc.gpsimd.tensor_tensor(v3(inj[:, q % 2, :]), mid(ident[0:S, 0:S], HM), v3(rows[0:S, q, 1, :]), ALU.mult).then_inc(inj_ready, 1)

            def skip(i, q):
                pool.wait_ge(mult, i + 3)
                nc.gpsimd.tensor_tensor(sc[:, q, :], sc[:, q, :], dI[:, :], ALU.add).then_inc(m_ready, 1)

            inject(0, 0)
            inject(1, 1)
            pool.wait_ge(d_ready, 1)

            def step(i, q, more):
                if more:
                    inject(i + 2, (q + 2) % RS)
                skip(i, q)

            batches(pool, step)

        @block.tensor
        def _(pe):
            pe.sem_inc(xg_done, 2)

            def front(i, p):
                pe.wait_ge(us_ready, i + 1)
                pe.wait_ge(x_ready, i + 1)
                for c in range(DC):
                    nc.tensor.matmul(x_ps[p][0:S, 0:INNER], us[:, p, c, :], win[:, c, INNER:2 * INNER], start=(c == 0), stop=(c == DC - 1))
                pe.wait_ge(mult, i + 1)
                nc.tensor.matmul(g_ps[p][0:S, 0:S], us[0:NST, p, DC, :], cT[:, bass.ds(i * S, S)], start=True, stop=True).then_inc(xg_done, 1)

            def back(i, q):
                p = q % 2
                pe.wait_ge(m_ready, i + 1)
                pe.wait_ge(y_out, i + 1)
                for h in range(HM):
                    o = (h % 2) * HD
                    mm = nc.tensor.matmul(y_ps[p][o:o + HD, h // 2, 0:S], xs[:, q, h * HD:(h + 1) * HD], sc[:, q, h * S:(h + 1) * S], start=True, stop=True)
                mm.then_inc(y_done, 1)

            front(0, 0)
            front(1, 1)

            def step(i, q, more):
                if more:
                    front(i + 2, q % 2)
                back(i, q)

            batches(pe, step)

        @block.vector
        def _(v):
            v.sem_inc(x_ready, 2)
            v.sem_inc(scanned, RS)
            v.sem_inc(mult, 2)
            v.sem_inc(y_done, RS)
            v.sem_inc(y_out, 2)
            v.wait_ge(consts, 32)

            def front(i, q):
                p = q % 2
                v.wait_ge(xg_done, i + 3)
                v.wait_ge(y_done, i + 1)
                nc.vector.tensor_tensor(xs[:, q, :], x_ps[p][0:S, 0:INNER], bx[:, :], ALU.add).then_inc(x_ready, 1)
                v.wait_ge(inj_ready, i + 1)
                nc.vector.tensor_tensor_scan(sc[:, q, :], rows[0:S, q, 0, :], inj[:, p, :], 0.0, ALU.mult, ALU.add).then_inc(scanned, 1)
                v.wait_ge(scanned, i + (1 + RS))
                nc.vector.tensor_tensor(v3(sc[:, q, :]), v3(sc[:, q, :]), mid(g_ps[p][0:S, 0:S], HM), ALU.mult).then_inc(mult, 1)

            def back(i, p):
                v.wait_ge(y_done, i + (1 + RS))
                g = cols(gate, i * S, S)
                nc.vector.tensor_tensor(g, y_ps[p][:, :, 0:S], g, ALU.mult).then_inc(y_out, 1)

            front(0, 0)
            front(1, 1)

            def step(i, q, more):
                if more:
                    front(i + 2, (q + 2) % RS)
                back(i, q % 2)

            batches(v, step)


def mamba_out(nc, a, out, m, ctx):
    project_and_route(nc, m, ctx, m["gate"], IC, a["m_wout"], True, a["f_norm"], a["f_gw"], a["f_gb"])


def project_and_route(nc, m, ctx, src, chunks, w_dram, rms, norm, gw_dram, gb_dram):
    OB = 3
    sb = lambda name, shape, dt=F32: m["sb"](name, shape, dt, ctx)
    sem = lambda name: m["sem"](name, ctx)
    H, R, ident, lg = m["H"], m["R"], m["ident"], m["lg"]
    w, gw, gb, nw = sb("w_out", [P, chunks, D]), sb("gw", [P, DC, E8]), sb("gb", [P, E8]), sb("nw", [P, DC])
    xT = sb("rxT", [P, 2, DC, P])
    o_ps = [m["ps"](f"o_ps{i}", [P, 512], ctx) for i in range(OB)]
    t_ps = [m["ps"](f"rt_ps{i}", [P, DC, P], ctx) for i in range(2)]
    l_ps = m["ps"]("rl_ps", [P, 512], ctx)
    w_loaded, loaded, o_done, added, stats, dve, var_ready, std_ready, r_ready, t_done, t_out, l_done, factors_ready = map(
        sem, ("wo_loaded", "rf_loaded", "o_done", "added", "rstats", "rdve", "rvar", "rstd_", "r_ready", "rt_done", "rt_out", "rl_done", "factors_ready"))
    LOADS = 16 * (2 if norm is None else 3)
    with nc.Block() as block:
        @block.sync
        def _(sp):
            sp.dma_start(w[:, :, :], w_dram).then_inc(w_loaded, 16)
            sp.dma_start(gw[:, :, :], gw_dram).then_inc(loaded, 16)
            sp.dma_start(gb[:, :], gb_dram.partition_broadcast(P)).then_inc(loaded, 16)
            if norm is not None:
                sp.dma_start(nw[:, :], norm).then_inc(loaded, 16)

        @block.tensor
        def _(pe):
            pe.wait_ge(w_loaded, 16)

            def project(i):
                if i >= OB:
                    pe.wait_ge(added, i - OB + 1)
                for c in range(chunks):
                    mm = nc.tensor.matmul(o_ps[i % OB][:, 0:D], src[:, c, i * P:(i + 1) * P], w[:, c, :], start=(c == 0), stop=(c == chunks - 1))
                mm.then_inc(o_done, 1)

            def turn(i):
                pe.wait_ge(r_ready, i + 1)
                if i >= 2:
                    pe.wait_ge(t_out, i - 1)
                for c in range(DC):
                    mm = nc.tensor.transpose(t_ps[i % 2][:, c, :], R[:, i, c * P:(c + 1) * P], ident[:, :])
                mm.then_inc(t_done, 1)

            def logits(i):
                pe.wait_ge(t_out, i + 1)
                for c in range(DC):
                    mm = nc.tensor.matmul(l_ps[:, i * E8:(i + 1) * E8], xT[:, i % 2, c, :], gw[:, c, :], start=(c == 0), stop=(c == DC - 1))
                mm.then_inc(l_done, 1)

            LAG = 2 * GT
            for i in range(T + LAG):
                if i < T:
                    project(i)
                if i == LAG:
                    pe.wait_ge(loaded, LOADS)
                if i >= LAG:
                    turn(i - LAG)
                    if i > LAG:
                        logits(i - LAG - 1)
            logits(T - 1)

        @block.vector
        def _(v):
            steps = Steps(v, dve)

            def add(tiles):
                for i in tiles:
                    v.wait_ge(o_done, i + 1)
                    nc.vector.tensor_tensor(H[:, i, :], o_ps[i % OB][:, 0:D], H[:, i, :], ALU.add).then_inc(added, 1)

            def moments(k):
                for i in group_tiles(k):
                    v.wait_ge(added, i + 1)
                    nc.vector.bn_stats(m["st"][:, i, :], H[:, i, :]).then_inc(stats, 1)
                v.wait_ge(stats, (k + 1) * GT)
                here = slice(k * GT, (k + 1) * GT)
                mean_and_var(nc, steps, m["st"][:, here, :], m["mean"][:, here], m["var"][:, here], m["tmp"][:, here])
                if rms:
                    steps.after(both_norms(nc, m, here, RMS_EPS))
                v.sem_inc(var_ready, 1)

            def normed(k):
                here = slice(k * GT, (k + 1) * GT)
                rstd = m["rstd2"] if rms else m["rstd"]
                v.wait_ge(std_ready, k + 1)
                if rms:
                    nc.vector.reciprocal(m["rstd2"][:, here], m["std2"][:, here])
                steps.after(nc.vector.reciprocal(m["rstd"][:, here], m["std"][:, here]))
                for i in group_tiles(k):
                    nc.vector.tensor_scalar(R[:, i, :], H[:, i, :], m["mean"][:, i:i + 1], rstd[:, i:i + 1], ALU.subtract, ALU.mult).then_inc(r_ready, 1)
                if rms:
                    nc.vector.tensor_scalar(m["var"][:, here], m["rstd"][:, here], 1.0, None, ALU.add)
                    steps.after(nc.vector.tensor_tensor(m["tmp"][:, here], m["mean"][:, here], m["rstd"][:, here], ALU.mult))
                    v.sem_inc(factors_ready, 1)

            add(group_tiles(0))
            for k in range(T // GT):
                after = group_tiles(k + 1) if k < T // GT - 1 else []
                moments(k)
                add(after[:GT - 1])
                normed(k)
                add(after[GT - 1:])
            v.wait_ge(loaded, LOADS)
            v.wait_ge(l_done, T)
            nc.vector.tensor_tensor(lg[:, :, :], l_ps[:, 0:ET].rearrange("p (t e) -> p t e", e=E8), mid(gb[:, :], T), ALU.add)

        @block.gpsimd
        def _(pool):
            if rms:
                for i in range(T):
                    if i % GT == 0:
                        pool.wait_ge(factors_ready, i // GT + 1)
                    pool.wait_ge(r_ready, i + 1)
                    nc.gpsimd.tensor_scalar(H[:, i, :], H[:, i, :], m["var"][:, i:i + 1], m["tmp"][:, i:i + 1], ALU.mult, ALU.subtract)

        @block.scalar
        def _(act):
            def turned(tiles):
                for i in tiles:
                    act.wait_ge(t_done, i + 1)
                    if i >= 2:
                        act.wait_ge(l_done, i - 1)
                    for c in range(DC):
                        scale = {} if norm is None else {"scale": nw[:, c:c + 1]}
                        ins = nc.scalar.activation(xT[:, i % 2, c, :], t_ps[i % 2][:, c, :], ACT.Copy, **scale)
                    ins.then_inc(t_out, 1)

            group_root(nc, act, m, 0, var_ready, std_ready, rms)
            act.wait_ge(loaded, LOADS)
            for k in range(1, T // GT):
                turned(range(max((k - 2) * GT + 1, 0), (k - 1) * GT + 1))
                group_root(nc, act, m, k, var_ready, std_ready, rms)
            turned(range(T - 2 * GT + 1, T))


def by_tile(x):
    return x.rearrange("p (e t) -> p e t", t=T)


def top2(nc, v, steps, m, t):
    lg, m8, ix8, ixf, oh, w = m["lg"], t["m8"], t["ix8"], t["ixf"], t["oh"], m["w"]
    for i in range(T):
        ins = nc.vector.max(m8[:, i, :], lg[:, i, :])
    steps.after(ins)
    for i in range(T):
        ins = nc.vector.max_index(ix8[:, i, :], m8[:, i, :], lg[:, i, :])
    steps.after(ins)
    steps.after(nc.vector.tensor_tensor(w[:, 1, :], m8[:, :, 1], m8[:, :, 0], ALU.subtract))
    v.sem_inc(t["gap_ready"], 1)
    for k in range(2):
        ins = nc.vector.tensor_copy(ixf[:, k, :], ix8[:, :, k])
    steps.after(ins)
    for k in range(2):
        ins = nc.vector.tensor_tensor(by_tile(oh[:, k, :]), mid(ixf[:, k, :], E8), last(m["iota8"][:, :], T), ALU.is_equal)
    steps.after(ins)
    for k in range(2):
        ins = nc.vector.tensor_tensor(by_tile(oh[:, k, :]), by_tile(oh[:, k, :]), mid(m["valid"][:, :], E8), ALU.mult)
    steps.after(ins)
    v.wait_ge(t["exp_ready"], 1)
    steps.after(nc.vector.tensor_scalar(w[:, 0, :], w[:, 1, :], 1.0, None, ALU.add))
    steps.after(nc.vector.reciprocal(w[:, 0, :], w[:, 0, :]))
    steps.after(nc.vector.tensor_tensor(w[:, 1, :], w[:, 1, :], w[:, 0, :], ALU.mult))


def positions(nc, v, steps, m, t, chosen, ps_before, ps_total, asked, counted, n):
    steps.after(nc.vector.tensor_copy(t["chosen_bf"][:, :], chosen))
    v.sem_inc(asked, 1)
    v.wait_ge(counted, n)
    steps.after(nc.vector.tensor_tensor_scan(t["incl"][:, :], m["keep"][:, :], ps_total[:, 0:ET], 0.0, ALU.mult, ALU.add))
    steps.after(nc.vector.tensor_tensor(t["pos"][:, :], t["incl"][:, :], ps_total[:, 0:ET], ALU.subtract))
    steps.after(nc.vector.tensor_tensor(t["pos"][:, :], ps_before[:, 0:ET], t["pos"][:, :], ALU.add))


def count_matmuls(nc, pe, m, t, ps_before, ps_total, asked, counted, n):
    pe.wait_ge(asked, n)
    nc.tensor.matmul(ps_before[:, 0:ET], m["before"][:, :], t["chosen_bf"][:, :], start=True, stop=True)
    nc.tensor.matmul(ps_total[:, 0:ET], m["ones_bf"][:, :], t["chosen_bf"][:, :], start=True, stop=True).then_inc(counted, 1)


def row_indices(nc, steps, m, t, taken):
    for k in range(2):
        steps.after(nc.vector.tensor_tensor(t["incl"][:, :], t["oh"][:, k, :], t["pos"][:, :], ALU.mult))
        steps.after(nc.vector.tensor_reduce(t["row"][:, k, :], t["incl"][:, :].rearrange("p (e t) -> p t e", t=T), AX.X, ALU.add))
        steps.after(nc.vector.tensor_copy(m["gidx"][:, k, :], t["row"][:, k, :]))
        steps.after(nc.vector.tensor_scalar(t["ixf"][:, k, :], taken[k], -FAR, FAR, ALU.mult, ALU.add))
        steps.after(nc.vector.tensor_tensor(m["sidx"][:, k, :], t["row"][:, k, :], t["ixf"][:, k, :], ALU.add))


def routing_tensors(m, ctx):
    sb = lambda name, shape, dt=F32: m["sb"](name, shape, dt, ctx)
    t = {"m8": sb("m8", [P, T, 8]), "ix8": sb("ix8", [P, T, 8], U32), "ixf": sb("ixf", [P, 2, T]),
         "oh": sb("oh", [P, 2, ET]), "chosen": sb("chosen", [P, ET]), "chosen_bf": sb("chosen_bf", [P, ET], BF16),
         "incl": sb("incl", [P, ET]), "pos": sb("pos_e", [P, ET]), "row": sb("row", [P, 2, T])}
    for n in ("gap_ready", "exp_ready"):
        t[n] = m["sem"](n, ctx)
    return t


def scatter_rows(nc, pool, m, rows, nrows, sem):
    for k in range(2):
        for i in range(T):
            nc.gpsimd.indirect_dma_start(
                out=rows[:, :], out_offset=bass.IndirectOffsetOnAxis(ap=m["sidx"][:, k, i:i + 1], axis=0),
                in_=m["R"][:, i, :], in_offset=None, bounds_check=nrows - 1, oob_is_err=False).then_inc(sem, 16)
    pool.wait_ge(sem, 16 * 2 * T)


def moe1(nc, a, out, m, ctx):
    sb = lambda name, shape, dt=F32: m["sb"](name, shape, dt, ctx)
    sem = lambda name: m["sem"](name, ctx)
    m["nw1"] = sb("nw1", [P, DC])
    b1, b2 = sb("b1", [P, E8, F1]), sb("b2", [P, E8, D])
    table = sb("table", [1, NBLK], I32)
    nw_loaded = sem("nw_loaded")
    with ExitStack() as c:
        t = routing_tensors(m, c)
        csb = lambda name, shape, dt=F32: m["sb"](name, shape, dt, c)
        iota_blk, full, nb, nbi = csb("iota_blk", [1, NBLK * E8]), csb("full", [1, NBLK * E8]), csb("nb", [P, E8]), csb("nbi", [P, E8], I32)
        ends, ones8, cntf = csb("ends", [P, E8]), csb("ones8", [P, E8]), csb("cntf", [1, NBLK])
        pb, pt = (m["ps"](n, [P, 512], c) for n in ("ps_before", "ps_total"))
        dve, asked, counted, idx_ready, scattered, iota_loaded = (m["sem"](n, c) for n in (
            "rt_dve", "asked", "counted", "idx_ready", "scattered", "iota_loaded"))
        with nc.Block() as block:
            @block.sync
            def _(sp):
                sp.dma_start(iota_blk[:, :], a["iota_blk"]).then_inc(iota_loaded, 16)
                sp.dma_start(b1[:, :, :], a["moe1_b1"].rearrange("(e f) -> e f", e=E8).partition_broadcast(P)).then_inc(nw_loaded, 16)
                sp.dma_start(b2[:, :, :], a["moe1_b2"].rearrange("(e f) -> e f", e=E8).partition_broadcast(P)).then_inc(nw_loaded, 16)
                sp.dma_start(m["nw1"][:, :], a["f_norm"]).then_inc(nw_loaded, 16)
                sp.wait_ge(nw_loaded, 48)

            @block.scalar
            def _(act):
                act.wait_ge(t["gap_ready"], 1)
                nc.scalar.activation(m["w"][:, 1, :], m["w"][:, 1, :], ACT.Exp).then_inc(t["exp_ready"], 1)

            @block.vector
            def _(v):
                steps = Steps(v, dve)
                top2(nc, v, steps, m, t)
                steps.after(nc.vector.tensor_tensor(t["chosen"][:, :], t["oh"][:, 0, :], t["oh"][:, 1, :], ALU.add))
                positions(nc, v, steps, m, t, t["chosen"][:, :], pb, pt, asked, counted, 1)
                steps.after(nc.vector.tensor_scalar(nbi[:, :], by_tile(t["incl"][:, :])[:, :, T - 1], float(P - 1), None, ALU.add))
                steps.after(nc.vector.tensor_scalar(nbi[:, :], nbi[:, :], 7, None, ALU.logical_shift_right))
                steps.after(nc.vector.tensor_copy(nb[:, :], nbi[:, :]))
                steps.after(nc.vector.memset(ones8[:, :], 1.0))
                steps.after(nc.vector.tensor_tensor_scan(ends[:, :], ones8[:, :], nb[:, :], 0.0, ALU.mult, ALU.add))
                steps.after(nc.vector.tensor_tensor(nb[:, :], ends[:, :], nb[:, :], ALU.subtract))
                steps.after(nc.vector.scalar_tensor_tensor(out=by_tile(t["pos"][:, :]), in0=last(nb[:, :], T), scalar=float(P),
                                                           in1=by_tile(t["pos"][:, :]), op0=ALU.mult, op1=ALU.add))
                row_indices(nc, steps, m, t, [m["valid"][:, :], m["valid"][:, :]])
                v.sem_inc(idx_ready, 1)
                v.wait_ge(iota_loaded, 16)
                steps.after(nc.vector.tensor_tensor(full[:, :].rearrange("p (n e) -> p n e", e=E8), iota_blk[:, :].rearrange("p (n e) -> p n e", e=E8),
                                                    mid(ends[0:1, :], NBLK), ALU.is_ge))
                steps.after(nc.vector.tensor_reduce(cntf[:, :], full[:, :].rearrange("p (n e) -> p n e", e=E8), AX.X, ALU.add))
                steps.after(nc.vector.tensor_scalar(table[:, :], cntf[:, :], float(E8 - 1), None, ALU.min))

            @block.tensor
            def _(pe):
                count_matmuls(nc, pe, m, t, pb, pt, asked, counted, 1)

            @block.gpsimd
            def _(pool):
                pool.wait_ge(m["zeros_stored1"], zeros_count(NBLK * P))
                pool.wait_ge(idx_ready, 1)
                scatter_rows(nc, pool, m, m["rows1"], NBLK * P, scattered)

    with ExitStack() as c:
        moe1_experts(nc, a, m, c, b1, b2, table)


def moe1_experts(nc, a, m, ctx, b1, b2, table):
    sb = lambda name, shape, dt=F32: m["sb"](name, shape, dt, ctx)
    sem = lambda name: m["sem"](name, ctx)
    ident, w1, w2 = m["ident"], m["w1"], m["w2"]
    XS = 4
    x = sb("ex", [P, XS, D])
    xT = sb("exT", [P, 2, DC, P])
    h = sb("eh", [P, 2, F1])
    sg = sb("esg", [P, 2, D])
    act_b = sb("eact", [P, 2, D])
    actT = sb("eactT", [P, 2, DC, P])
    o = sb("eo", [P, 2, D])
    psum = lambda name: [m["ps"](f"{name}{i}", [P, 512], ctx) for i in range(2)]
    x_ps, h_ps, t_ps, o_ps = psum("ex_ps"), psum("eh_ps"), psum("et_ps"), psum("eo_ps")
    x_used, xT_ready, h_done, h_out, glu_ready, sig_ready, act_ready, t_done, actT_ready, o_done, o_ready, dve = map(
        sem, ("x_used", "xT_ready", "h_done", "h_out", "glu_ready", "sig_ready", "act_ready", "et_done", "actT_ready", "eo_done", "o_ready", "e_dve"))
    x_loaded = [sem(f"x_loaded{q}") for q in range(XS)]
    o_stored = [sem(f"o_stored{p}") for p in range(2)]

    def middle_blocks(eng, step):
        for i in range(2, XS):
            step(i, i)
        with eng.Fori(1, NBLK // XS) as j:
            for q in range(XS):
                step(j * XS + q, q)
        for i in range(NBLK // XS * XS, NBLK - 1):
            step(i, i % XS)

    with nc.Block() as block:
        @block.sync
        def _(sp):
            def load(i, q):
                sp.wait_ge(x_used, i + 1)
                sp.dma_start(x[:, q, :], m["rows1"][bass.ds(i * P, P), :]).then_inc(x_loaded[q], 16)

            for i in range(XS):
                load(i, i)
            with sp.Fori(1, NBLK // XS) as j:
                for q in range(XS):
                    load(j * XS + q, q)
            for i in range(NBLK // XS * XS, NBLK):
                load(i, i % XS)

        @block.tensor
        def _(pe):
            pe.sem_inc(x_used, XS)
            pe.sem_inc(t_done, 2)
            pe.wait_ge(m["moe1_loaded"], 32)

            def turn_x(i, q):
                pe.wait_ge(x_loaded[q], (i - q) * (16 // XS) + 16)
                pe.wait_ge(xT_ready, i + 1)
                for c in range(DC):
                    mm = nc.tensor.transpose(x_ps[q % 2][:, c * P:(c + 1) * P], x[:, q, c * P:(c + 1) * P], ident[:, :])
                mm.then_inc(x_used, 1)

            def expert(i):
                return nc.tensor.value_load(table[0:1, bass.ds(i, 1)], min_val=0, max_val=E8 - 1)

            def hidden(i, p, e):
                pe.wait_ge(xT_ready, i + 3)
                pe.wait_ge(h_out, i + 1)
                for c in range(DC):
                    mm = nc.tensor.matmul(h_ps[p][:, :], xT[:, p, c, :], w1[:, bass.ds(e, 1), c, :].rearrange("p a f -> p (a f)"),
                                          start=(c == 0), stop=(c == DC - 1))
                mm.then_inc(h_done, 1)

            def turn_act(i, p):
                pe.wait_ge(act_ready, i + 1)
                pe.wait_ge(actT_ready, i + 1)
                for c in range(DC):
                    mm = nc.tensor.transpose(t_ps[p][:, c * P:(c + 1) * P], act_b[:, p, c * P:(c + 1) * P], ident[:, :])
                mm.then_inc(t_done, 1)

            def output(i, p, e):
                pe.wait_ge(actT_ready, i + 3)
                pe.wait_ge(o_ready, i + 1)
                for c in range(DC):
                    mm = nc.tensor.matmul(o_ps[p][:, 0:D], actT[:, p, c, :], w2[:, bass.ds(e, 1), c, :].rearrange("p a f -> p (a f)"),
                                          start=(c == 0), stop=(c == DC - 1))
                mm.then_inc(o_done, 1)

            turn_x(0, 0)
            turn_x(1, 1)
            experts = [expert(0), expert(1), None, None]
            hidden(0, 0, experts[0])
            turn_x(2, 2)
            hidden(1, 1, experts[1])

            def step(i, q):
                e = experts[q] = expert(i)
                turn_act(i - 2, q % 2)
                turn_x(i + 1, (q + 1) % XS)
                hidden(i, q % 2, e)
                output(i - 2, q % 2, experts[q - 2] if q >= 2 else expert(i - 2))

            middle_blocks(pe, step)
            i = NBLK - 1
            turn_act(i - 2, i % 2)
            hidden(i, i % 2, expert(i))
            output(i - 2, i % 2, expert(i - 2))
            for i in (NBLK - 2, NBLK - 1):
                turn_act(i, i % 2)
                output(i, i % 2, expert(i))

        @block.scalar
        def _(act):
            act.sem_inc(xT_ready, 2)
            act.sem_inc(actT_ready, 2)

            for p in range(2):
                act.sem_inc(o_stored[p], 16)

            def store(i, p):
                act.wait_ge(o_ready, i + 3)
                act.dma_start(m["outs1"][bass.ds(i * P, P), :], o[:, p, :]).then_inc(o_stored[p], 16)

            def turned_x(i, p):
                act.wait_ge(x_used, i + (1 + XS))
                act.wait_ge(h_done, i + 1)
                for c in range(DC):
                    ins = nc.scalar.activation(xT[:, p, c, :], x_ps[p][:, c * P:(c + 1) * P], ACT.Copy, scale=m["nw1"][:, c:c + 1])
                ins.then_inc(xT_ready, 1)

            def sigmoid(i, p):
                act.wait_ge(glu_ready, i + 1)
                nc.scalar.activation(sg[:, p, :], h[:, p, 0:D], ACT.Sigmoid, scale=1.702).then_inc(sig_ready, 1)

            def turned_act(i, p):
                act.wait_ge(t_done, i + 3)
                act.wait_ge(o_done, i + 1)
                nc.scalar.activation(actT[:, p, :, :], t_ps[p][:, 0:D], ACT.Copy).then_inc(actT_ready, 1)

            turned_x(0, 0)
            turned_x(1, 1)
            sigmoid(0, 0)
            turned_x(2, 0)
            sigmoid(1, 1)

            def step(i, q):
                turned_act(i - 2, q % 2)
                turned_x(i + 1, (q + 1) % 2)
                if not (isinstance(i, int) and i < 4):
                    store(i - 4, q % 2)
                sigmoid(i, q % 2)

            middle_blocks(act, step)
            i = NBLK - 1
            turned_act(i - 2, i % 2)
            store(i - 4, i % 2)
            sigmoid(i, i % 2)
            store(i - 3, (i + 1) % 2)
            for i in (NBLK - 2, NBLK - 1):
                turned_act(i, i % 2)
                store(i - 1, (i + 1) % 2)
            store(NBLK - 1, (NBLK - 1) % 2)
            for p in range(2):
                act.wait_ge(o_stored[p], 16 * (NBLK // 2 + 1))

        @block.vector
        def _(v):
            v.sem_inc(h_out, 2)
            v.sem_inc(h_done, 2)
            v.sem_inc(o_done, 2)
            v.sem_inc(o_ready, 2)

            def expert(i):
                return nc.vector.value_load(table[0:1, bass.ds(i, 1)], min_val=0, max_val=E8 - 1)

            experts = [expert(0), None, None, None]

            def swiglu(i, q):
                p, e = q % 2, experts[q]
                v.wait_ge(h_done, i + 3)
                nc.vector.tensor_tensor(h[:, p, :], h_ps[p][:, :], b1[:, bass.ds(e, 1), :].rearrange("p a f -> p (a f)"), ALU.add).then_inc(h_out, 1)
                v.wait_ge(h_out, i + 3)
                nc.vector.tensor_scalar(h[:, p, 0:D], h[:, p, 0:D], 7.0, None, ALU.min).then_inc(glu_ready, 1)
                nc.vector.tensor_scalar(h[:, p, D:F1], h[:, p, D:F1], 7.0, -7.0, ALU.min, ALU.max).then_inc(dve, 1)
                if not (isinstance(i, int) and i < 3):
                    finish(i - 3, 1 - p, experts[0] if q == 3 else expert(i - 3))
                v.wait_ge(sig_ready, i + 1)
                v.wait_ge(t_done, i + 1)
                nc.vector.tensor_tensor(sg[:, p, :], sg[:, p, :], h[:, p, 0:D], ALU.mult).then_inc(dve, 1)
                if q < XS - 1 and not (isinstance(i, int) and i == NBLK - 1):
                    experts[q + 1] = expert(i + 1)
                v.wait_ge(dve, i * 2 + 2)
                nc.vector.scalar_tensor_tensor(out=act_b[:, p, :], in0=h[:, p, D:F1], scalar=1.0, in1=sg[:, p, :], op0=ALU.add, op1=ALU.mult).then_inc(act_ready, 1)

            def finish(i, p, e):
                v.wait_ge(o_done, i + 3)
                v.wait_ge(o_stored[p], (i - p) * 8 + 16)
                nc.vector.tensor_tensor(o[:, p, :], o_ps[p][:, 0:D], b2[:, bass.ds(e, 1), :].rearrange("p a f -> p (a f)"), ALU.add).then_inc(o_ready, 1)

            swiglu(0, 0)
            swiglu(1, 1)

            def step(i, q):
                if q == 0:
                    experts[0] = expert(i)
                swiglu(i, q)

            middle_blocks(v, step)
            swiglu(NBLK - 1, (NBLK - 1) % XS)
            for i in (NBLK - 3, NBLK - 2, NBLK - 1):
                finish(i, i % 2, expert(i))


def gather_rows(nc, pool, m, outs, nrows, got, loaded, used, slots):
    n = 0
    for i in range(T):
        for k in range(2):
            if n >= slots:
                pool.wait_ge(used, n - slots + 1)
            nc.gpsimd.indirect_dma_start(
                out=got[:, n % slots, :], out_offset=None, in_=outs[:, :],
                in_offset=bass.IndirectOffsetOnAxis(ap=m["gidx"][:, k, i:i + 1], axis=0),
                bounds_check=nrows - 1, oob_is_err=False).then_inc(loaded[n % slots], 16)
            n += 1


def attention(nc, a, out, m, ctx):
    sb = lambda name, shape: m["sb"](name, shape, F32, ctx)
    m["uT"] = sb("auT", [P, DC, NPAD])
    m["qT"], m["kT"] = sb("qT", [P, DC, NPAD]), sb("kT", [P, DC, NPAD])
    m["aw"] = sb("aw", [S, B, 2 * NH])
    m["ctxT"] = sb("ctxT", [P, DC, NPAD])
    for part in (combine1_and_project, windows, attention_core):
        with ExitStack() as c:
            part(nc, a, m, c)
    with ExitStack() as c:
        project_and_route(nc, m, c, m["ctxT"], DC, a["a_wo"], False, None, a["r_gw"], a["r_gb"])


def collect(nc, v, steps, m, tiles, got, loaded, used, stats, var_ready, into, first_in=None):
    w, slots = m["w"], len(loaded)
    for i in tiles:
        for k in range(2) if first_in is None else (1,):
            n = 2 * i + k
            v.wait_ge(loaded[n % slots], 16 * (n // slots + 1))
            if first_in is not None:
                v.wait_ge(first_in, i + 1)
            elif k:
                v.wait_ge(used, n)
            nc.vector.scalar_tensor_tensor(out=into[:, i, :], in0=got[:, n % slots, :], scalar=w[:, k, i:i + 1], in1=into[:, i, :],
                                           op0=ALU.mult, op1=ALU.add).then_inc(used, 1 if first_in is None else 2)
        v.wait_ge(used, 2 * i + 2)
        nc.vector.bn_stats(m["st"][:, i, :], into[:, i, :]).then_inc(stats, 1)
    v.wait_ge(stats, tiles[-1] + 1)
    here = slice(tiles[0], tiles[-1] + 1)
    mean_and_var(nc, steps, m["st"][:, here, :], m["mean"][:, here], m["var"][:, here], m["tmp"][:, here])
    v.sem_inc(var_ready, 1)


def combine1_and_project(nc, a, m, ctx):
    SL, US, QB = 6, 6, 6
    NQ = 4
    GN = GT * P
    sb = lambda name, shape: m["sb"](name, shape, F32, ctx)
    sem = lambda name: m["sem"](name, ctx)
    H, uT, ident = m["H"], m["uT"], m["ident"]
    got, u = sb("got", [P, SL, D]), sb("fu", [P, US, D])
    wq, wk, bq, bk = sb("wq", [P, DC, D]), sb("wk", [P, DC, D]), sb("bq", [P, DC]), sb("bk", [P, DC])
    ut = [m["ps"](f"fut{i}", [P, 512], ctx) for i in range(2)]
    ps = [m["ps"](f"qk_ps{i}", [P, 512], ctx) for i in range(QB)]
    loaded = [sem(f"g_loaded{i}") for i in range(SL)]
    used, stats, dve, var_ready, std_ready, u_ready, ut_done, ut_out, w_loaded, qk_done, qk_out, padded = map(
        sem, ("g_used", "fstats", "fdve", "fvar", "fstd", "fu_ready", "fut_done", "fut_out", "qk_loaded", "qk_done", "qk_out", "ct_padded"))
    with nc.Block() as block:
        @block.sync
        def _(sp):
            for t, k in ((wq, "a_wq"), (wk, "a_wk")):
                sp.dma_start(t[:, :, :], a[k]).then_inc(w_loaded, 16)
            for t, k in ((bq, "a_bq"), (bk, "a_bk")):
                sp.dma_start(t[:, :], a[k]).then_inc(w_loaded, 16)

        @block.gpsimd
        def _(pool):
            gather_rows(nc, pool, m, m["outs1"], NBLK * P, got, loaded, used, SL)
            nc.gpsimd.memset(m["ctxT"][:, :, N:NPAD], 0.0).then_inc(padded, 1)

        @block.vector
        def _(v):
            steps = Steps(v, dve)

            def norm(k):
                here = slice(k * GT, (k + 1) * GT)
                v.wait_ge(std_ready, k + 1)
                steps.after(nc.vector.reciprocal(m["rstd"][:, here], m["std"][:, here]))
                for i in group_tiles(k):
                    if i >= US:
                        v.wait_ge(ut_done, i - US + 1)
                    nc.vector.tensor_scalar(u[:, i % US, :], H[:, i, :], m["mean"][:, i:i + 1], m["rstd"][:, i:i + 1], ALU.subtract, ALU.mult).then_inc(u_ready, 1)

            for k in range(T // GT):
                collect(nc, v, steps, m, group_tiles(k), got, loaded, used, stats, var_ready, H)
                norm(k)

        @block.scalar
        def _(act):
            act.wait_ge(w_loaded, 64)

            def turned(k):
                for i in group_tiles(k):
                    act.wait_ge(ut_done, i + 1)
                    nc.scalar.activation(uT[:, :, i * P:(i + 1) * P], ut[i % 2][:, 0:D].rearrange("p (c q) -> p c q", q=P), ACT.Copy).then_inc(ut_out, 1)

            def projected(k):
                for n in range(NQ):
                    b, to, bias = k * NQ + n, (m["qT"], m["kT"])[n // DC], (bq, bk)[n // DC]
                    act.wait_ge(qk_done, b + 1)
                    nc.scalar.activation(to[:, n % DC, k * GN:(k + 1) * GN], ps[b % QB][:, 0:GN], ACT.Identity, bias=bias[:, n % DC:n % DC + 1]).then_inc(qk_out, 1)

            for k in range(T // GT):
                group_root(nc, act, m, k, var_ready, std_ready)
                turned(k)
                if k:
                    projected(k - 1)
            projected(T // GT - 1)

        @block.tensor
        def _(pe):
            pe.wait_ge(w_loaded, 64)
            for k in range(T // GT):
                for i in group_tiles(k):
                    pe.wait_ge(u_ready, i + 1)
                    if i >= 2:
                        pe.wait_ge(ut_out, i - 1)
                    for c in range(DC):
                        mm = nc.tensor.transpose(ut[i % 2][:, c * P:(c + 1) * P], u[:, i % US, c * P:(c + 1) * P], ident[:, :])
                    mm.then_inc(ut_done, 1)
                pe.wait_ge(ut_out, (k + 1) * GT)
                for n in range(NQ):
                    b, w = k * NQ + n, (wq, wk)[n // DC]
                    if b >= QB:
                        pe.wait_ge(qk_out, b - QB + 1)
                    for c in range(DC):
                        mm = nc.tensor.matmul(ps[b % QB][:, 0:GN], w[:, c, (n % DC) * P:(n % DC + 1) * P], uT[:, c, k * GN:(k + 1) * GN],
                                              start=(c == 0), stop=(c == DC - 1))
                    mm.then_inc(qk_done, 1)


def windows(nc, a, m, ctx):
    sb = lambda name, shape: m["sb"](name, shape, F32, ctx)
    sem = lambda name: m["sem"](name, ctx)
    qT, aw = m["qT"], m["aw"]
    wfq, wfg = sb("wfq", [P, DC, D]), sb("wfg", [P, DC, D])
    upz, bfq, bfg = sb("upz", [P, DC, 2 * NH]), sb("bfq", [P, DC]), sb("bfg", [P, DC])
    glo, gb = sb("glo", [P, DC, B]), sb("gbias", [P, DC, B])
    cT = sb("c_T", [P, 2, DC, G4])
    e = sb("epz", [S, 2, 4, 2 * NH])
    rp = sb("rp", [S, 2, 4, NH])
    bo = sb("bo", [P, D])
    bo_loaded, bo_added = sem("bo_loaded"), sem("bo_added")
    ROOT2 = 2.0 ** 0.5
    c_ps = [m["ps"](f"c_ps{i}", [P, 2, 512], ctx) for i in range(2)]
    pz_ps = [m["ps"](f"pz_ps{i}", [P, 2, 512], ctx) for i in range(2)]
    loaded, dve, glo_ready, g_done, c_done, c_in, c_ready, pz_done, e_ready, aw_ready = map(
        sem, ("w_loaded", "w_dve", "glo_ready", "g_done", "c_done", "c_in", "c_ready", "pz_done", "e_ready", "aw_ready"))
    with nc.Block() as block:
        @block.sync
        def _(sp):
            for t, k in ((wfq, "a_wfq"), (wfg, "a_wfg"), (upz, "a_upz")):
                sp.dma_start(t[:, :, :], a[k]).then_inc(loaded, 16)
            for t, k in ((bfq, "a_bfq"), (bfg, "a_bfg")):
                sp.dma_start(t[:, :], a[k]).then_inc(loaded, 16)
            sp.dma_start(bo[:, :], a["a_bo_row"].partition_broadcast(P)).then_inc(bo_loaded, 16)

        @block.gpsimd
        def _(pool):
            pool.wait_ge(bo_loaded, 16)
            nc.gpsimd.tensor_tensor(m["H"][:, :, :], m["H"][:, :, :], mid(bo[:, :], T), ALU.add).then_inc(bo_added, 1)

        @block.tensor
        def _(pe):
            pe.wait_ge(loaded, 80)
            pe.wait_ge(glo_ready, 1)
            for n in range(DC):
                for c in range(DC):
                    mm = nc.tensor.matmul(pz_ps[0][:, n, 0:B], wfg[:, c, n * P:(n + 1) * P], glo[:, c, :], start=(c == 0), stop=(c == DC - 1))
            mm.then_inc(g_done, 1)

            def c_args(i, p):
                pe.wait_ge(c_in, i + 1)
                for n in range(DC):
                    for c in range(DC):
                        mm = nc.tensor.matmul(c_ps[p][:, n, 0:G4], wfq[:, c, n * P:(n + 1) * P], qT[:, c, bass.ds(i * G4, G4)], start=(c == 0), stop=(c == DC - 1))
                mm.then_inc(c_done, 1)

            def pz(i, p):
                pe.wait_ge(c_ready, i + 1)
                pe.wait_ge(e_ready, i + 1)
                for k in range(4):
                    for c in range(DC):
                        mm = nc.tensor.matmul(pz_ps[p][0:S, 0, k * 2 * NH:(k + 1) * 2 * NH], cT[:, p, c, k * S:(k + 1) * S], upz[:, c, :], start=(c == 0), stop=(c == DC - 1))
                mm.then_inc(pz_done, 1)

            c_args(0, 0)
            with pe.Fori(0, NG // 2 - 1) as j:
                for p in range(2):
                    c_args(j * 2 + (p + 1), 1 - p)
                    pz(j * 2 + p, p)
            c_args(NG - 1, 1)
            pz(NG - 2, 0)
            pz(NG - 1, 1)

        @block.vector
        def _(v):
            steps = Steps(v, dve)
            v.sem_inc(c_in, 2)
            v.sem_inc(pz_done, 2)
            v.sem_inc(aw_ready, 2)
            for c in range(DC):
                ins = nc.vector.tensor_reduce(glo[:, c, :], qT[:, c, 0:N].rearrange("p (b s) -> p b s", s=S), AX.X, ALU.add)
            steps.after(ins)
            steps.after(nc.vector.tensor_scalar(glo[:, :, :], glo[:, :, :], 1.0 / S, None, ALU.mult))
            v.sem_inc(glo_ready, 1)
            v.wait_ge(loaded, 80)
            steps.after(nc.vector.tensor_tensor(bfq[:, :], bfq[:, :], bfg[:, :], ALU.add))
            v.wait_ge(g_done, 1)
            steps.after(nc.vector.tensor_tensor(gb[:, :, :], pz_ps[0][:, :, 0:B], last(bfq[:, :], B), ALU.add))
            v.sem_inc(e_ready, 2)
            base = steps.n

            def add_global(i, p):
                v.wait_ge(c_done, i + 1)
                v.wait_ge(pz_done, i + 1)
                g = gb[:, :, bass.ds(i * 4, 4)]
                for n in range(DC):
                    ins = nc.vector.tensor_tensor(cT[:, p, n, :].rearrange("p (b s) -> p b s", s=S), c_ps[p][:, n, 0:G4].rearrange("p (b s) -> p b s", s=S),
                                                  g[:, n, :].unsqueeze(2).broadcast_to([P, 4, S]), ALU.add)
                ins.then_inc(c_in, 1)

            def weights(i, p):
                v.wait_ge(e_ready, i + 3)
                ep, ez = e[:, p, :, 0:NH], e[:, p, :, NH:2 * NH]
                nc.vector.tensor_scalar(e[:, p, :, :], e[:, p, :, :], 1.0, None, ALU.add).then_inc(dve, 1)
                v.wait_ge(dve, i * 2 + (base + 1))
                nc.vector.reciprocal(rp[:, p, :, :], ep).then_inc(dve, 1)
                here = aw[0:S, bass.ds(i * 4, 4), :]
                nc.vector.tensor_scalar(here[:, :, 0:NH], ez, ROOT2 / S, None, ALU.mult)
                v.wait_ge(dve, i * 2 + (base + 2))
                nc.vector.scalar_tensor_tensor(out=here[:, :, NH:2 * NH], in0=ez, scalar=-ROOT2, in1=rp[:, p, :, :], op0=ALU.mult, op1=ALU.mult).then_inc(aw_ready, 1)

            add_global(0, 0)
            with v.Fori(0, NG // 2 - 1) as j:
                for p in range(2):
                    add_global(j * 2 + (p + 1), 1 - p)
                    weights(j * 2 + p, p)
            add_global(NG - 1, 1)
            weights(NG - 2, 0)
            weights(NG - 1, 1)

        @block.scalar
        def _(act):
            def tanh(i, p):
                act.wait_ge(c_in, i + 3)
                nc.scalar.activation(cT[:, p, :, :], cT[:, p, :, :], ACT.Tanh).then_inc(c_ready, 1)

            def exps(i, p):
                act.wait_ge(pz_done, i + 3)
                act.wait_ge(aw_ready, i + 1)
                nc.scalar.activation(e[:, p, :, :].rearrange("p k n -> p (k n)"), pz_ps[p][0:S, 0, 0:8 * NH], ACT.Exp, scale=-1.0).then_inc(e_ready, 1)

            tanh(0, 0)
            with act.Fori(0, NG // 2 - 1) as j:
                for p in range(2):
                    tanh(j * 2 + (p + 1), 1 - p)
                    exps(j * 2 + p, p)
            tanh(NG - 1, 1)
            exps(NG - 2, 0)
            exps(NG - 1, 1)


def attention_core(nc, a, m, ctx):
    sb = lambda name, shape: m["sb"](name, shape, F32, ctx)
    sem = lambda name: m["sem"](name, ctx)
    uT, qT, kT, aw, ctxT, ident = m["uT"], m["qT"], m["kT"], m["aw"], m["ctxT"], m["ident"]
    UH = 4
    UPB = NH // UH
    UC = UH * S
    CH = P // AD
    VW = AD + 1
    AHEAD = 3
    SQC = UPB + 1
    place, eo, bv, wv = sb("place", [S, S]), sb("head_of", [P, CH]), sb("bv", [S, D]), sb("wv", [P, DC, D])
    us, qs, ks, ws = sb("aus", [P, 2, DC, S]), sb("qs", [P, 2, DC, S]), sb("ks", [P, 2, DC, CH, S]), sb("ws", [S, 2, 2 * NH])
    vs = sb("vs", [P, 2, NH * VW])
    sq, ss, mx = sb("sq", [S, UPB, UC]), sb("ss", [P, UPB, UC]), sb("mx", [S, UPB, UH])
    pts, cx, rc = sb("pts", [P, 2, UC]), sb("cx", [S, 2, D]), sb("rc", [S, NH])
    s_ps = [m["ps"](f"s_ps{i}", [P, 512], ctx) for i in range(UPB)]
    p_ps = [m["ps"](f"p_ps{i}", [P, 512], ctx) for i in range(2)]
    v_ps, c_ps = m["ps"]("v_ps", [P, 512], ctx), m["ps"]("cx_ps", [P, 512], ctx)
    consts, ones_set, copied, k_ready, v_done, v_out, s_done, sq_ready, ss_ready, mx_ready, sh_ready, pr_ready, pt_done, pt_out, c_done, c_out, rc_ready, ct_done, ct_out = map(
        sem, ("at_consts", "ones_set", "copied", "k_ready", "v_done", "v_out", "s_done", "sq_ready", "ss_ready", "mx_ready", "sh_ready", "pr_ready",
              "pt_done", "pt_out", "cx_done", "cx_out", "rc_ready", "ct_done", "ct_out"))

    def heads(x):
        return x.rearrange("p (h s) -> p h s", s=S)

    def units(step):
        def run(eng):
            for u in range(UPB):
                step(u, u, 0, 0, True, B - 1)
            with eng.Fori(0, B // 2 - 2) as j:
                for r in range(2 * UPB):
                    k, u = r // UPB, r % UPB
                    step(j * (2 * UPB) + (UPB + r), u, j * 2 + (k + 1), 1 - k, False, 3)
            for b in range(B - 3, B):
                for u in range(UPB):
                    step(b * UPB + u, u, b, b % 2, False, B - 1 - b)
        return run

    with nc.Block() as block:
        @block.sync
        def _(sp):
            sp.dma_start(place[:, :], a["place"].partition_broadcast(S)).then_inc(consts, 16)
            sp.dma_start(eo[:, :], a["head_of"]).then_inc(consts, 16)
            sp.dma_start(bv[:, :], a["a_bv_row"].partition_broadcast(S)).then_inc(consts, 16)
            sp.dma_start(wv[:, :, :], a["a_wv"]).then_inc(consts, 16)
            store_zeros(sp, m, m["rows2"], m["zeros_stored2"])

        @block.tensor
        def _(pe):
            pe.sem_inc(s_done, 2 * UPB)
            pe.sem_inc(v_done, 2)
            pe.wait_ge(consts, 64)

            def values(b, q):
                pe.wait_ge(copied, b + 1)
                pe.wait_ge(ct_out, b + 1)
                for c in range(DC):
                    mm = nc.tensor.matmul(v_ps[0:S, 0:D], us[:, q, c, :], wv[:, c, :], start=(c == 0), stop=(c == DC - 1))
                mm.then_inc(v_done, 1)

            def scores(n, u, b, q):
                if u == 0:
                    pe.wait_ge(copied, b + 1)
                    pe.wait_ge(k_ready, b + 1)
                pe.wait_ge(ss_ready, n + 1)
                h = u % 2 * UH
                nc.tensor.matmul(s_ps[u][0:S, 0:UC], qs[:, q, u // 2, :],
                                 ks[:, q, u // 2, h:h + UH, :].rearrange("p a s -> p (a s)"), start=True, stop=True).then_inc(s_done, 1)

            def turn(n, u):
                pe.wait_ge(pr_ready, n + 1)
                pe.wait_ge(pt_out, n + 1)
                for h in range(UH):
                    mm = nc.tensor.transpose(p_ps[u % 2][0:S, h * S:(h + 1) * S], ss[0:S, u, h * S:(h + 1) * S], ident[0:S, 0:S])
                mm.then_inc(pt_done, 1)

            def context(n, u, b, q):
                if u == 0:
                    pe.wait_ge(v_out, b + 1)
                    pe.wait_ge(c_out, b + 1)
                pe.wait_ge(pt_out, n + 3)
                for h in range(UH):
                    g = u * UH + h
                    mm = nc.tensor.matmul(c_ps[0:S, g * VW:(g + 1) * VW], pts[:, u % 2, h * S:(h + 1) * S], vs[:, q, g * VW:(g + 1) * VW], start=True, stop=True)
                if u == UPB - 1:
                    mm.then_inc(c_done, 1)

            def turn_context(b, q, final=False):
                pe.wait_ge(c_out, b + 2)
                if not final:
                    pe.wait_ge(v_out, b + 2)
                pe.wait_ge(ct_out, b + 2)
                for c in range(DC):
                    mm = nc.tensor.transpose(v_ps[:, D + c * S:D + (c + 1) * S], cx[:, q, c * P:(c + 1) * P], ident[0:S, 0:S])
                mm.then_inc(ct_done, 1)

            values(0, 0)
            for u in range(AHEAD):
                scores(u, u, 0, 0)

            def step(n, u, b, q, first, left):
                u3 = (u + AHEAD) % UPB
                if u3 > u:
                    scores(n + AHEAD, u3, b, q)
                elif left:
                    scores(n + AHEAD, u3, b + 1, 1 - q)
                turn(n, u)
                if u > 0:
                    context(n - 1, u - 1, b, q)
                elif not first:
                    context(n - 1, UPB - 1, b - 1, 1 - q)
                if u == 1 and not first:
                    turn_context(b - 1, 1 - q)
                if u == UPB - 1 and left:
                    values(b + 1, 1 - q)

            units(step)(pe)
            context(B * UPB - 1, UPB - 1, B - 1, 1)
            turn_context(B - 1, 1, True)

        @block.scalar
        def _(act):
            act.sem_inc(sq_ready, SQC)
            act.sem_inc(ct_out, 2)
            act.wait_ge(consts, 64)

            def square(n, u, b, q):
                if u == 0:
                    act.wait_ge(copied, b + 1)
                act.wait_ge(ss_ready, n + 1)
                for h in range(UH):
                    g = u * UH + h
                    ins = nc.scalar.activation(sq[:, u, h * S:(h + 1) * S], place[:, :], ACT.Square, scale=ws[:, q, g:g + 1], bias=ws[:, q, NH + g:NH + g + 1])
                ins.then_inc(sq_ready, 1)

            def exp(n, u):
                act.wait_ge(sh_ready, n + 1)
                nc.scalar.activation(ss[0:S, u, :], ss[0:S, u, :], ACT.Exp).then_inc(pr_ready, 1)

            def context_out(b):
                act.wait_ge(ct_done, b + 1)
                nc.scalar.activation(cols(ctxT, b * S, S), v_ps[:, D:D + DC * S].rearrange("p (c s) -> p c s", s=S), ACT.Copy).then_inc(ct_out, 1)

            for u in range(UPB):
                square(u, u, 0, 0)
            exp(0, 0)

            def step(n, u, b, q, first, left):
                if left or u < UPB - 1:
                    exp(n + 1, (u + 1) % UPB)
                if left:
                    square(n + UPB, u, b + 1, 1 - q)
                if u == 2 and not first:
                    context_out(b - 1)

            units(step)(act)
            context_out(B - 1)

        @block.gpsimd
        def _(pool):
            def copies(b, q):
                pool.wait_ge(s_done, b * UPB + UPB)
                pool.wait_ge(v_done, b + 1)
                pool.wait_ge(sq_ready, b * UPB + 1)
                here = b * S
                nc.gpsimd.tensor_copy(us[:, q, :, :], cols(uT, here, S))
                nc.gpsimd.tensor_copy(qs[:, q, :, :], cols(qT, here, S))
                nc.gpsimd.tensor_copy(ws[:, q, :], tile_of(aw, b)[0:S, :]).then_inc(copied, 1)

            for b in range(2):
                copies(b, b)

            def step(n, u, b, q, first, left):
                pool.wait_ge(mx_ready, n + 1)
                nc.gpsimd.tensor_tensor(heads(ss[0:S, u, :]), heads(ss[0:S, u, :]), last(mx[:, u, :], S), ALU.subtract).then_inc(sh_ready, 1)
                if u == 2 and left >= 2:
                    copies(b + 2, q)

            units(step)(pool)

        @block.vector
        def _(v):
            v.sem_inc(ss_ready, UPB)
            v.sem_inc(pt_out, 2)
            v.sem_inc(c_out, 1)
            for t in (vs, ss, pts):
                nc.vector.memset(t[:, :, :], 0.0).then_inc(ones_set, 1)
            v.wait_ge(ones_set, 3)
            nc.vector.memset(vs[0:S, :, :], 1.0).then_inc(ones_set, 1)
            v.wait_ge(ones_set, 4)
            v.wait_ge(consts, 64)

            def keys(b, q):
                v.wait_ge(s_done, b * UPB + UPB)
                for e in range(CH):
                    ins = nc.vector.tensor_scalar(ks[:, q, :, e, :], cols(kT, b * S, S), eo[:, e:e + 1], 0.25, ALU.mult, ALU.mult)
                ins.then_inc(k_ready, 1)

            def values(b, q):
                v.wait_ge(v_done, b + 3)
                nc.vector.tensor_tensor(vs[0:S, q, :].rearrange("p (h w) -> p h w", w=VW)[:, :, 0:AD], v_ps[0:S, 0:D].rearrange("p (h w) -> p h w", w=AD),
                                        bv[:, :].rearrange("p (h w) -> p h w", w=AD), ALU.add).then_inc(v_out, 1)

            def scores(n, u):
                v.wait_ge(s_done, n + (1 + 2 * UPB))
                v.wait_ge(sq_ready, n + (1 + SQC))
                nc.vector.tensor_tensor(ss[0:S, u, :], s_ps[u][0:S, 0:UC], sq[:, u, :], ALU.subtract).then_inc(ss_ready, 1)
                v.wait_ge(ss_ready, n + (1 + UPB))
                nc.vector.tensor_reduce(mx[:, u, :], heads(ss[0:S, u, :]), AX.X, ALU.max).then_inc(mx_ready, 1)

            def turned(n, u):
                v.wait_ge(pt_done, n + 1)
                nc.vector.tensor_copy(pts[0:S, u % 2, :], p_ps[u % 2][0:S, 0:UC]).then_inc(pt_out, 1)

            def context(b, q):
                v.wait_ge(c_done, b + 1)
                c3 = c_ps[0:S, 0:NH * VW].rearrange("p (h w) -> p h w", w=VW)
                nc.vector.reciprocal(rc[:, :], c3[:, :, AD]).then_inc(rc_ready, 1)
                v.wait_ge(rc_ready, b + 1)
                nc.vector.tensor_tensor(cx[:, q, :].rearrange("p (h w) -> p h w", w=AD), c3[:, :, 0:AD], last(rc[:, :], AD), ALU.mult).then_inc(c_out, 1)

            for b in range(2):
                keys(b, b)
            values(0, 0)
            for u in range(AHEAD):
                scores(u, u)

            def step(n, u, b, q, first, left):
                if left or u == 0:
                    scores(n + AHEAD, (u + AHEAD) % UPB)
                turned(n, u)
                if u == 0 and not first:
                    context(b - 1, 1 - q)
                if u == 2 and left >= 2:
                    keys(b + 2, q)
                if u == UPB - 1 and left:
                    values(b + 1, 1 - q)

            units(step)(v)
            context(B - 1, 1)


def moe2(nc, a, out, m, ctx):
    sb = lambda name, shape, dt=F32: m["sb"](name, shape, dt, ctx)
    w1, w2 = sb("x_w1", [P, 2, DC, HID]), sb("x_w2", [P, 2, MC, D])
    m["ln_g"], m["ln_b"] = sb("lng", [P, D]), sb("lnb", [P, D])
    w_loaded = [m["sem"](f"xw_loaded{p}", ctx) for p in range(2)]
    with ExitStack() as c:
        capacity_routing(nc, a, m, c, w1, w2, w_loaded)
    with ExitStack() as c:
        moe2_experts(nc, a, m, c, w1, w2, w_loaded)
    with ExitStack() as c:
        combine2(nc, a, out, m, c)


def load_expert(sp, a, w1, w2, w_loaded, e, p):
    sp.dma_start(w1[:, p, :, :], a["x_w1"][bass.ds(e, 1)].rearrange("o p c n -> (o p) c n")).then_inc(w_loaded[p], 16)
    sp.dma_start(w2[:, p, :, :], a["x_w2"][bass.ds(e, 1)].rearrange("o p c n -> (o p) c n")).then_inc(w_loaded[p], 16)


def capacity_routing(nc, a, m, ctx, w1, w2, w_loaded):
    csb = lambda name, shape, dt=F32: m["sb"](name, shape, dt, ctx)
    t = routing_tensors(m, ctx)
    C3 = 3
    wt, hit, hits, cnt = csb("wt", [P, ET]), csb("hit", [P, ET]), csb("hits", [P, C3, ET]), csb("cnt", [P, C3, E8], BF16)
    thr, cand, bits = csb("thr", [P, E8], U32), csb("cand", [P, C3, E8], U32), csb("bits", [P, C3, E8], U32)
    best = csb("best", [P, C3 + 1, E8])
    room, taken = csb("room", [P, E8]), csb("taken", [P, 2, T])
    pb, pt, pc = (m["ps"](n, [P, 512], ctx) for n in ("ps_before", "ps_total", "ps_count"))
    dve, asked, counted, idx_ready, scattered, cnt_ready, cnt_done, srch = (m["sem"](n, ctx) for n in (
        "rt_dve", "asked", "counted", "idx_ready", "scattered", "cnt_ready", "cnt_done", "search"))
    ROUNDS = 15
    PER = 5
    with nc.Block() as block:
        @block.sync
        def _(sp):
            for e in range(2):
                load_expert(sp, a, w1, w2, w_loaded, e, e)

        @block.scalar
        def _(act):
            act.wait_ge(t["gap_ready"], 1)
            nc.scalar.activation(m["w"][:, 1, :], m["w"][:, 1, :], ACT.Exp).then_inc(t["exp_ready"], 1)

        @block.tensor
        def _(pe):
            with pe.Fori(0, ROUNDS) as i:
                pe.wait_ge(cnt_ready, i + 1)
                nc.tensor.matmul(pc[:, 0:C3 * E8], m["ones_bf"][:, :], cnt[:, :, :].rearrange("p c e -> p (c e)"), start=True, stop=True).then_inc(cnt_done, 1)
            for n in range(3):
                count_matmuls(nc, pe, m, t, pb, pt, asked, counted, n + 1)

        @block.vector
        def _(v):
            steps = Steps(v, dve)
            top2(nc, v, steps, m, t)
            w, oh = m["w"], t["oh"]
            steps.after(nc.vector.tensor_tensor(by_tile(wt[:, :]), by_tile(oh[:, 0, :]), mid(w[:, 0, :], E8), ALU.mult))
            steps.after(nc.vector.tensor_tensor(by_tile(hit[:, :]), by_tile(oh[:, 1, :]), mid(w[:, 1, :], E8), ALU.mult))
            steps.after(nc.vector.tensor_tensor(wt[:, :], wt[:, :], hit[:, :], ALU.add))
            steps.after(nc.vector.memset(thr[:, :].bitcast(F32), 0.0))
            for c in range(C3):
                steps.after(nc.vector.memset(bits[:, c, :].bitcast(F32), (2.0 ** -95, 2.0 ** -63, 2.0 ** -31)[c]))
            steps.after(nc.vector.memset(best[:, C3, :], 0.0))
            with v.Fori(0, ROUNDS) as i:
                nc.vector.tensor_tensor(cand[:, :, :], mid(thr[:, :], C3), bits[:, :, :], ALU.bitwise_or).then_inc(srch, 1)
                v.wait_ge(srch, i * PER + 1)
                nc.vector.tensor_tensor(hits[:, :, :].rearrange("p c (e t) -> p c e t", t=T), by_tile(wt[:, :]).unsqueeze(1).broadcast_to([P, C3, E8, T]),
                                        cand[:, :, :].bitcast(F32).unsqueeze(3).broadcast_to([P, C3, E8, T]), ALU.is_ge).then_inc(srch, 1)
                nc.vector.tensor_scalar(bits[:, :, :], bits[:, :, :], 2, None, ALU.logical_shift_right)
                v.wait_ge(srch, i * PER + 2)
                with nc.allow_low_precision(reason="counts up to 18 are exact in bfloat16"):
                    nc.vector.tensor_reduce(cnt[:, :, :], hits[:, :, :].rearrange("p c (e t) -> p c e t", t=T), AX.X, ALU.add).then_inc(cnt_ready, 1)
                v.wait_ge(cnt_done, i + 1)
                nc.vector.scalar_tensor_tensor(out=best[:, 0:C3, :], in0=pc[:, 0:C3 * E8].rearrange("p (c e) -> p c e", e=E8), scalar=float(CAP),
                                               in1=cand[:, :, :].bitcast(F32), op0=ALU.is_ge, op1=ALU.mult).then_inc(srch, 1)
                v.wait_ge(srch, i * PER + 3)
                nc.vector.tensor_reduce(thr[:, :].bitcast(F32), best[:, :, :].rearrange("p c e -> p e c"), AX.X, ALU.max).then_inc(srch, 1)
                v.wait_ge(srch, i * PER + 4)
                nc.vector.tensor_copy(best[:, C3, :], thr[:, :].bitcast(F32)).then_inc(srch, 1)
                v.wait_ge(srch, i * PER + 5)
            limit = last(thr[:, :].bitcast(F32), T)
            steps.after(nc.vector.tensor_tensor(by_tile(t["chosen"][:, :]), by_tile(wt[:, :]), limit, ALU.is_gt))
            positions(nc, v, steps, m, t, t["chosen"][:, :], pb, pt, asked, counted, 1)
            steps.after(nc.vector.tensor_scalar(room[:, :], by_tile(t["incl"][:, :])[:, :, T - 1], -1.0, float(CAP), ALU.mult, ALU.add))
            steps.after(nc.vector.tensor_tensor(by_tile(hit[:, :]), by_tile(wt[:, :]), limit, ALU.is_equal))
            steps.after(nc.vector.scalar_tensor_tensor(out=hit[:, :], in0=wt[:, :], scalar=0.0, in1=hit[:, :], op0=ALU.is_gt, op1=ALU.mult))
            positions(nc, v, steps, m, t, hit[:, :], pb, pt, asked, counted, 2)
            steps.after(nc.vector.tensor_tensor(by_tile(t["pos"][:, :]), by_tile(t["pos"][:, :]), last(room[:, :], T), ALU.is_lt))
            steps.after(nc.vector.tensor_tensor(hit[:, :], hit[:, :], t["pos"][:, :], ALU.mult))
            steps.after(nc.vector.tensor_tensor(t["chosen"][:, :], t["chosen"][:, :], hit[:, :], ALU.add))
            positions(nc, v, steps, m, t, t["chosen"][:, :], pb, pt, asked, counted, 3)
            steps.after(nc.vector.scalar_tensor_tensor(out=by_tile(t["pos"][:, :]), in0=last(m["iota8"][:, :], T), scalar=float(ROWS),
                                                       in1=by_tile(t["pos"][:, :]), op0=ALU.mult, op1=ALU.add))
            for k in range(2):
                steps.after(nc.vector.tensor_tensor(oh[:, k, :], oh[:, k, :], t["chosen"][:, :], ALU.mult))
                steps.after(nc.vector.tensor_reduce(taken[:, k, :], oh[:, k, :].rearrange("p (e t) -> p t e", t=T), AX.X, ALU.add))
            steps.after(nc.vector.tensor_tensor(w[:, :, :], w[:, :, :], taken[:, :, :], ALU.mult))
            row_indices(nc, steps, m, t, [taken[:, 0, :], taken[:, 1, :]])
            v.sem_inc(idx_ready, 1)

        @block.gpsimd
        def _(pool):
            pool.wait_ge(m["zeros_stored2"], zeros_count(E8 * ROWS))
            pool.wait_ge(idx_ready, 1)
            scatter_rows(nc, pool, m, m["rows2"], E8 * ROWS, scattered)


def moe2_experts(nc, a, m, ctx, w1, w2, w_loaded):
    sb = lambda name, shape, dt=F32: m["sb"](name, shape, dt, ctx)
    sem = lambda name: m["sem"](name, ctx)
    ident = m["ident"]
    b1, b2 = sb("x_b1", [P, E8, MC]), sb("x_b2", [P, E8, DC])
    x = sb("xx", [XQ, 2, XG, D])
    xT = sb("xxT", [P, 2, DC, ROWS])
    hT = sb("xhT", [P, MC, ROWS])
    oT = sb("xoT", [P, DC, ROWS])
    r = sb("xr", [XQ, 2, XG, D])
    pair = lambda name: [m["ps"](f"{name}{i}", [P, 512], ctx) for i in range(2)]
    x_ps, h_ps, o_ps, r_ps = pair("xx_ps"), pair("xh_ps"), pair("xo_ps"), pair("xr_ps")
    biases, x_turned, xT_out, h_done, h_out, o_done, o_out, r_done, r_out = map(
        sem, ("x_biases", "x_turned", "xT_out", "xh_done", "xh_out", "xo_done", "xo_out", "xr_done", "xr_out"))
    x_loaded = [sem(f"xx_loaded{p}") for p in range(2)]
    stored = [sem(f"xr_stored{p}") for p in range(2)]
    ln_loaded, h_plus_b = sem("ln_loaded"), sem("h_plus_b")

    def rows(dram, e):
        return dram[bass.ds(e * ROWS, ROWS), :].rearrange("(g q) d -> q g d", q=XQ)

    def for_experts(eng, step):
        step(0, 0, True, False)
        with eng.Fori(0, E8 // 2 - 1) as j:
            for p in range(2):
                step(j * 2 + (p + 1), 1 - p, False, False)
        step(E8 - 1, 1, False, True)

    with nc.Block() as block:
        @block.sync
        def _(sp):
            sp.dma_start(b1[:, :, :], a["x_b1"]).then_inc(biases, 16)
            sp.dma_start(b2[:, :, :], a["x_b2"]).then_inc(biases, 16)
            sp.dma_start(m["ln_b"][:, :], a["ln_b"].partition_broadcast(P)).then_inc(ln_loaded, 16)
            sp.dma_start(m["ln_g"][:, :], a["ln_g"].partition_broadcast(P)).then_inc(ln_loaded, 16)
            for p in range(2):
                sp.sem_inc(stored[p], 16)

            def load_x(e, p):
                sp.wait_ge(x_turned, e + 1)
                sp.dma_start(x[:, p, :, :], rows(m["rows2"], e)).then_inc(x_loaded[p], 16)

            def step(e, p, first, final):
                if not final:
                    if not first:
                        sp.wait_ge(o_done, e + 1)
                        load_expert(sp, a, w1, w2, w_loaded, e + 1, 1 - p)
                    load_x(e + 1, 1 - p)
                if not first:
                    sp.wait_ge(r_out, e + 1)
                    sp.dma_start(rows(m["outs2"], e - 1), r[:, 1 - p, :, :]).then_inc(stored[1 - p], 16)

            load_x(0, 0)
            for_experts(sp, step)
            sp.wait_ge(r_out, E8 + 1)
            sp.dma_start(rows(m["outs2"], E8 - 1), r[:, 1, :, :]).then_inc(stored[1], 16)
            for p in range(2):
                sp.wait_ge(stored[p], 16 * (E8 // 2 + 1))

        @block.gpsimd
        def _(pool):
            pool.wait_ge(ln_loaded, 32)
            nc.gpsimd.tensor_tensor(m["H"][:, :, :], m["H"][:, :, :], mid(m["ln_b"][:, :], T), ALU.add).then_inc(h_plus_b, 1)

        @block.tensor
        def _(pe):
            pe.sem_inc(x_turned, 2)

            def turn_x(e, p):
                pe.wait_ge(x_loaded[p], (e - p) * 8 + 16)
                for c in range(DC):
                    for g in range(XG):
                        mm = nc.tensor.transpose(x_ps[c][:, g * XQ:(g + 1) * XQ], x[:, p, g, c * P:(c + 1) * P], ident[0:XQ, 0:XQ])
                mm.then_inc(x_turned, 1)

            def turn_out(e, p):
                pe.wait_ge(o_out, e + 2)
                pe.wait_ge(r_out, e + 1)
                for g in range(XG):
                    for c in range(DC):
                        o = (g % 2) * D + c * P
                        mm = nc.tensor.transpose(r_ps[g // 2][0:XQ, o:o + P], oT[:, c, g * XQ:(g + 1) * XQ], ident[:, :])
                mm.then_inc(r_done, 1)

            def step(e, p, first, final):
                pe.wait_ge(w_loaded[p], (e - p) * 16 + 32)
                pe.wait_ge(xT_out, e + 1)
                for k in range(MC):
                    pe.wait_ge(h_out, e * MC + (k + 1))
                    for c in range(DC):
                        mm = nc.tensor.matmul(h_ps[k % 2][:, 0:ROWS], w1[:, p, c, k * P:(k + 1) * P], xT[:, p, c, :], start=(c == 0), stop=(c == DC - 1))
                    mm.then_inc(h_done, 1)
                if not first:
                    turn_out(e - 1, 1 - p)
                if not final:
                    turn_x(e + 1, 1 - p)
                pe.wait_ge(o_out, e + 1)
                for o in range(DC):
                    for k in range(MC):
                        if o == 0:
                            pe.wait_ge(h_out, e * MC + (k + 3))
                        mm = nc.tensor.matmul(o_ps[o][:, 0:ROWS], w2[:, p, k, o * P:(o + 1) * P], hT[:, k, :], start=(k == 0), stop=(k == MC - 1))
                mm.then_inc(o_done, 1)

            turn_x(0, 0)
            for_experts(pe, step)
            turn_out(E8 - 1, 1)

        @block.scalar
        def _(act):
            act.sem_inc(h_out, 2)
            act.sem_inc(o_done, 1)
            act.wait_ge(biases, 32)

            def turned(e, p):
                act.wait_ge(x_turned, e + 3)
                for c in range(DC):
                    ins = nc.scalar.activation(xT[:, p, c, :], x_ps[c][:, 0:ROWS], ACT.Copy)
                ins.then_inc(xT_out, 1)

            def step(e, p, first, final):
                for k in range(MC):
                    act.wait_ge(h_done, e * MC + (k + 1))
                    if k == 0:
                        act.wait_ge(o_done, e + 1)
                    nc.scalar.activation(hT[:, k, :], h_ps[k % 2][:, 0:ROWS], ACT.Gelu, bias=b1[:, bass.ds(e, 1), k]).then_inc(h_out, 1)
                if not final:
                    turned(e + 1, 1 - p)

            turned(0, 0)
            for_experts(act, step)

        @block.vector
        def _(v):
            v.sem_inc(o_out, 1)
            v.sem_inc(r_out, 1)
            v.sem_inc(r_done, 1)
            v.wait_ge(biases, 32)

            def turned_out(e, p):
                v.wait_ge(r_done, e + 2)
                v.wait_ge(stored[p], (e - p) * 8 + 16)
                for g in range(2):
                    ins = nc.vector.tensor_copy(r[:, p, 2 * g:2 * g + 2, :], r_ps[g][0:XQ, 0:2 * D].rearrange("p (g d) -> p g d", d=D))
                ins.then_inc(r_out, 1)

            def step(e, p, first, final):
                if not first:
                    turned_out(e - 1, 1 - p)
                v.wait_ge(o_done, e + 2)
                v.wait_ge(r_done, e + 1)
                for o in range(DC):
                    ins = nc.vector.tensor_scalar(oT[:, o, :], o_ps[o][:, 0:ROWS], b2[:, bass.ds(e, 1), o], None, ALU.add)
                ins.then_inc(o_out, 1)

            for_experts(v, step)
            turned_out(E8 - 1, 1)


def combine2(nc, a, out, m, ctx):
    SL = 12
    sb = lambda name, shape: m["sb"](name, shape, F32, ctx)
    sem = lambda name: m["sem"](name, ctx)
    H, A, g = m["H"], m["A"], m["ln_g"]
    got = sb("got", [P, SL, D])
    loaded = [sem(f"g_loaded{i}") for i in range(SL)]
    first_in, used, stats, dve, var_ready, std_ready, scaled, fin, stored = map(
        sem, ("first_in", "g_used", "cstats", "cdve", "cvar", "cstd", "scaled", "fin", "out_stored"))
    rows = out.rearrange("b s d -> (b s) d")
    with nc.Block() as block:
        @block.sync
        def _(sp):
            with sp.Fori(0, T - 1) as i:
                sp.wait_ge(fin, i + 1)
                sp.dma_start(rows[bass.ds(i * P, P), :], tile_of(A, i)).then_inc(stored, 16)
            sp.wait_ge(fin, T)
            sp.dma_start(rows[(T - 1) * P:N, :], A[0:LAST, T - 1, :]).then_inc(stored, 16)
            sp.wait_ge(stored, 16 * T)

        @block.gpsimd
        def _(pool):
            gather_rows(nc, pool, m, m["outs2"], E8 * ROWS, got, loaded, used, SL)

        @block.scalar
        def _(act):
            def weigh_first(k):
                for i in group_tiles(k):
                    n = 2 * i
                    act.wait_ge(loaded[n % SL], 16 * (n // SL + 1))
                    nc.scalar.activation(A[:, i, :], got[:, n % SL, :], ACT.Copy, scale=m["w"][:, 0, i:i + 1]).then_inc(first_in, 1)

            weigh_first(0)
            for k in range(T // GT):
                if k < T // GT - 1:
                    weigh_first(k + 1)
                group_root(nc, act, m, k, var_ready, std_ready)

        @block.vector
        def _(v):
            steps = Steps(v, dve)

            def norm(k):
                here = slice(k * GT, (k + 1) * GT)
                v.wait_ge(std_ready, k + 1)
                steps.after(nc.vector.reciprocal(m["rstd"][:, here], m["std"][:, here]))
                for i in range(k * GT, (k + 1) * GT):
                    nc.vector.scalar_tensor_tensor(out=A[:, i, :], in0=A[:, i, :], scalar=m["mean"][:, i:i + 1], in1=g[:, :],
                                                   op0=ALU.subtract, op1=ALU.mult).then_inc(scaled, 1)
                for i in range(k * GT, (k + 1) * GT):
                    v.wait_ge(scaled, i + 1)
                    nc.vector.scalar_tensor_tensor(out=A[:, i, :], in0=A[:, i, :], scalar=m["rstd"][:, i:i + 1], in1=H[:, i, :],
                                                   op0=ALU.mult, op1=ALU.add).then_inc(fin, 1)

            for k in range(T // GT):
                collect(nc, v, steps, m, group_tiles(k), got, loaded, used, stats, var_ready, A, first_in)
                if k:
                    norm(k - 1)
            norm(T // GT - 1)


def _laid_out(x):
    import numpy as np

    def chunks(w):
        c = w.shape[0] // P
        return w.reshape(c, P, -1).transpose(1, 0, 2)

    def column(v):
        return v.reshape(-1, P).T

    r = {k: np.asarray(v) for k, v in x.items()}
    o = {}
    px = r["x"].reshape(B, 3, 6, 16, 6, 16).transpose(1, 3, 5, 2, 4, 0).reshape(KC, P, PT, P)
    o["patches"] = px.transpose(2, 1, 0, 3)
    o["patch_w"] = chunks(r["L0_tok_W"].T)
    o["patch_b"] = r["L0_tok_b"]
    o["cls"] = r["L0_tok_class_token"].reshape(D)
    o["pos"] = r["L0_tok_pos_embedding"].reshape(1 + NPATCH, D)
    o["txt"] = r["txt"]
    o["m_gamma"], o["m_beta"] = column(r["L0_attn_ln_gamma"]), column(r["L0_attn_ln_beta"])
    o["m_win"] = chunks(r["L0_attn_W_in"])
    bi = r["L0_attn_b_in"]
    o["m_bz"] = column(bi[0:INNER])
    o["m_bx"] = bi[INNER:2 * INNER]
    o["m_bb"] = bi[2 * INNER:2 * INNER + NST].reshape(NST, 1)
    o["m_bc"] = bi[2 * INNER + NST:2 * INNER + 2 * NST].reshape(NST, 1)
    o["m_bdt"] = bi[2 * INNER + 2 * NST:].reshape(HM, 1)
    o["m_dtb"] = r["L0_attn_dt_bias"].reshape(HM, 1)
    o["m_alog"] = r["L0_attn_A_log"].reshape(HM, 1)
    o["m_d"] = r["L0_attn_D_skip"]
    o["m_wout"] = chunks(r["L0_attn_W_out"])
    o["m_bout"] = r["L0_attn_b_out"]
    o["f_norm"] = column(r["L0_ffn_norm_w"])
    o["f_gw"] = chunks(r["L0_ffn_gate_w"].T)
    o["f_gb"] = r["L0_ffn_gate_b"]
    w1 = r["L0_ffn_mlp1_w"].reshape(E8, 256, 2, DC, P)
    o["moe1_w1"] = w1.transpose(4, 0, 3, 2, 1).reshape(P, E8, DC, F1)
    o["moe1_b1"] = r["L0_ffn_mlp1_b"].reshape(E8, 256, 2).transpose(0, 2, 1).reshape(E8 * F1)
    o["moe1_w2"] = r["L0_ffn_mlp2_w"].reshape(E8, D, DC, P).transpose(3, 0, 2, 1)
    o["moe1_b2"] = r["L0_ffn_mlp2_b"].reshape(E8 * D)
    for k in ("q", "k", "v", "o", "fq", "fg"):
        o["a_w" + k] = chunks(r["L1_attn_w" + k])
        o["a_b" + k] = column(r["L1_attn_b" + k])
    o["a_bv_row"], o["a_bo_row"] = r["L1_attn_bv"], r["L1_attn_bo"]
    u = np.zeros((2, NH, AD, NH), r["L1_attn_up"].dtype)
    for i, k in enumerate(("up", "uz")):
        for h in range(NH):
            u[i, h, :, h] = r["L1_attn_" + k][h, 0]
    o["a_upz"] = chunks(np.concatenate((u[0].reshape(D, NH), u[1].reshape(D, NH)), axis=1))
    o["r_gw"] = chunks(r["L1_ffn_router_w"])
    o["r_gb"] = r["L1_ffn_router_b"]
    o["x_w1"] = r["L1_ffn_w1"].reshape(E8, DC, P, HID).transpose(0, 2, 1, 3)
    o["x_w2"] = r["L1_ffn_w2"].reshape(E8, MC, P, D).transpose(0, 2, 1, 3)
    o["x_b1"] = r["L1_ffn_b1"].reshape(E8, MC, P).transpose(2, 0, 1)
    o["x_b2"] = r["L1_ffn_b2"].reshape(E8, DC, P).transpose(2, 0, 1)
    o["ln_g"], o["ln_b"] = r["L1_ffn_ln_g"], r["L1_ffn_ln_b"]
    f = np.float32
    n = np.arange(P)
    o["ident"] = np.eye(P, dtype=f)
    bf16_one = 0x3F80
    o["before"] = np.where(n[:, None] < n[None, :], bf16_one, 0).astype(np.uint16)
    o["ones_bf"] = np.full((P, P), bf16_one, np.uint16)
    o["place"] = np.arange(S, dtype=f)
    keep = np.ones((P, E8, T), f)
    keep[:, :, 0] = 0.0
    o["keep"] = keep.reshape(P, ET)
    o["iota8"] = np.tile(np.arange(E8, dtype=f), (P, 1))
    o["iota_blk"] = np.repeat(np.arange(NBLK, dtype=f), E8).reshape(1, NBLK * E8)
    valid = np.ones((P, T), f)
    valid[LAST:, T - 1] = 0.0
    o["valid"] = valid
    o["head_of"] = ((n // AD)[:, None] == np.arange(P // AD)[None, :]).astype(f)
    return {k: np.ascontiguousarray(v) for k, v in o.items()}


def kernel(**inputs):
    import numpy as _np
    import concourse.bacc as _bacc
    from concourse import mybir as _mybir
    from concourse.bass_utils import run_bass_kernel_spmd as _run

    nc = _bacc.Bacc("TRN2", target_bir_lowering=False, num_devices=1)
    arrays, args = {}, {}
    for name, v in _laid_out(inputs).items():
        arrays[f"in_{name}"] = v
        args[name] = nc.dram_tensor(f"in_{name}", v.shape, _mybir.dt.from_np(v.dtype), kind="ExternalInput").ap()
    out = nc.dram_tensor("out_0", (B, S, D), F32, kind="ExternalOutput").ap()
    build(nc, args, out)
    r = _run(nc, [arrays], core_ids=[0])
    return r.results[0]["out_0"]
```
